# Optimizing a Trainium2 kernel written in Bass

```python
import numpy as np
import jax
import jax.numpy as jnp

def _softmax(x, axis=-1):
    return jax.nn.softmax(x, axis=axis)

def _gelu(x):
    return jax.nn.gelu(x, approximate=True)

def _silu(x):
    return jax.nn.silu(x)

def _sigmoid(x):
    return jax.nn.sigmoid(x)

def _layernorm(x, axis=-1, eps=1e-05):
    m = jnp.mean(x, axis=axis, keepdims=True)
    v = jnp.var(x, axis=axis, keepdims=True)
    return (x - m) / jnp.sqrt(v + eps)

def _scatter_add(tgt, idx, src, axis=0):
    return tgt.at[idx].add(src)

def _segment_sum(src, seg, n):
    return jax.ops.segment_sum(src, seg, n)
kernel_name = 'mk_recurrent_d1_jaxref_r8_544e58'

def setup_inputs(seed: int=0):
    np.random.seed(seed)
    _w = jnp.asarray

    def _L0_attn_setup():
        import jax, jax.numpy as jnp
        import numpy as np
        B, L, SIZE, ATT, LIN = (8, 256, 128, 128, 512)
        EPS = 1e-05

        def layer_norm(x, g, b):
            m = x.mean(-1, keepdims=True)
            v = ((x - m) ** 2).mean(-1, keepdims=True)
            return (x - m) * jax.lax.rsqrt(v + EPS) * g + b

        def time_shift(x):
            return jnp.pad(x, ((0, 0), (1, 0), (0, 0)))[:, :-1]

        def wkv(time_decay, time_first, k, v):
            w = -jnp.exp(time_decay)
            u = time_first

            def step(carry, kv):
                p, q, o = carry
                kt, vt = kv
                no = jnp.maximum(o, u + kt)
                A = jnp.exp(o - no)
                Bc = jnp.exp(u + kt - no)
                out = (A * p + Bc * vt) / (A * q + Bc)
                no2 = jnp.maximum(o + w, kt)
                A2 = jnp.exp(o + w - no2)
                B2 = jnp.exp(kt - no2)
                return ((A2 * p + B2 * vt, A2 * q + B2, no2), out)
            Bn, Ln, D = k.shape
            init = (jnp.zeros((Bn, D), k.dtype), jnp.zeros((Bn, D), k.dtype), jnp.full((Bn, D), -1e+38, k.dtype))
            _, out = jax.lax.scan(step, init, (jnp.moveaxis(k, 1, 0), jnp.moveaxis(v, 1, 0)))
            return jnp.moveaxis(out, 0, 1)
        key = jax.random.key(seed)
        ks = jax.random.split(key, 20)
        n = lambda i, shape, s=1.0: jax.random.normal(ks[i], shape, jnp.float32) * s
        u = lambda i, shape: jax.random.uniform(ks[i], shape, jnp.float32)
        return {'x': n(0, (B, L, SIZE)), 'ln_att_g': jnp.ones((SIZE,), jnp.float32), 'ln_att_b': jnp.zeros((SIZE,), jnp.float32), 'ln_ffn_g': jnp.ones((SIZE,), jnp.float32), 'ln_ffn_b': jnp.zeros((SIZE,), jnp.float32), 'att_time_decay': n(1, (ATT,), 0.5), 'att_time_first': n(2, (ATT,), 0.5), 'att_mix_k': u(3, (SIZE,)), 'att_mix_v': u(4, (SIZE,)), 'att_mix_r': u(5, (SIZE,)), 'att_wk': n(6, (SIZE, ATT), 0.02), 'att_wv': n(7, (SIZE, ATT), 0.02), 'att_wr': n(8, (SIZE, ATT), 0.02), 'att_wo': n(9, (ATT, SIZE), 0.02), 'ffn_mix_k': u(10, (SIZE,)), 'ffn_mix_r': u(11, (SIZE,)), 'ffn_wk': n(12, (SIZE, LIN), 0.02), 'ffn_wv': n(13, (LIN, SIZE), 0.02), 'ffn_wr': n(14, (SIZE, SIZE), 0.02)}
    _L0_attn_in = _L0_attn_setup()

    def _L0_ffn_setup():
        import jax, jax.numpy as jnp
        import numpy as np
        E = 8
        C = 160
        D = 128
        H = 512
        B, S = (4, 256)
        key = jax.random.key(seed)
        ks = jax.random.split(key, 12)
        sc = 0.02
        return {'input': jax.random.normal(ks[0], (B, S, D), jnp.float32), 'router_w': jax.random.normal(ks[1], (D, E), jnp.float32) * sc, 'router_b': jnp.zeros((E,), jnp.float32), 'w1': jax.random.normal(ks[2], (E, D, H), jnp.float32) * sc, 'b1': jnp.zeros((E, H), jnp.float32), 'w2': jax.random.normal(ks[3], (E, H, D), jnp.float32) * sc, 'b2': jnp.zeros((E, D), jnp.float32), 'ow1': jax.random.normal(ks[4], (D, H), jnp.float32) * sc, 'ob1': jnp.zeros((H,), jnp.float32), 'ow2': jax.random.normal(ks[5], (H, D), jnp.float32) * sc, 'ob2': jnp.zeros((D,), jnp.float32)}
    _L0_ffn_in = _L0_ffn_setup()
    _d = {'L0_attn_x': _L0_attn_in['x'], 'L0_attn_ln_att_g': _L0_attn_in['ln_att_g'], 'L0_attn_ln_att_b': _L0_attn_in['ln_att_b'], 'L0_attn_ln_ffn_g': _L0_attn_in['ln_ffn_g'], 'L0_attn_ln_ffn_b': _L0_attn_in['ln_ffn_b'], 'L0_attn_att_time_decay': _L0_attn_in['att_time_decay'], 'L0_attn_att_time_first': _L0_attn_in['att_time_first'], 'L0_attn_att_mix_k': _L0_attn_in['att_mix_k'], 'L0_attn_att_mix_v': _L0_attn_in['att_mix_v'], 'L0_attn_att_mix_r': _L0_attn_in['att_mix_r'], 'L0_attn_att_wk': _L0_attn_in['att_wk'], 'L0_attn_att_wv': _L0_attn_in['att_wv'], 'L0_attn_att_wr': _L0_attn_in['att_wr'], 'L0_attn_att_wo': _L0_attn_in['att_wo'], 'L0_attn_ffn_mix_k': _L0_attn_in['ffn_mix_k'], 'L0_attn_ffn_mix_r': _L0_attn_in['ffn_mix_r'], 'L0_attn_ffn_wk': _L0_attn_in['ffn_wk'], 'L0_attn_ffn_wv': _L0_attn_in['ffn_wv'], 'L0_attn_ffn_wr': _L0_attn_in['ffn_wr'], 'L0_ffn_router_w': _L0_ffn_in['router_w'], 'L0_ffn_router_b': _L0_ffn_in['router_b'], 'L0_ffn_w1': _L0_ffn_in['w1'], 'L0_ffn_b1': _L0_ffn_in['b1'], 'L0_ffn_w2': _L0_ffn_in['w2'], 'L0_ffn_b2': _L0_ffn_in['b2'], 'L0_ffn_ow1': _L0_ffn_in['ow1'], 'L0_ffn_ob1': _L0_ffn_in['ob1'], 'L0_ffn_ow2': _L0_ffn_in['ow2'], 'L0_ffn_ob2': _L0_ffn_in['ob2']}
    _x0 = _d['L0_attn_x']
    _d['L0_attn_x'] = jax.random.normal(jax.random.fold_in(jax.random.key(seed), 1), (2, 1024, 128), dtype=_x0.dtype)
    del _x0
    return _d

def reference(L0_attn_x, L0_attn_ln_att_g, L0_attn_ln_att_b, L0_attn_ln_ffn_g, L0_attn_ln_ffn_b, L0_attn_att_time_decay, L0_attn_att_time_first, L0_attn_att_mix_k, L0_attn_att_mix_v, L0_attn_att_mix_r, L0_attn_att_wk, L0_attn_att_wv, L0_attn_att_wr, L0_attn_att_wo, L0_attn_ffn_mix_k, L0_attn_ffn_mix_r, L0_attn_ffn_wk, L0_attn_ffn_wv, L0_attn_ffn_wr, L0_ffn_router_w, L0_ffn_router_b, L0_ffn_w1, L0_ffn_b1, L0_ffn_w2, L0_ffn_b2, L0_ffn_ow1, L0_ffn_ob1, L0_ffn_ow2, L0_ffn_ob2):

    def _L0_attn_ref(x, ln_att_g, ln_att_b, ln_ffn_g, ln_ffn_b, att_time_decay, att_time_first, att_mix_k, att_mix_v, att_mix_r, att_wk, att_wv, att_wr, att_wo, ffn_mix_k, ffn_mix_r, ffn_wk, ffn_wv, ffn_wr):
        import jax, jax.numpy as jnp
        import numpy as np
        B, L, SIZE, ATT, LIN = (8, 256, 128, 128, 512)
        EPS = 1e-05

        def layer_norm(x, g, b):
            m = x.mean(-1, keepdims=True)
            v = ((x - m) ** 2).mean(-1, keepdims=True)
            return (x - m) * jax.lax.rsqrt(v + EPS) * g + b

        def time_shift(x):
            return jnp.pad(x, ((0, 0), (1, 0), (0, 0)))[:, :-1]

        def wkv(time_decay, time_first, k, v):
            w = -jnp.exp(time_decay)
            u = time_first

            def step(carry, kv):
                p, q, o = carry
                kt, vt = kv
                no = jnp.maximum(o, u + kt)
                A = jnp.exp(o - no)
                Bc = jnp.exp(u + kt - no)
                out = (A * p + Bc * vt) / (A * q + Bc)
                no2 = jnp.maximum(o + w, kt)
                A2 = jnp.exp(o + w - no2)
                B2 = jnp.exp(kt - no2)
                return ((A2 * p + B2 * vt, A2 * q + B2, no2), out)
            Bn, Ln, D = k.shape
            init = (jnp.zeros((Bn, D), k.dtype), jnp.zeros((Bn, D), k.dtype), jnp.full((Bn, D), -1e+38, k.dtype))
            _, out = jax.lax.scan(step, init, (jnp.moveaxis(k, 1, 0), jnp.moveaxis(v, 1, 0)))
            return jnp.moveaxis(out, 0, 1)
        h = layer_norm(x, ln_att_g, ln_att_b)
        sx = time_shift(h)
        k = (h * att_mix_k + sx * (1.0 - att_mix_k)) @ att_wk
        v = (h * att_mix_v + sx * (1.0 - att_mix_v)) @ att_wv
        r = jax.nn.sigmoid((h * att_mix_r + sx * (1.0 - att_mix_r)) @ att_wr)
        att = r * wkv(att_time_decay, att_time_first, k, v) @ att_wo
        x = x + att
        h = layer_norm(x, ln_ffn_g, ln_ffn_b)
        sx = time_shift(h)
        kf = jnp.square(jax.nn.relu((h * ffn_mix_k + sx * (1.0 - ffn_mix_k)) @ ffn_wk))
        rf = jax.nn.sigmoid((h * ffn_mix_r + sx * (1.0 - ffn_mix_r)) @ ffn_wr)
        return x + rf * (kf @ ffn_wv)

    def _L0_ffn_ref(input, router_w, router_b, w1, b1, w2, b2, ow1, ob1, ow2, ob2):
        import jax, jax.numpy as jnp
        import numpy as np
        E = 8
        C = 160
        D = 128
        H = 512
        B, S = (4, 256)
        Bq, Sq, Dq = input.shape
        N = Bq * Sq
        xf = input.reshape(N, Dq)
        probs = jax.nn.softmax(xf @ router_w + router_b, axis=-1)
        eid = jnp.argmax(probs, axis=-1)
        onehot = jax.nn.one_hot(eid, E, dtype=xf.dtype)
        rank = (jnp.cumsum(onehot, axis=0)[jnp.arange(N), eid] - 1.0).astype(jnp.int32)
        valid = rank < C
        pos = jnp.where(valid, rank, 0)
        vmask = valid.astype(xf.dtype)[:, None]
        buf = jnp.zeros((E, C, Dq), xf.dtype).at[eid, pos].add(xf * vmask)
        h = jax.nn.relu(jnp.einsum('ecd,edh->ech', buf, w1) + b1[:, None, :])
        y = jnp.einsum('ech,ehd->ecd', h, w2) + b2[:, None, :]
        y_tok = y[eid, pos] * vmask
        yov = jax.nn.relu(xf @ ow1 + ob1) @ ow2 + ob2
        out = y_tok + yov * (1.0 - vmask)
        return out.reshape(Bq, Sq, Dq)
    x = L0_attn_x
    xn = _layernorm(x, axis=-1)
    s = _L0_attn_ref(xn, L0_attn_ln_att_g, L0_attn_ln_att_b, L0_attn_ln_ffn_g, L0_attn_ln_ffn_b, L0_attn_att_time_decay, L0_attn_att_time_first, L0_attn_att_mix_k, L0_attn_att_mix_v, L0_attn_att_mix_r, L0_attn_att_wk, L0_attn_att_wv, L0_attn_att_wr, L0_attn_att_wo, L0_attn_ffn_mix_k, L0_attn_ffn_mix_r, L0_attn_ffn_wk, L0_attn_ffn_wv, L0_attn_ffn_wr)
    g = _silu(_L0_ffn_ref(xn, L0_ffn_router_w, L0_ffn_router_b, L0_ffn_w1, L0_ffn_b1, L0_ffn_w2, L0_ffn_b2, L0_ffn_ow1, L0_ffn_ob1, L0_ffn_ow2, L0_ffn_ob2))
    x = x + s * g
    return x

_drawn_inputs = setup_inputs


def setup_inputs(seed=0):
    import zlib

    import numpy as np

    out = dict(_drawn_inputs(seed))
    spreads = {'L0_attn_ln_att_g': (1.0, 0.6),
     'L0_attn_ln_att_b': (0.0, 0.8),
     'L0_attn_ln_ffn_g': (1.0, 0.6),
     'L0_attn_ln_ffn_b': (0.0, 0.8),
     'L0_ffn_router_b': (0.0, 0.1),
     'L0_ffn_b1': (0.0, 0.666),
     'L0_ffn_b2': (0.0, 0.1),
     'L0_ffn_ob1': (0.0, 0.8),
     'L0_ffn_ob2': (0.0, 0.1)}
    factors = {'L0_attn_att_time_decay': 8.0,
     'L0_attn_att_time_first': 8.0,
     'L0_attn_att_mix_k': 8.0,
     'L0_attn_att_mix_v': 8.0,
     'L0_attn_att_mix_r': 8.0,
     'L0_attn_att_wk': 8.0,
     'L0_attn_att_wv': 8.0,
     'L0_attn_att_wr': 8.0,
     'L0_attn_att_wo': 8.0,
     'L0_attn_ffn_mix_k': 8.0,
     'L0_attn_ffn_mix_r': 8.0,
     'L0_attn_ffn_wk': 8.0,
     'L0_attn_ffn_wv': 8.0,
     'L0_attn_ffn_wr': 8.0,
     'L0_ffn_ow1': 2.956}
    for name, (base, spread) in spreads.items():
        noise = np.random.default_rng([zlib.crc32(name.encode()), seed]).standard_normal(out[name].shape)
        drawn = base * np.exp(spread * noise) if base else spread * noise
        out[name] = jnp.asarray(drawn.astype(out[name].dtype))
    for name, factor in factors.items():
        out[name] = (out[name] * factor).astype(out[name].dtype)
    return out
```

```python
from contextlib import ExitStack

import concourse.bass as bass
from concourse import mybir

ALU = mybir.AluOpType
ACT = mybir.ActivationFunctionType
F32 = mybir.dt.float32
I32 = mybir.dt.int32
AX_X = mybir.AxisListType.X

P = 128
EPS = 1e-5
CAPACITY = 160
NO_STATE = -1e38
SKIP = 4096.0

PARAMS = {"ln_att_g": 1, "ln_att_b": 1, "ln_ffn_g": 1, "ln_ffn_b": 1, "decay": 1, "first": 1, "mix_k": 1, "mix_v": 1,
          "mix_r": 1, "ffn_mix_k": 1, "ffn_mix_r": 1, "ob2": 1, "ob1": 4, "b1": 32, "b2": 8, "router_b": 8, "router_w": 8}
WEIGHTS = {"wk": 128, "wv": 128, "wr": 128, "wo": 128, "ffn_wr": 128, "ffn_wk": 512, "ffn_wv": 512, "ow1": 512, "ow2": 512}
EARLY_WEIGHTS = 3 * P

SEMAPHORES = """
x_loaded0 x_loaded1 x_loaded2 x_loaded3 params_loaded early_weights_loaded weights_loaded
w1_loaded0 w1_loaded1 w1_loaded2 w1_loaded3 w2_loaded0 w2_loaded1 w2_loaded2 w2_loaded3
ident_cleared ident_ready tri_ready ones_ready pow_ready expert_code_ready run_mask_set run_mask_ready zeros_ready
column_zeroed state_zeroed decay_exp w_ready buf_zeroed
x_stats x_mv x_var_eps x_rstd xn_ready xn_stats xn_mv xn_var_eps xn_rstd h_ready
xn_turned h_turned xnT_ready hT_ready hT_diff mixed_k mixed_v mixed_r k_done v_done r_done k_ready v_ready r_ready
logits_done logits_biased logit_max is_max max_code code_max onehot_ready counts_done counts_run rank_a rank_b rank_hot
rank_ready expert_base slot_a slot_over slot_b slot_ready scattered buf_loaded buf_turned bufT_ready
o_ready gap_t gap_s gap_max gap_min exp_neg exp_pos bv2_ready bv_ready p_ready q_ready ap_ready aq_ready num_ready den_ready
den_ln den_inv rn_ready newton_a newton_b wkvT_ready
att_done x2_ready x2_stats x2_mv x2_var_eps x2_rstd h3_ready h3_turned h3T_ready h3_diff mixed_fk mixed_fr
over_hidden_done over_hidden_ready over_out_done over_outT_ready over_turned over_ready
hidden_done hidden_ready y_done yT_ready y_turned y_rows_ready y_stored0 y_stored1 gathered
ffn_hidden_done ffn_relu_ready ffn_hidden_ready ffn_r_done rf_ready ffn_out_done ffn_gated ffn_turned s_ready
gate_sigmoid gate_ready s_gated out_ready out_stored
""".split()


def columns(table):
    at, out = 0, {}
    for name, n in table.items():
        out[name] = (at, at + n)
        at += n
    return out


def build(nc, x, params, weights, w1, w2, out):
    n_tokens = x.shape[0]
    TILES = n_tokens // P
    CHUNK = 4
    BLOCKS = TILES // CHUNK
    NB = CHUNK * P
    SEQ = n_tokens // 2
    E, D, H = w1.shape
    HC = H // P
    SLOTS = E * CAPACITY
    SLOT_TILES = SLOTS // P
    HALF = CAPACITY // 2
    RING = 4
    pcol, wcol = columns(PARAMS), columns(WEIGHTS)

    x_tiles = x.rearrange("(t p) d -> p t d", p=P)
    out_tiles = out.rearrange("(t p) d -> p t d", p=P)
    slot_rows = nc.dram_tensor("slot_rows", (SLOTS, D), F32, kind="Internal").ap()
    y_rows = nc.dram_tensor("y_rows", (SLOTS, D), F32, kind="Internal").ap()

    with ExitStack() as ctx:
        def sb(name, shape, dt=F32):
            return ctx.enter_context(nc.sbuf_tensor(name, shape, dt))

        s = {n: ctx.enter_context(nc.semaphore(n)) for n in SEMAPHORES}
        x_loaded = [s["x_loaded0"], s["x_loaded1"], s["x_loaded2"], s["x_loaded3"]]
        y_stored = [s["y_stored0"], s["y_stored1"]]
        w1_loaded = [s["w1_loaded0"], s["w1_loaded1"], s["w1_loaded2"], s["w1_loaded3"]]
        w2_loaded = [s["w2_loaded0"], s["w2_loaded1"], s["w2_loaded2"], s["w2_loaded3"]]
        bank = [ctx.enter_context(nc.psum_tensor(f"bank{i}", [P, 512], F32)) for i in range(8)]

        par = sb("par", [P, sum(PARAMS.values())])
        wts = sb("wts", [P, sum(WEIGHTS.values())])
        w1_sb = sb("w1_sb", [P, RING, H])
        w2_sb = sb("w2_sb", [P, RING, HC, D])
        ident = sb("ident", [P, P])
        tri = sb("tri", [P, P])
        ones = sb("ones", [P, P])
        zeros = sb("zeros", [P, D])
        minus_half = sb("minus_half", [P, TILES])
        expert_code = sb("expert_code", [P, E, TILES])
        run_mask = sb("run_mask", [P, E, TILES])
        w_neg = sb("w_neg", [P, 1])
        w_exp = sb("w_exp", [P, 1])

        x_sb = sb("x_sb", [P, TILES, D])
        xn = sb("xn", [P, TILES, D])
        h_tok = sb("h_tok", [P, 2, CHUNK, D])
        stats = sb("stats", [P, 3, TILES, 6])
        mv = sb("mv", [P, 3, TILES, 2])
        var_eps = sb("var_eps", [P, 3, TILES])
        rstd = sb("rstd", [P, 3, TILES])
        xnT = sb("xnT", [P, n_tokens])
        hT = sb("hT", [P, 2, SEQ + 1])
        diff = sb("diff", [P, 2, NB])
        mixed = sb("mixed", [P, 2, 3, NB])
        kT = sb("kT", [P, n_tokens])
        vT = sb("vT", [P, n_tokens])
        rT = sb("rT", [P, n_tokens])

        logits = sb("logits", [P, E, TILES])
        row_max = sb("row_max", [P, TILES])
        is_max = sb("is_max", [P, E, TILES])
        code = sb("code", [P, E, TILES])
        code_max = sb("code_max", [P, TILES])
        onehot = sb("onehot", [P, E, TILES])
        counts = sb("counts", [P, E, TILES])
        rank_e = sb("rank_e", [P, E, TILES])
        rank = sb("rank", [P, TILES])
        base = sb("base", [P, TILES])
        over = sb("over", [P, TILES])
        slot_f = sb("slot_f", [P, TILES])
        slot = sb("slot", [P, TILES], I32)

        o_state = sb("o_state", [P, 2, SEQ + 1])
        p_state = sb("p_state", [P, 2, SEQ + 1])
        q_state = sb("q_state", [P, 2, SEQ + 1])
        gap = sb("gap", [P, 2, 2, NB])
        e_neg = sb("e_neg", [P, 2, 2, NB])
        e_pos = gap
        bv = sb("bv", [P, 2, NB])
        bv2 = sb("bv2", [P, 2, NB])
        num = sb("num", [P, 2, NB])
        den = bv2
        inv = sb("inv", [P, 2, NB])
        inv_err = sb("inv_err", [P, 2, NB])
        den_log = inv_err
        wkvT = sb("wkvT", [P, 2, NB])

        x2 = xn
        rfT = rT[:, 0:2 * NB].rearrange("p (i n) -> p i n", i=2)
        hid = sb("hid", [P, 2, HC, NB])
        e_hid = hid[:, :, 0:2, :].rearrange("p i c n -> p i (c n)")[:, :, 0:HC * CAPACITY].rearrange(
            "p i (c n) -> p i c n", c=HC)
        over_outT = sb("over_outT", [P, 2, NB])
        yT = over_outT[:, :, 0:CAPACITY]
        gatedT = over_outT
        moe = sb("moe", [P, TILES, D])
        buf_rows = mixed[:, :, :, :].rearrange("p i n c -> p (i n c)")[:, 0:SLOT_TILES * D].rearrange(
            "p (t d) -> p t d", d=D)
        bufT = xnT
        y_sb = sb("y_sb", [HALF, 2, 2, D])
        gate = kT[:, :].rearrange("p (t d) -> p t d", d=D)

        def param(name, i=0):
            at = pcol[name][0] + i
            return par[:, at:at + 1]

        def weight(name, c=0):
            at = wcol[name][0] + c * P
            return wts[:, at:at + P]

        def seq_cols(b, shift):
            at = (b % 2) * NB + shift
            return b // 2, slice(at, at + NB)

        def blk(b):
            return slice(b * NB, (b + 1) * NB)

        def tls(b):
            return slice(b * CHUNK, (b + 1) * CHUNK)

        block = ctx.enter_context(nc.Block())

        @block.sync
        def _(sp):
            for b in range(BLOCKS):
                sp.dma_start(x_sb[:, tls(b), :], x_tiles[:, tls(b), :]).then_inc(x_loaded[b], 16)

            def load_expert(e):
                sp.dma_start(w1_sb[:, e % RING, :], w1[e]).then_inc(w1_loaded[e % RING], 16)
                sp.dma_start(w2_sb[:, e % RING, :, :], w2[e].rearrange("(c p) d -> p c d", p=P)).then_inc(
                    w2_loaded[e % RING], 16)

            sp.wait_ge(s["zeros_ready"], 1)
            sp.dma_start(slot_rows.rearrange("(p r) d -> p r d", p=P),
                         zeros[:, :].unsqueeze(1).to_broadcast([P, SLOT_TILES, D])).then_inc(s["buf_zeroed"], 16)
            for e in range(RING):
                load_expert(e)
            sp.wait_ge(s["r_done"], BLOCKS)
            sp.wait_ge(s["scattered"], 16 * TILES)
            sp.dma_start(buf_rows[:, :, :], slot_rows.rearrange("(t p) d -> p t d", p=P)).then_inc(s["buf_loaded"], 16)
            for e in range(E):
                sp.wait_ge(s["y_rows_ready"], e + 1)
                sp.dma_start(y_rows.rearrange("(e a p) d -> p e a d", e=E, a=2)[:, e], y_sb[:, e % 2, :, :]).then_inc(
                    y_stored[e % 2], 16)
                if e + RING < E:
                    sp.wait_ge(s["y_done"], e + 1)
                    load_expert(e + RING)
            for b in range(BLOCKS):
                sp.wait_ge(s["out_ready"], b + 1)
                sp.dma_start(out_tiles[:, tls(b), :], x_sb[:, tls(b), :]).then_inc(s["out_stored"], 16)
            sp.wait_ge(s["out_stored"], 16 * BLOCKS)

        @block.gpsimd
        def _(pool):
            nc.gpsimd.memset(minus_half[:], -0.5).then_inc(s["pow_ready"], 1)
            nc.gpsimd.memset(ident[:], 0.0).then_inc(s["ident_cleared"], 1)
            nc.gpsimd.memset(ones[:], 1.0).then_inc(s["ones_ready"], 1)
            pool.wait_ge(s["ident_cleared"], 1)
            nc.gpsimd.affine_select(out=ident[:], in_=ident[:], compare_op=ALU.not_equal, fill=1.0, base=0,
                                    pattern=[[-1, P]], channel_multiplier=1).then_inc(s["ident_ready"], 1)
            pool.wait_ge(s["pow_ready"], 1)

            def root(n, var_ready, eps_done, rstd_done, b):
                pool.wait_ge(var_ready, CHUNK * (b + 1))
                nc.gpsimd.tensor_scalar(var_eps[:, n, tls(b)], mv[:, n, tls(b), 1], EPS, 1.0, ALU.add,
                                        ALU.mult).then_inc(eps_done, 1)
                pool.wait_ge(eps_done, b + 1)
                nc.gpsimd.tensor_tensor(rstd[:, n, tls(b)], var_eps[:, n, tls(b)], minus_half[:, tls(b)],
                                        ALU.pow).then_inc(rstd_done, 1)

            root(0, s["x_mv"], s["x_var_eps"], s["x_rstd"], 0)
            nc.gpsimd.memset(hT[:, :, 0:1], 0.0).then_inc(s["column_zeroed"], 1)
            for b in range(BLOCKS):
                if b + 1 < BLOCKS:
                    root(0, s["x_mv"], s["x_var_eps"], s["x_rstd"], b + 1)
                root(1, s["xn_mv"], s["xn_var_eps"], s["xn_rstd"], b)

            pool.wait_ge(s["ones_ready"], 1)
            nc.gpsimd.affine_select(out=tri[:], in_=ones[:], compare_op=ALU.is_ge, fill=0.0, base=0,
                                    pattern=[[1, P]], channel_multiplier=-1).then_inc(s["tri_ready"], 1)
            nc.gpsimd.iota(expert_code[:, :, :], [[-1, E], [0, TILES]], base=E, channel_multiplier=0,
                           allow_small_or_imprecise_dtypes=True).then_inc(s["expert_code_ready"], 1)
            nc.gpsimd.memset(run_mask[:], 1.0).then_inc(s["run_mask_set"], 1)
            pool.wait_ge(s["run_mask_set"], 1)
            nc.gpsimd.memset(run_mask[:, :, 0:1], 0.0).then_inc(s["run_mask_ready"], 1)
            nc.gpsimd.memset(zeros[:], 0.0).then_inc(s["zeros_ready"], 1)
            nc.gpsimd.memset(o_state[:, :, 0:1], NO_STATE).then_inc(s["state_zeroed"], 1)
            nc.gpsimd.memset(p_state[:, :, 0:1], 0.0).then_inc(s["state_zeroed"], 1)
            nc.gpsimd.memset(q_state[:, :, 0:1], 0.0).then_inc(s["state_zeroed"], 1)

            def scatter(t):
                nc.gpsimd.indirect_dma_start(slot_rows, bass.IndirectOffsetOnAxis(ap=slot[:, t:t + 1], axis=0),
                                             xn[:, t, :], None, bounds_check=SLOTS - 1,
                                             oob_is_err=False).then_inc(s["scattered"], 16)

            def wkv_products(b):
                i = b % 2
                if b >= 2:
                    pool.wait_ge(s["wkvT_ready"], b - 1)
                pool.wait_ge(s["v_ready"], b + 1)
                pool.wait_ge(s["exp_neg"], b + 1)
                nc.gpsimd.tensor_tensor(bv2[:, i, :], e_neg[:, i, 1, :], vT[:, blk(b)], ALU.mult).then_inc(s["bv2_ready"], 1)
                pool.wait_ge(s["exp_pos"], b + 1)
                nc.gpsimd.tensor_tensor(bv[:, i, :], e_pos[:, i, 0, :], vT[:, blk(b)], ALU.mult).then_inc(s["bv_ready"], 1)

            def wkv_times_r(b):
                i = b % 2
                pool.wait_ge(s["num_ready"], b + 1)
                pool.wait_ge(s["r_ready"], b + 1)
                nc.gpsimd.tensor_tensor(bv[:, i, :], num[:, i, :], rT[:, blk(b)], ALU.mult).then_inc(s["rn_ready"], 1)

            pool.wait_ge(s["slot_ready"], 1)
            pool.wait_ge(s["buf_zeroed"], 16)
            for t in range(TILES // 2):
                scatter(t)
            wkv_products(0)
            for t in range(TILES // 2, TILES):
                scatter(t)
            wkv_products(1)
            wkv_times_r(0)
            wkv_products(2)
            wkv_times_r(1)
            wkv_products(3)
            root(2, s["x2_mv"], s["x2_var_eps"], s["x2_rstd"], 0)
            wkv_times_r(2)
            root(2, s["x2_mv"], s["x2_var_eps"], s["x2_rstd"], 1)
            wkv_times_r(3)
            root(2, s["x2_mv"], s["x2_var_eps"], s["x2_rstd"], 2)
            root(2, s["x2_mv"], s["x2_var_eps"], s["x2_rstd"], 3)

            pool.wait_ge(s["over_ready"], BLOCKS)
            for stored in y_stored:
                pool.wait_ge(stored, 16 * E // 2)
            for t in range(TILES):
                nc.gpsimd.indirect_dma_start(moe[:, t, :], None, y_rows,
                                             bass.IndirectOffsetOnAxis(ap=slot[:, t:t + 1], axis=0),
                                             bounds_check=SLOTS - 1, oob_is_err=False).then_inc(s["gathered"], 16)
            for b in range(BLOCKS):
                pool.wait_ge(s["gate_sigmoid"], b + 1)
                nc.gpsimd.tensor_tensor(gate[:, tls(b), :], gate[:, tls(b), :], moe[:, tls(b), :],
                                        ALU.mult).then_inc(s["gate_ready"], 1)

        @block.tensor
        def _(pe):
            def turn_tokens(b):
                if b == 0:
                    pe.wait_ge(s["ident_ready"], 1)
                if b >= 2:
                    pe.wait_ge(s["xnT_ready"], b - 1)
                pe.wait_ge(s["xn_ready"], CHUNK * (b + 1))
                for t in range(CHUNK):
                    last = nc.tensor.transpose(bank[b % 2][:, t * P:(t + 1) * P], xn[:, b * CHUNK + t, :], ident[:])
                last.then_inc(s["xn_turned"], 1)
                if b >= 2:
                    pe.wait_ge(s["hT_ready"], b - 1)
                pe.wait_ge(s["h_ready"], CHUNK * (b + 1))
                for t in range(CHUNK):
                    last = nc.tensor.transpose(bank[2 + b % 2][:, t * P:(t + 1) * P], h_tok[:, b % 2, t, :],
                                               ident[:])
                last.then_inc(s["h_turned"], 1)

            def project(b):
                if b == 0:
                    pe.wait_ge(s["early_weights_loaded"], 16)
                for n, (name, ready, used, done) in enumerate((
                        ("wk", s["mixed_k"], s["k_ready"], s["k_done"]), ("wv", s["mixed_v"], s["v_ready"], s["v_done"]),
                        ("wr", s["mixed_r"], s["r_ready"], s["r_done"]))):
                    pe.wait_ge(ready, b + 1)
                    if b:
                        pe.wait_ge(used, b)
                    nc.tensor.matmul(bank[4 + n][:, :], weight(name), mixed[:, b % 2, n, :], start=True,
                                     stop=True).then_inc(done, 1)

            def route_logits():
                pe.wait_ge(s["params_loaded"], 16)
                pe.wait_ge(s["xnT_ready"], BLOCKS)
                at = pcol["router_w"][0]
                for t in range(TILES):
                    last = nc.tensor.matmul(bank[7][:, 0:E * TILES].rearrange("p (e t) -> p e t", e=E)[:, :, t],
                                            xnT[:, t * P:(t + 1) * P], par[:, at:at + E], start=True, stop=True)
                last.then_inc(s["logits_done"], 1)

            def count_tokens():
                pe.wait_ge(s["onehot_ready"], 1)
                pe.wait_ge(s["tri_ready"], 1)
                flat = onehot[:, :, :].rearrange("p e t -> p (e t)")
                nc.tensor.matmul(bank[7][:, 128:256], tri[:], flat, start=True, stop=True)
                nc.tensor.matmul(bank[7][:, 256:384], ones[:], flat, start=True, stop=True).then_inc(s["counts_done"], 1)

            def overflow_hidden(b):
                if b == 0:
                    pe.wait_ge(s["weights_loaded"], 16)
                for c in range(HC):
                    n = b * HC + c
                    if n < 4:
                        pe.wait_ge(s["xnT_ready"] if n < 2 else s["hT_ready"], BLOCKS)
                    else:
                        pe.wait_ge(s["over_hidden_ready"], n - 3)
                    nc.tensor.matmul(bank[n % 4][:, :], weight("ow1", c), xnT[:, blk(b)], start=True,
                                     stop=True).then_inc(s["over_hidden_done"], 1)

            def overflow_out(b):
                if b == 0:
                    pe.wait_ge(s["k_ready"], BLOCKS)
                else:
                    pe.wait_ge(s["over_outT_ready"], b)
                for c in range(HC):
                    pe.wait_ge(s["over_hidden_ready"], b * HC + c + 1)
                    last = nc.tensor.matmul(bank[4][:, :], weight("ow2", c), hid[:, b % 2, c, :], start=(c == 0),
                                            stop=(c == HC - 1))
                last.then_inc(s["over_out_done"], 1)

            def overflow_turn(b):
                if b == 0:
                    pe.wait_ge(s["r_ready"], BLOCKS)
                else:
                    pe.wait_ge(s["over_ready"], b)
                pe.wait_ge(s["over_outT_ready"], b + 1)
                for t in range(CHUNK):
                    last = nc.tensor.transpose(bank[6][:, t * P:(t + 1) * P], over_outT[:, b % 2, t * P:(t + 1) * P],
                                               ident[:])
                last.then_inc(s["over_turned"], 1)

            def turn_slots(g):
                if g == 0:
                    pe.wait_ge(s["over_ready"], BLOCKS)
                    pe.wait_ge(s["buf_loaded"], 16)
                else:
                    pe.wait_ge(s["bufT_ready"], g)
                for n, t in enumerate(range(4 * g, min(4 * g + 4, SLOT_TILES))):
                    last = nc.tensor.transpose(bank[6][:, n * P:(n + 1) * P], buf_rows[:, t, :], ident[:])
                last.then_inc(s["buf_turned"], 1)

            def expert_hidden(e):
                pe.wait_ge(w1_loaded[e % RING], 16 * (e // RING + 1))
                pe.wait_ge(s["bufT_ready"], min(3, -(-(e + 1) * CAPACITY // NB)))
                for c in range(HC):
                    n = e * HC + c
                    if n < 4:
                        pe.wait_ge(s["over_hidden_ready"], BLOCKS * HC - 3 + n)
                    else:
                        pe.wait_ge(s["hidden_ready"], n - 3)
                    nc.tensor.matmul(bank[n % 4][:, 0:CAPACITY], w1_sb[:, e % RING, c * P:(c + 1) * P],
                                     bufT[:, e * CAPACITY:(e + 1) * CAPACITY], start=True,
                                     stop=True).then_inc(s["hidden_done"], 1)

            def expert_out(e):
                pe.wait_ge(w2_loaded[e % RING], 16 * (e // RING + 1))
                if e == 0:
                    pe.wait_ge(s["over_outT_ready"], BLOCKS)
                else:
                    pe.wait_ge(s["yT_ready"], e)
                for c in range(HC):
                    pe.wait_ge(s["hidden_ready"], e * HC + c + 1)
                    last = nc.tensor.matmul(bank[4][:, 0:CAPACITY], w2_sb[:, e % RING, c, :], e_hid[:, e % 2, c, :],
                                            start=(c == 0), stop=(c == HC - 1))
                last.then_inc(s["y_done"], 1)

            def expert_turn(e):
                if e == 0:
                    pe.wait_ge(s["bufT_ready"], 3)
                else:
                    pe.wait_ge(s["y_rows_ready"], e)
                pe.wait_ge(s["yT_ready"], e + 1)
                for a in range(2):
                    last = nc.tensor.transpose(bank[6][0:HALF, a * P:(a + 1) * P], yT[:, e % 2, a * HALF:(a + 1) * HALF],
                                               ident[:])
                last.then_inc(s["y_turned"], 1)

            def attention_out(b):
                if b == 0:
                    pe.wait_ge(s["rank_b"], 1)
                else:
                    pe.wait_ge(s["x2_ready"], b)
                pe.wait_ge(s["wkvT_ready"], b + 1)
                for t in range(CHUNK):
                    last = nc.tensor.matmul(bank[7][:, t * P:(t + 1) * P], wkvT[:, b % 2, t * P:(t + 1) * P],
                                            weight("wo"), start=True, stop=True)
                last.then_inc(s["att_done"], 1)

            def turn_h3(b):
                if b == 0:
                    pe.wait_ge(s["v_ready"], BLOCKS)
                else:
                    pe.wait_ge(s["h3T_ready"], b)
                pe.wait_ge(s["h3_ready"], CHUNK * (b + 1))
                for t in range(CHUNK):
                    last = nc.tensor.transpose(bank[5][:, t * P:(t + 1) * P], h_tok[:, b % 2, t, :], ident[:])
                last.then_inc(s["h3_turned"], 1)

            def ffn_hidden(b):
                pe.wait_ge(s["mixed_fk"], b + 1)
                for c in range(HC):
                    n = b * HC + c
                    if n < 4:
                        pe.wait_ge(s["hidden_ready"], E * HC - 3 + n)
                    else:
                        pe.wait_ge(s["ffn_hidden_ready"], n - 3)
                    nc.tensor.matmul(bank[n % 4][:, :], weight("ffn_wk", c), mixed[:, b % 2, 0, :], start=True,
                                     stop=True).then_inc(s["ffn_hidden_done"], 1)

            def ffn_gate(b):
                pe.wait_ge(s["mixed_fr"], b + 1)
                pe.wait_ge(s["h3T_ready"], BLOCKS)
                if b:
                    pe.wait_ge(s["rf_ready"], b)
                nc.tensor.matmul(bank[5][:, :], weight("ffn_wr"), mixed[:, b % 2, 1, :], start=True,
                                 stop=True).then_inc(s["ffn_r_done"], 1)

            def ffn_out(b):
                if b == 0:
                    pe.wait_ge(s["yT_ready"], E)
                else:
                    pe.wait_ge(s["ffn_gated"], b)
                for c in range(HC):
                    pe.wait_ge(s["ffn_hidden_ready"], b * HC + c + 1)
                    last = nc.tensor.matmul(bank[4][:, :], weight("ffn_wv", c), hid[:, b % 2, c, :], start=(c == 0),
                                            stop=(c == HC - 1))
                last.then_inc(s["ffn_out_done"], 1)

            def ffn_turn(b):
                if b == 0:
                    pe.wait_ge(s["y_rows_ready"], E)
                else:
                    pe.wait_ge(s["s_ready"], b)
                pe.wait_ge(s["ffn_gated"], b + 1)
                for t in range(CHUNK):
                    last = nc.tensor.transpose(bank[6][:, t * P:(t + 1) * P], gatedT[:, b % 2, t * P:(t + 1) * P],
                                               ident[:])
                last.then_inc(s["ffn_turned"], 1)

            turn_tokens(0)
            turn_tokens(1)
            project(0)
            turn_tokens(2)
            project(1)
            turn_tokens(3)
            route_logits()
            project(2)
            count_tokens()
            project(3)
            overflow_hidden(0)
            overflow_hidden(1)
            overflow_out(0)
            overflow_hidden(2)
            overflow_turn(0)
            overflow_out(1)
            overflow_hidden(3)
            overflow_turn(1)
            attention_out(0)
            overflow_out(2)
            overflow_turn(2)
            overflow_out(3)
            overflow_turn(3)
            for g in range(3):
                turn_slots(g)
            expert_hidden(0)
            attention_out(1)
            for e in range(1, E + 1):
                if e < E:
                    expert_hidden(e)
                expert_out(e - 1)
                if e >= 2:
                    expert_turn(e - 2)
                if e == 4:
                    turn_h3(0)
                if e == 5:
                    attention_out(2)
                if e == 7:
                    turn_h3(1)
            expert_turn(E - 1)
            attention_out(3)
            turn_h3(2)
            ffn_hidden(0)
            turn_h3(3)
            ffn_gate(0)
            for b in range(1, BLOCKS):
                ffn_hidden(b)
                ffn_out(b - 1)
                ffn_gate(b)
                ffn_turn(b - 1)
            ffn_out(BLOCKS - 1)
            ffn_turn(BLOCKS - 1)

        @block.scalar
        def _(act):
            act.dma_start(par[:, :], params).then_inc(s["params_loaded"], 16)
            act.dma_start(wts[:, 0:EARLY_WEIGHTS], weights[:, 0:EARLY_WEIGHTS]).then_inc(s["early_weights_loaded"], 16)
            act.dma_start(wts[:, EARLY_WEIGHTS:], weights[:, EARLY_WEIGHTS:]).then_inc(s["weights_loaded"], 16)
            act.wait_ge(s["params_loaded"], 16)
            nc.scalar.activation(w_exp[:], param("decay"), ACT.Exp).then_inc(s["decay_exp"], 1)

            def copy_tokens(b):
                act.wait_ge(s["xn_turned"], b + 1)
                nc.scalar.copy(xnT[:, blk(b)], bank[b % 2][:, :]).then_inc(s["xnT_ready"], 1)
                act.wait_ge(s["h_turned"], b + 1)
                q, cols = seq_cols(b, 1)
                nc.scalar.activation(hT[:, q, cols], bank[2 + b % 2][:, :], ACT.Identity, bias=param("ln_att_b"),
                                     scale=param("ln_att_g")).then_inc(s["hT_ready"], 1)

            def copy_projected(b):
                act.wait_ge(s["k_done"], b + 1)
                nc.scalar.copy(kT[:, blk(b)], bank[4][:, :]).then_inc(s["k_ready"], 1)
                act.wait_ge(s["v_done"], b + 1)
                nc.scalar.copy(vT[:, blk(b)], bank[5][:, :]).then_inc(s["v_ready"], 1)
                act.wait_ge(s["r_done"], b + 1)
                nc.scalar.activation(rT[:, blk(b)], bank[6][:, :], ACT.Sigmoid).then_inc(s["r_ready"], 1)

            def wkv_exponentials(b):
                i = b % 2
                act.wait_ge(s["gap_max"], b + 1)
                nc.scalar.activation(e_neg[:, i, :, :], e_neg[:, i, :, :], ACT.Exp, scale=-1.0).then_inc(s["exp_neg"], 1)
                act.wait_ge(s["gap_min"], b + 1)
                nc.scalar.activation(e_pos[:, i, :, :], e_pos[:, i, :, :], ACT.Exp).then_inc(s["exp_pos"], 1)

            def wkv_reciprocal(b):
                i = b % 2
                act.wait_ge(s["den_ready"], b + 1)
                if b >= 2:
                    act.wait_ge(s["wkvT_ready"], b - 1)
                nc.scalar.activation(den_log[:, i, :], den[:, i, :], ACT.Ln).then_inc(s["den_ln"], 1)
                act.wait_ge(s["den_ln"], b + 1)
                nc.scalar.activation(inv[:, i, :], den_log[:, i, :], ACT.Exp, scale=-1.0).then_inc(s["den_inv"], 1)

            def overflow_relu(b):
                if b >= 2:
                    act.wait_ge(s["over_out_done"], b - 1)
                for c in range(HC):
                    n = b * HC + c
                    act.wait_ge(s["over_hidden_done"], n + 1)
                    nc.scalar.activation(hid[:, b % 2, c, :], bank[n % 4][:, :], ACT.Relu,
                                         bias=param("ob1", c)).then_inc(s["over_hidden_ready"], 1)

            def overflow_bias(b):
                act.wait_ge(s["over_out_done"], b + 1)
                if b >= 2:
                    act.wait_ge(s["over_turned"], b - 1)
                nc.scalar.activation(over_outT[:, b % 2, :], bank[4][:, :], ACT.Identity,
                                     bias=param("ob2")).then_inc(s["over_outT_ready"], 1)

            def overflow_tokens(b):
                act.wait_ge(s["over_turned"], b + 1)
                nc.scalar.copy(moe[:, tls(b), :], bank[6][:, :].rearrange("p (t d) -> p t d", d=D)).then_inc(
                    s["over_ready"], 1)

            def copy_slots(g):
                act.wait_ge(s["buf_turned"], g + 1)
                n = min(NB, SLOTS - g * NB)
                nc.scalar.copy(bufT[:, g * NB:g * NB + n], bank[6][:, 0:n]).then_inc(s["bufT_ready"], 1)

            def expert_relu(e):
                if e == 0:
                    act.wait_ge(s["over_out_done"], BLOCKS)
                if e >= 2:
                    act.wait_ge(s["y_done"], e - 1)
                for c in range(HC):
                    n = e * HC + c
                    act.wait_ge(s["hidden_done"], n + 1)
                    nc.scalar.activation(e_hid[:, e % 2, c, :], bank[n % 4][:, 0:CAPACITY], ACT.Relu,
                                         bias=param("b1", n)).then_inc(s["hidden_ready"], 1)

            def expert_bias(e):
                act.wait_ge(s["y_done"], e + 1)
                if e == 0:
                    act.wait_ge(s["over_turned"], BLOCKS)
                if e >= 2:
                    act.wait_ge(s["y_turned"], e - 1)
                nc.scalar.activation(yT[:, e % 2, :], bank[4][:, 0:CAPACITY], ACT.Identity,
                                     bias=param("b2", e)).then_inc(s["yT_ready"], 1)

            def expert_rows(e):
                act.wait_ge(s["y_turned"], e + 1)
                if e >= 2:
                    act.wait_ge(y_stored[e % 2], 16 * (e // 2))
                nc.scalar.copy(y_sb[:, e % 2, :, :], bank[6][0:HALF, 0:2 * P].rearrange("p (a d) -> p a d", a=2)).then_inc(
                    s["y_rows_ready"], 1)

            def copy_h3(b):
                act.wait_ge(s["h3_turned"], b + 1)
                if b == 0:
                    act.wait_ge(s["mixed_r"], BLOCKS)
                q, cols = seq_cols(b, 1)
                nc.scalar.activation(hT[:, q, cols], bank[5][:, :], ACT.Identity, bias=param("ln_ffn_b"),
                                     scale=param("ln_ffn_g")).then_inc(s["h3T_ready"], 1)

            def ffn_relu(b):
                for c in range(HC):
                    n = b * HC + c
                    act.wait_ge(s["ffn_hidden_done"], n + 1)
                    if n == 0:
                        act.wait_ge(s["y_done"], E)
                    if b >= 2:
                        act.wait_ge(s["ffn_out_done"], b - 1)
                    nc.scalar.activation(hid[:, b % 2, c, :], bank[n % 4][:, :], ACT.Relu).then_inc(s["ffn_relu_ready"], 1)

            def ffn_sigmoid(b):
                act.wait_ge(s["ffn_r_done"], b + 1)
                if b == 0:
                    act.wait_ge(s["rn_ready"], BLOCKS)
                if b >= 2:
                    act.wait_ge(s["ffn_gated"], b - 1)
                nc.scalar.activation(rfT[:, b % 2, :], bank[5][:, :], ACT.Sigmoid).then_inc(s["rf_ready"], 1)

            def gate_sigmoid(b):
                act.wait_ge(s["gathered"], 16 * TILES)
                nc.scalar.activation(gate[:, tls(b), :], moe[:, tls(b), :], ACT.Sigmoid).then_inc(s["gate_sigmoid"], 1)

            copy_tokens(0)
            copy_tokens(1)
            copy_projected(0)
            copy_tokens(2)
            copy_projected(1)
            copy_tokens(3)
            copy_projected(2)
            copy_projected(3)
            wkv_exponentials(0)
            overflow_relu(0)
            overflow_relu(1)
            wkv_exponentials(1)
            overflow_bias(0)
            wkv_reciprocal(0)
            overflow_relu(2)
            overflow_tokens(0)
            overflow_bias(1)
            wkv_exponentials(2)
            overflow_relu(3)
            overflow_tokens(1)
            wkv_reciprocal(1)
            overflow_bias(2)
            overflow_tokens(2)
            wkv_exponentials(3)
            overflow_bias(3)
            overflow_tokens(3)
            for g in range(3):
                copy_slots(g)
            expert_relu(0)
            wkv_reciprocal(2)
            for e in range(1, E + 1):
                if e < E:
                    expert_relu(e)
                expert_bias(e - 1)
                if e >= 2:
                    expert_rows(e - 2)
                if e == 4:
                    copy_h3(0)
                if e == 5:
                    wkv_reciprocal(3)
                if e == 7:
                    copy_h3(1)
            expert_rows(E - 1)
            copy_h3(2)
            ffn_relu(0)
            copy_h3(3)
            ffn_sigmoid(0)
            for b in range(1, BLOCKS):
                ffn_relu(b)
                ffn_sigmoid(b)
                gate_sigmoid(b - 1)
            gate_sigmoid(BLOCKS - 1)

        @block.vector
        def _(dve):
            def statistics(n, src, arrived, stats_done, mv_done, b):
                for t in range(b * CHUNK, (b + 1) * CHUNK):
                    arrived(t)
                    nc.vector.bn_stats(stats[:, n, t, :], src[:, t, :]).then_inc(stats_done, 1)
                for t in range(b * CHUNK, (b + 1) * CHUNK):
                    dve.wait_ge(stats_done, t + 1)
                    nc.vector.bn_aggr(mv[:, n, t, :], stats[:, n, t, :]).then_inc(mv_done, 1)

            def normalise(n, dst, src, rstd_done, done, b):
                dve.wait_ge(rstd_done, b + 1)
                for t in range(b * CHUNK, (b + 1) * CHUNK):
                    nc.vector.tensor_scalar(dst[:, t - b * CHUNK, :], src[:, t, :], mv[:, n, t, 0:1], rstd[:, n, t:t + 1],
                                            ALU.subtract, ALU.mult).then_inc(done, 1)

            def mix(b, ready, names, diffs, dones, first_use):
                dve.wait_ge(ready, b + 1)
                if b == 0:
                    dve.wait_ge(s["column_zeroed"], 1)
                q, here = seq_cols(b, 1)
                _, before = seq_cols(b, 0)
                nc.vector.tensor_tensor(diff[:, b % 2, :], hT[:, q, here], hT[:, q, before],
                                        ALU.subtract).then_inc(diffs, 1)
                dve.wait_ge(diffs, b + 1)
                first_use()
                for n, name in enumerate(names):
                    nc.vector.scalar_tensor_tensor(out=mixed[:, b % 2, n, :], in0=diff[:, b % 2, :], scalar=param(name),
                                                   in1=hT[:, q, before], op0=ALU.mult, op1=ALU.add).then_inc(dones[n], 1)

            def x_stats(b):
                statistics(0, x_sb, lambda t: dve.wait_ge(x_loaded[t // CHUNK], 16), s["x_stats"], s["x_mv"], b)

            def xn_and_stats(b):
                normalise(0, xn[:, tls(b), :], x_sb, s["x_rstd"], s["xn_ready"], b)
                statistics(1, xn, lambda t: dve.wait_ge(s["xn_ready"], t + 1), s["xn_stats"], s["xn_mv"], b)

            def h_normalise(b):
                if b >= 2:
                    dve.wait_ge(s["h_turned"], b - 1)
                normalise(1, h_tok[:, b % 2, :, :], xn, s["xn_rstd"], s["h_ready"], b)

            def att_mix(b):
                def first_use():
                    if b >= 2:
                        dve.wait_ge(s["r_done"], b - 1)
                mix(b, s["hT_ready"], ("mix_k", "mix_v", "mix_r"), s["hT_diff"], (s["mixed_k"], s["mixed_v"], s["mixed_r"]), first_use)

            def route_choose():
                at = pcol["router_b"][0]
                dve.wait_ge(s["logits_done"], 1)
                nc.vector.tensor_tensor(logits[:, :, :], bank[7][:, 0:E * TILES].rearrange("p (e t) -> p e t", e=E),
                                        par[:, at:at + E].unsqueeze(2).to_broadcast([P, E, TILES]),
                                        ALU.add).then_inc(s["logits_biased"], 1)
                dve.wait_ge(s["logits_biased"], 1)
                nc.vector.tensor_reduce(row_max[:, :], logits[:, :, :].rearrange("p e t -> p t e"), AX_X,
                                        ALU.max).then_inc(s["logit_max"], 1)
                dve.wait_ge(s["logit_max"], 1)
                nc.vector.tensor_tensor(is_max[:, :, :], logits[:, :, :], row_max[:, :].unsqueeze(1).to_broadcast([P, E, TILES]),
                                        ALU.is_equal).then_inc(s["is_max"], 1)
                dve.wait_ge(s["is_max"], 1)
                dve.wait_ge(s["expert_code_ready"], 1)
                nc.vector.tensor_tensor(code[:, :, :], is_max[:, :, :], expert_code[:, :, :], ALU.mult).then_inc(s["max_code"], 1)
                dve.wait_ge(s["max_code"], 1)
                nc.vector.tensor_reduce(code_max[:, :], code[:, :, :].rearrange("p e t -> p t e"), AX_X,
                                        ALU.max).then_inc(s["code_max"], 1)
                dve.wait_ge(s["code_max"], 1)
                nc.vector.tensor_tensor(onehot[:, :, :], expert_code[:, :, :],
                                        code_max[:, :].unsqueeze(1).to_broadcast([P, E, TILES]),
                                        ALU.is_equal).then_inc(s["onehot_ready"], 1)
                nc.vector.tensor_scalar(base[:, :], code_max[:, :], -float(CAPACITY), float(E * CAPACITY - 1), ALU.mult,
                                        ALU.add).then_inc(s["expert_base"], 1)

            def route_slots():
                in_tile = bank[7][:, 128:256]
                totals = bank[7][:, 256:384]
                dve.wait_ge(s["counts_done"], 1)
                dve.wait_ge(s["run_mask_ready"], 1)
                nc.vector.tensor_tensor_scan(counts[:, :, :].rearrange("p e t -> p (e t)"),
                                             run_mask[:, :, :].rearrange("p e t -> p (e t)"), totals, 0.0, ALU.mult,
                                             ALU.add).then_inc(s["counts_run"], 1)
                dve.wait_ge(s["counts_run"], 1)
                nc.vector.tensor_tensor(rank_e[:, :, :].rearrange("p e t -> p (e t)"), in_tile,
                                        counts[:, :, :].rearrange("p e t -> p (e t)"), ALU.add).then_inc(s["rank_a"], 1)
                dve.wait_ge(s["rank_a"], 1)
                nc.vector.tensor_tensor(code[:, :, :].rearrange("p e t -> p (e t)"),
                                        rank_e[:, :, :].rearrange("p e t -> p (e t)"), totals,
                                        ALU.subtract).then_inc(s["rank_b"], 1)
                dve.wait_ge(s["rank_b"], 1)
                nc.vector.tensor_tensor(rank_e[:, :, :], code[:, :, :], onehot[:, :, :], ALU.mult).then_inc(s["rank_hot"], 1)
                dve.wait_ge(s["rank_hot"], 1)
                nc.vector.tensor_reduce(rank[:, :], rank_e[:, :, :].rearrange("p e t -> p t e"), AX_X,
                                        ALU.add).then_inc(s["rank_ready"], 1)
                dve.wait_ge(s["rank_ready"], 1)
                nc.vector.tensor_tensor(slot_f[:, :], base[:, :], rank[:, :], ALU.add).then_inc(s["slot_a"], 1)
                nc.vector.tensor_scalar(over[:, :], rank[:, :], float(CAPACITY), SKIP, ALU.is_gt,
                                        ALU.mult).then_inc(s["slot_over"], 1)
                dve.wait_ge(s["slot_a"], 1)
                dve.wait_ge(s["slot_over"], 1)
                nc.vector.tensor_tensor(slot[:, :], slot_f[:, :], over[:, :], ALU.add).then_inc(s["slot_ready"], 1)

            def wkv_gaps(b):
                i, (q, here), (_, before) = b % 2, seq_cols(b, 1), seq_cols(b, 0)
                dve.wait_ge(s["k_ready"], b + 1)
                if b == 0:
                    dve.wait_ge(s["decay_exp"], 1)
                    nc.vector.tensor_scalar(w_neg[:], w_exp[:], -1.0, None, ALU.mult).then_inc(s["w_ready"], 1)
                    dve.wait_ge(s["w_ready"], 1)
                    dve.wait_ge(s["state_zeroed"], 3)
                else:
                    dve.wait_ge(s["o_ready"], b)
                nc.vector.tensor_tensor_scan(o_state[:, q, here], w_neg[:].to_broadcast([P, NB]), kT[:, blk(b)],
                                             o_state[:, q, before.start:before.start + 1], ALU.add,
                                             ALU.max).then_inc(s["o_ready"], 1)
                dve.wait_ge(s["o_ready"], b + 1)
                nc.vector.scalar_tensor_tensor(out=gap[:, i, 0, :], in0=kT[:, blk(b)], scalar=param("first"),
                                               in1=o_state[:, q, before], op0=ALU.add,
                                               op1=ALU.subtract).then_inc(s["gap_t"], 1)
                nc.vector.scalar_tensor_tensor(out=gap[:, i, 1, :], in0=o_state[:, q, before], scalar=w_neg[:],
                                               in1=kT[:, blk(b)], op0=ALU.add, op1=ALU.subtract).then_inc(s["gap_s"], 1)
                dve.wait_ge(s["gap_t"], b + 1)
                dve.wait_ge(s["gap_s"], b + 1)
                nc.vector.tensor_scalar(e_neg[:, i, :, :], gap[:, i, :, :], 0.0, None, ALU.max).then_inc(s["gap_max"], 1)
                nc.vector.tensor_scalar(e_pos[:, i, :, :], gap[:, i, :, :], 0.0, None, ALU.min).then_inc(s["gap_min"], 1)

            def wkv_states(b):
                i, (q, here), (_, before) = b % 2, seq_cols(b, 1), seq_cols(b, 0)
                start = slice(before.start, before.start + 1)
                dve.wait_ge(s["exp_neg"], b + 1)
                dve.wait_ge(s["exp_pos"], b + 1)
                if b:
                    dve.wait_ge(s["q_ready"], b)
                nc.vector.tensor_tensor_scan(q_state[:, q, here], e_pos[:, i, 1, :], e_neg[:, i, 1, :],
                                             q_state[:, q, start], ALU.mult, ALU.add).then_inc(s["q_ready"], 1)
                dve.wait_ge(s["bv2_ready"], b + 1)
                if b:
                    dve.wait_ge(s["p_ready"], b)
                nc.vector.tensor_tensor_scan(p_state[:, q, here], e_pos[:, i, 1, :], bv2[:, i, :],
                                             p_state[:, q, start], ALU.mult, ALU.add).then_inc(s["p_ready"], 1)
                dve.wait_ge(s["q_ready"], b + 1)
                dve.wait_ge(s["p_ready"], b + 1)
                nc.vector.tensor_tensor(den[:, i, :], e_neg[:, i, 0, :], q_state[:, q, before],
                                        ALU.mult).then_inc(s["aq_ready"], 1)
                nc.vector.tensor_tensor(num[:, i, :], e_neg[:, i, 0, :], p_state[:, q, before],
                                        ALU.mult).then_inc(s["ap_ready"], 1)
                dve.wait_ge(s["aq_ready"], b + 1)
                nc.vector.tensor_tensor(den[:, i, :], den[:, i, :], e_pos[:, i, 0, :], ALU.add).then_inc(s["den_ready"], 1)
                dve.wait_ge(s["ap_ready"], b + 1)
                dve.wait_ge(s["bv_ready"], b + 1)
                nc.vector.tensor_tensor(num[:, i, :], num[:, i, :], bv[:, i, :], ALU.add).then_inc(s["num_ready"], 1)

            def wkv_divide(b):
                i = b % 2
                dve.wait_ge(s["den_inv"], b + 1)
                nc.vector.tensor_tensor(inv_err[:, i, :], den[:, i, :], inv[:, i, :], ALU.mult).then_inc(s["newton_a"], 1)
                dve.wait_ge(s["newton_a"], b + 1)
                nc.vector.scalar_tensor_tensor(out=inv_err[:, i, :], in0=inv_err[:, i, :], scalar=-2.0, in1=inv[:, i, :],
                                               op0=ALU.add, op1=ALU.mult).then_inc(s["newton_b"], 1)
                dve.wait_ge(s["newton_b"], b + 1)
                dve.wait_ge(s["rn_ready"], b + 1)
                if b >= 2:
                    dve.wait_ge(s["att_done"], b - 1)
                nc.vector.scalar_tensor_tensor(out=wkvT[:, i, :], in0=inv_err[:, i, :], scalar=-1.0, in1=bv[:, i, :],
                                               op0=ALU.mult, op1=ALU.mult).then_inc(s["wkvT_ready"], 1)

            def x2_and_stats(b):
                dve.wait_ge(s["att_done"], b + 1)
                if b == 0:
                    dve.wait_ge(s["scattered"], 16 * TILES)
                nc.vector.tensor_tensor(x2[:, tls(b), :], bank[7][:, :].rearrange("p (t d) -> p t d", d=D),
                                        xn[:, tls(b), :], ALU.add).then_inc(s["x2_ready"], 1)
                statistics(2, x2, lambda t: dve.wait_ge(s["x2_ready"], t // CHUNK + 1), s["x2_stats"], s["x2_mv"], b)

            def h3_normalise(b):
                if b < 2:
                    dve.wait_ge(s["h_turned"], BLOCKS)
                else:
                    dve.wait_ge(s["h3_turned"], b - 1)
                normalise(2, h_tok[:, b % 2, :, :], x2, s["x2_rstd"], s["h3_ready"], b)

            def ffn_mix(b):
                def first_use():
                    if b < 2:
                        dve.wait_ge(s["buf_turned"], 3)
                    else:
                        dve.wait_ge(s["ffn_r_done"], b - 1)
                        dve.wait_ge(s["ffn_hidden_done"], HC * (b - 1))
                mix(b, s["h3T_ready"], ("ffn_mix_k", "ffn_mix_r"), s["h3_diff"], (s["mixed_fk"], s["mixed_fr"]), first_use)

            def ffn_square(b):
                for c in range(HC):
                    n = b * HC + c
                    dve.wait_ge(s["ffn_relu_ready"], n + 1)
                    nc.vector.tensor_tensor(hid[:, b % 2, c, :], hid[:, b % 2, c, :], bank[n % 4][:, :],
                                            ALU.mult).then_inc(s["ffn_hidden_ready"], 1)

            def ffn_gated(b):
                dve.wait_ge(s["ffn_out_done"], b + 1)
                dve.wait_ge(s["rf_ready"], b + 1)
                if b == 0:
                    dve.wait_ge(s["y_turned"], E)
                if b >= 2:
                    dve.wait_ge(s["ffn_turned"], b - 1)
                nc.vector.tensor_tensor(gatedT[:, b % 2, :], bank[4][:, :], rfT[:, b % 2, :], ALU.mult).then_inc(s["ffn_gated"], 1)

            def add_channel_mix(b):
                dve.wait_ge(s["ffn_turned"], b + 1)
                nc.vector.tensor_tensor(x2[:, tls(b), :], bank[6][:, :].rearrange("p (t d) -> p t d", d=D),
                                        x2[:, tls(b), :], ALU.add).then_inc(s["s_ready"], 1)

            def finish(b):
                dve.wait_ge(s["s_ready"], b + 1)
                dve.wait_ge(s["gate_ready"], b + 1)
                nc.vector.tensor_tensor(x2[:, tls(b), :], x2[:, tls(b), :], gate[:, tls(b), :],
                                        ALU.mult).then_inc(s["s_gated"], 1)
                dve.wait_ge(s["s_gated"], b + 1)
                nc.vector.tensor_tensor(x_sb[:, tls(b), :], x_sb[:, tls(b), :], x2[:, tls(b), :],
                                        ALU.add).then_inc(s["out_ready"], 1)

            dve.wait_ge(s["params_loaded"], 16)
            x_stats(0)
            x_stats(1)
            xn_and_stats(0)
            x_stats(2)
            xn_and_stats(1)
            h_normalise(0)
            x_stats(3)
            xn_and_stats(2)
            h_normalise(1)
            att_mix(0)
            xn_and_stats(3)
            h_normalise(2)
            att_mix(1)
            h_normalise(3)
            att_mix(2)
            route_choose()
            att_mix(3)
            route_slots()
            wkv_gaps(0)
            wkv_gaps(1)
            wkv_states(0)
            wkv_gaps(2)
            wkv_divide(0)
            wkv_states(1)
            wkv_gaps(3)
            wkv_divide(1)
            wkv_states(2)
            x2_and_stats(0)
            wkv_divide(2)
            wkv_states(3)
            h3_normalise(0)
            x2_and_stats(1)
            wkv_divide(3)
            h3_normalise(1)
            ffn_mix(0)
            x2_and_stats(2)
            ffn_mix(1)
            x2_and_stats(3)
            h3_normalise(2)
            h3_normalise(3)
            ffn_square(0)
            ffn_mix(2)
            for b in range(1, BLOCKS):
                ffn_square(b)
                if b + 2 < BLOCKS:
                    ffn_mix(b + 2)
                ffn_gated(b - 1)
                add_channel_mix(b - 1)
                finish(b - 1)
            ffn_gated(BLOCKS - 1)
            add_channel_mix(BLOCKS - 1)
            finish(BLOCKS - 1)


def kernel(**inputs):
    import numpy as np
    import concourse.bacc as bacc
    from concourse.bass_utils import run_bass_kernel_spmd

    a = {name: np.asarray(value) for name, value in inputs.items()}
    att, ffn = "L0_attn_", "L0_ffn_"

    def column(v):
        return v.reshape(-1, P).T

    def chunks(w):
        return w.reshape(-1, P, w.shape[1]).transpose(1, 0, 2).reshape(P, -1)

    packed = {"ln_att_g": column(a[att + "ln_att_g"]), "ln_att_b": column(a[att + "ln_att_b"]),
              "ln_ffn_g": column(a[att + "ln_ffn_g"]), "ln_ffn_b": column(a[att + "ln_ffn_b"]),
              "decay": column(a[att + "att_time_decay"]), "first": column(a[att + "att_time_first"]),
              "mix_k": column(a[att + "att_mix_k"]), "mix_v": column(a[att + "att_mix_v"]),
              "mix_r": column(a[att + "att_mix_r"]), "ffn_mix_k": column(a[att + "ffn_mix_k"]),
              "ffn_mix_r": column(a[att + "ffn_mix_r"]), "ob2": column(a[ffn + "ob2"]), "ob1": column(a[ffn + "ob1"]),
              "b1": column(a[ffn + "b1"]), "b2": column(a[ffn + "b2"]),
              "router_b": np.repeat(a[ffn + "router_b"][None], P, axis=0), "router_w": a[ffn + "router_w"]}
    mats = {"wk": a[att + "att_wk"], "wv": a[att + "att_wv"], "wr": a[att + "att_wr"], "wo": a[att + "att_wo"],
            "ffn_wr": a[att + "ffn_wr"], "ffn_wk": a[att + "ffn_wk"], "ffn_wv": chunks(a[att + "ffn_wv"]),
            "ow1": a[ffn + "ow1"], "ow2": chunks(a[ffn + "ow2"])}
    x = a[att + "x"]
    arrays = {"x_dram": np.ascontiguousarray(x.reshape(-1, x.shape[-1])),
              "params_dram": np.ascontiguousarray(np.concatenate([packed[n] for n in PARAMS], axis=1)),
              "weights_dram": np.ascontiguousarray(np.concatenate([mats[n] for n in WEIGHTS], axis=1)),
              "w1_dram": np.ascontiguousarray(a[ffn + "w1"]), "w2_dram": np.ascontiguousarray(a[ffn + "w2"])}

    nc = bacc.Bacc("TRN2", target_bir_lowering=False, num_devices=1)
    args = [nc.dram_tensor(n, v.shape, mybir.dt.from_np(v.dtype), kind="ExternalInput").ap() for n, v in arrays.items()]
    out = nc.dram_tensor("out_dram", arrays["x_dram"].shape, F32, kind="ExternalOutput").ap()
    build(nc, *args, out)
    result = run_bass_kernel_spmd(nc, [arrays], core_ids=[0])
    return result.results[0]["out_dram"].reshape(x.shape)
```

```python
from contextlib import ExitStack

import concourse.bass as bass
from concourse import mybir

ALU = mybir.AluOpType
ACT = mybir.ActivationFunctionType
F32 = mybir.dt.float32
I32 = mybir.dt.int32
AX_X = mybir.AxisListType.X

P = 128
EPS = 1e-5
CAPACITY = 160
NO_STATE = -1e38
SKIP = 4096.0

PARAMS = {"ln_att_g": 1, "ln_att_b": 1, "ln_ffn_g": 1, "ln_ffn_b": 1, "decay": 1, "first": 1, "mix_k": 1, "mix_v": 1,
          "mix_r": 1, "ffn_mix_k": 1, "ffn_mix_r": 1, "ob2": 1, "ob1": 4, "b1": 32, "b2": 8, "router_b": 8, "router_w": 8}
WEIGHTS = {"wk": 128, "wv": 128, "wr": 128, "wo": 128, "ffn_wr": 128, "ffn_wk": 512, "ffn_wv": 512, "ow1": 512, "ow2": 512}
EARLY_WEIGHTS = 3 * P

SEMAPHORES = """
x_loaded0 x_loaded1 x_loaded2 x_loaded3 params_loaded early_weights_loaded weights_loaded
w1_loaded0 w1_loaded1 w1_loaded2 w2_loaded0 w2_loaded1 w2_loaded2
ident_cleared ident_ready tri_ready ones_ready pow_ready expert_code_ready run_mask_set run_mask_ready zeros_ready
column_zeroed state_zeroed decay_exp w_ready buf_zeroed
x_stats x_mv x_neg_mean x_var_eps h_var_eps x_rstd h_bias_ready xn_ready h_ready
xn_turned h_turned xnT_ready hT_ready hT_diff mixed_k mixed_v mixed_r k_done v_done r_done k_ready v_ready r_ready
logits_done logits_biased logit_max is_max max_code code_max onehot_ready counts_done counts_run rank_a rank_b rank_hot
rank_ready expert_base slot_a slot_over slot_b slot_ready scattered buf_loaded buf_turned bufT_ready
o_ready gap_t gap_s gap_max gap_min exp_neg exp_pos bv2_ready bv_ready p_ready q_ready ap_ready aq_ready num_ready den_ready
den_ln den_inv rn_ready newton_a newton_b wkvT_ready
att_done x2_ready x2_stats x2_mv x2_var_eps x2_rstd h3_ready h3_turned h3T_ready h3_diff mixed_fk mixed_fr
over_hidden_done over_hidden_ready over_out_done over_outT_ready over_turned over_ready
hidden_done hidden_ready y_done yT_ready y_turned y_rows_ready y_stored0 y_stored1
gathered0 gathered1 gathered2 gathered3
ffn_hidden_done ffn_relu_ready ffn_hidden_ready ffn_square_ready ffn_r_done rf_ready ffn_out_done ffn_gated ffn_turned s_ready
gate_sigmoid gate_ready s_gated out_ready out_stored
""".split()


def columns(table):
    at, out = 0, {}
    for name, n in table.items():
        out[name] = (at, at + n)
        at += n
    return out


def build(nc, x, params, weights, w1, w2, out):
    n_tokens = x.shape[0]
    TILES = n_tokens // P
    CHUNK = 4
    BLOCKS = TILES // CHUNK
    NB = CHUNK * P
    SEQ = n_tokens // 2
    E, D, H = w1.shape
    HC = H // P
    SLOTS = E * CAPACITY
    SLOT_TILES = SLOTS // P
    HALF = CAPACITY // 2
    RING = 3
    pcol, wcol = columns(PARAMS), columns(WEIGHTS)

    x_tiles = x.rearrange("(t p) d -> p t d", p=P)
    out_tiles = out.rearrange("(t p) d -> p t d", p=P)
    slot_rows = nc.dram_tensor("slot_rows", (SLOTS, D), F32, kind="Internal").ap()
    y_rows = nc.dram_tensor("y_rows", (SLOTS, D), F32, kind="Internal").ap()

    with ExitStack() as ctx:
        def sb(name, shape, dt=F32):
            return ctx.enter_context(nc.sbuf_tensor(name, shape, dt))

        s = {n: ctx.enter_context(nc.semaphore(n)) for n in SEMAPHORES}
        x_loaded = [s["x_loaded0"], s["x_loaded1"], s["x_loaded2"], s["x_loaded3"]]
        y_stored = [s["y_stored0"], s["y_stored1"]]
        gathered = [s["gathered0"], s["gathered1"], s["gathered2"], s["gathered3"]]
        w1_loaded = [s["w1_loaded0"], s["w1_loaded1"], s["w1_loaded2"]]
        w2_loaded = [s["w2_loaded0"], s["w2_loaded1"], s["w2_loaded2"]]
        bank = [ctx.enter_context(nc.psum_tensor(f"bank{i}", [P, 512], F32)) for i in range(8)]

        par = sb("par", [P, sum(PARAMS.values())])
        wts = sb("wts", [P, sum(WEIGHTS.values())])
        w1_sb = sb("w1_sb", [P, RING, H])
        w2_sb = sb("w2_sb", [P, RING, HC, D])
        ident = sb("ident", [P, P])
        tri = sb("tri", [P, P])
        ones = sb("ones", [P, P])
        zeros = sb("zeros", [P, D])
        minus_half = sb("minus_half", [P, 2, CHUNK])
        expert_code = sb("expert_code", [P, E, TILES])
        run_mask = sb("run_mask", [P, E, TILES])
        w_neg = sb("w_neg", [P, 1])
        w_exp = sb("w_exp", [P, 1])

        x_sb = sb("x_sb", [P, TILES, D])
        xn = sb("xn", [P, TILES, D])
        h_tok = sb("h_tok", [P, 2, CHUNK, D])
        stats = sb("stats", [P, 3, TILES, 6])
        mv = sb("mv", [P, 3, TILES, 2])
        neg_mean = sb("neg_mean", [P, TILES])
        h_bias = sb("h_bias", [P, TILES])
        var_eps = sb("var_eps", [P, 3, TILES])
        rstd = sb("rstd", [P, 3, TILES])
        xnT = sb("xnT", [P, n_tokens])
        hT = sb("hT", [P, 2, SEQ + 1])
        diff = sb("diff", [P, 2, NB])
        mixed = sb("mixed", [P, 2, 3, NB])
        kT = sb("kT", [P, n_tokens])
        vT = sb("vT", [P, n_tokens])
        rT = sb("rT", [P, n_tokens])

        logits = sb("logits", [P, E, TILES])
        row_max = sb("row_max", [P, TILES])
        is_max = sb("is_max", [P, E, TILES])
        code = sb("code", [P, E, TILES])
        code_max = sb("code_max", [P, TILES])
        onehot = sb("onehot", [P, E, TILES])
        counts = sb("counts", [P, E, TILES])
        rank_e = sb("rank_e", [P, E, TILES])
        rank = sb("rank", [P, TILES])
        base = sb("base", [P, TILES])
        over = sb("over", [P, TILES])
        slot_f = sb("slot_f", [P, TILES])
        slot = sb("slot", [P, TILES], I32)

        o_state = sb("o_state", [P, 2, SEQ + 1])
        p_state = sb("p_state", [P, 2, SEQ + 1])
        q_state = sb("q_state", [P, 2, SEQ + 1])
        gap = sb("gap", [P, 2, 2, NB])
        e_neg = sb("e_neg", [P, 2, 2, NB])
        e_pos = gap
        bv = sb("bv", [P, 2, NB])
        bv2 = sb("bv2", [P, 2, NB])
        num = sb("num", [P, 2, NB])
        den = bv2
        inv = sb("inv", [P, 2, NB])
        den_log = inv
        inv_err = den
        wkvT = sb("wkvT", [P, 2, NB])

        x2 = xn
        rfT = rT[:, 0:2 * NB].rearrange("p (i n) -> p i n", i=2)
        hid = sb("hid", [P, 2, HC, NB])
        e_hid = sb("e_hid", [P, 2, HC, CAPACITY])
        over_outT = sb("over_outT", [P, 2, NB])
        yT = over_outT[:, :, 0:CAPACITY]
        gatedT = sb("gatedT", [P, 2, NB])
        moe = sb("moe", [P, TILES, D])
        buf_rows = mixed[:, :, :, :].rearrange("p i n c -> p (i n c)")[:, 0:SLOT_TILES * D].rearrange(
            "p (t d) -> p t d", d=D)
        bufT = xnT
        y_sb = sb("y_sb", [HALF, 2, 2, D])
        gate = kT[:, :].rearrange("p (t d) -> p t d", d=D)

        def param(name, i=0):
            at = pcol[name][0] + i
            return par[:, at:at + 1]

        def weight(name, c=0):
            at = wcol[name][0] + c * P
            return wts[:, at:at + P]

        def seq_cols(b, shift):
            at = (b % 2) * NB + shift
            return b // 2, slice(at, at + NB)

        def blk(b):
            return slice(b * NB, (b + 1) * NB)

        def tls(b):
            return slice(b * CHUNK, (b + 1) * CHUNK)

        block = ctx.enter_context(nc.Block())

        @block.sync
        def _(sp):
            for b in range(BLOCKS):
                sp.dma_start(x_sb[:, tls(b), :], x_tiles[:, tls(b), :]).then_inc(x_loaded[b], 16)

            def load_expert(e):
                sp.dma_start(w1_sb[:, e % RING, :], w1[e]).then_inc(w1_loaded[e % RING], 16)
                sp.dma_start(w2_sb[:, e % RING, :, :], w2[e].rearrange("(c p) d -> p c d", p=P)).then_inc(
                    w2_loaded[e % RING], 16)

            sp.wait_ge(s["zeros_ready"], 1)
            sp.dma_start(slot_rows.rearrange("(p r) d -> p r d", p=P),
                         zeros[:, :].unsqueeze(1).to_broadcast([P, SLOT_TILES, D])).then_inc(s["buf_zeroed"], 16)
            for e in range(RING):
                load_expert(e)
            sp.wait_ge(s["r_done"], BLOCKS - 1)
            sp.wait_ge(s["scattered"], 16 * TILES)
            sp.dma_start(buf_rows[:, :, :], slot_rows.rearrange("(t p) d -> p t d", p=P)).then_inc(s["buf_loaded"], 16)
            for e in range(E):
                if e + RING < E:
                    sp.wait_ge(s["y_done"], e + 1)
                    load_expert(e + RING)
                sp.wait_ge(s["y_rows_ready"], e + 1)
                sp.dma_start(y_rows.rearrange("(e a p) d -> p e a d", e=E, a=2)[:, e], y_sb[:, e % 2, :, :]).then_inc(
                    y_stored[e % 2], 16)
            for b in range(BLOCKS):
                sp.wait_ge(s["out_ready"], b + 1)
                sp.dma_start(out_tiles[:, tls(b), :], x_sb[:, tls(b), :]).then_inc(s["out_stored"], 16)
            sp.wait_ge(s["out_stored"], 16 * BLOCKS)

        @block.gpsimd
        def _(pool):
            nc.gpsimd.memset(ident[:], 0.0).then_inc(s["ident_cleared"], 1)
            nc.gpsimd.memset(minus_half[:], -0.5).then_inc(s["pow_ready"], 1)
            nc.gpsimd.memset(ones[:], 1.0).then_inc(s["ones_ready"], 1)
            pool.wait_ge(s["ident_cleared"], 1)
            nc.gpsimd.affine_select(out=ident[:], in_=ident[:], compare_op=ALU.not_equal, fill=1.0, base=0,
                                    pattern=[[-1, P]], channel_multiplier=1).then_inc(s["ident_ready"], 1)
            nc.gpsimd.memset(zeros[:], 0.0).then_inc(s["zeros_ready"], 1)
            nc.gpsimd.memset(hT[:, :, 0:1], 0.0).then_inc(s["column_zeroed"], 1)
            pool.wait_ge(s["ones_ready"], 1)
            nc.gpsimd.affine_select(out=tri[:], in_=ones[:], compare_op=ALU.is_ge, fill=0.0, base=0,
                                    pattern=[[1, P]], channel_multiplier=-1).then_inc(s["tri_ready"], 1)
            nc.gpsimd.iota(expert_code[:, :, :], [[-1, E], [0, TILES]], base=E, channel_multiplier=0,
                           allow_small_or_imprecise_dtypes=True).then_inc(s["expert_code_ready"], 1)
            nc.gpsimd.memset(run_mask[:], 1.0).then_inc(s["run_mask_set"], 1)
            pool.wait_ge(s["run_mask_set"], 1)
            nc.gpsimd.memset(run_mask[:, :, 0:1], 0.0).then_inc(s["run_mask_ready"], 1)
            nc.gpsimd.memset(o_state[:, :, 0:1], NO_STATE).then_inc(s["state_zeroed"], 1)
            nc.gpsimd.memset(p_state[:, :, 0:1], 0.0).then_inc(s["state_zeroed"], 1)
            nc.gpsimd.memset(q_state[:, :, 0:1], 0.0).then_inc(s["state_zeroed"], 1)
            pool.wait_ge(s["pow_ready"], 1)

            def input_roots(b):
                pool.wait_ge(s["x_mv"], CHUNK * (b + 1))
                var = mv[:, 0, tls(b), 1]
                nc.gpsimd.tensor_scalar(var_eps[:, 0, tls(b)], var, EPS, 1.0, ALU.add, ALU.mult).then_inc(s["x_var_eps"], 1)
                nc.gpsimd.tensor_scalar(var_eps[:, 1, tls(b)], var, 1.0 + EPS, EPS * EPS, ALU.mult,
                                        ALU.add).then_inc(s["h_var_eps"], 1)
                nc.gpsimd.tensor_scalar(neg_mean[:, tls(b)], mv[:, 0, tls(b), 0], -1.0, 0.0, ALU.mult,
                                        ALU.add).then_inc(s["x_neg_mean"], 1)
                pool.wait_ge(s["x_var_eps"], b + 1)
                pool.wait_ge(s["h_var_eps"], b + 1)
                nc.gpsimd.tensor_tensor(rstd[:, 0:2, tls(b)], var_eps[:, 0:2, tls(b)], minus_half[:, :, :],
                                        ALU.pow).then_inc(s["x_rstd"], 1)
                pool.wait_ge(s["x_rstd"], b + 1)
                pool.wait_ge(s["x_neg_mean"], b + 1)
                nc.gpsimd.tensor_tensor(h_bias[:, tls(b)], neg_mean[:, tls(b)], rstd[:, 1, tls(b)],
                                        ALU.mult).then_inc(s["h_bias_ready"], 1)

            def x2_root(b):
                pool.wait_ge(s["x2_mv"], CHUNK * (b + 1))
                nc.gpsimd.tensor_scalar(var_eps[:, 2, tls(b)], mv[:, 2, tls(b), 1], EPS, 1.0, ALU.add,
                                        ALU.mult).then_inc(s["x2_var_eps"], 1)
                pool.wait_ge(s["x2_var_eps"], b + 1)
                nc.gpsimd.tensor_tensor(rstd[:, 2, tls(b)], var_eps[:, 2, tls(b)], minus_half[:, 0, :],
                                        ALU.pow).then_inc(s["x2_rstd"], 1)

            def less_before(b, ready, mixed_last, done):
                pool.wait_ge(ready, b + 1)
                if b >= 2:
                    pool.wait_ge(mixed_last, b - 1)
                else:
                    pool.wait_ge(s["column_zeroed"], 1)
                q, here = seq_cols(b, 1)
                _, before = seq_cols(b, 0)
                nc.gpsimd.tensor_tensor(diff[:, b % 2, :], hT[:, q, here], hT[:, q, before],
                                        ALU.subtract).then_inc(done, 1)

            def shift_diff(b):
                less_before(b, s["hT_ready"], s["mixed_r"], s["hT_diff"])

            def h3_diff(b):
                less_before(b, s["h3T_ready"], s["mixed_fr"], s["h3_diff"])

            def scatter(t):
                if t == 0:
                    pool.wait_ge(s["slot_ready"], 1)
                    pool.wait_ge(s["xn_ready"], TILES)
                    pool.wait_ge(s["buf_zeroed"], 16)
                nc.gpsimd.indirect_dma_start(slot_rows, bass.IndirectOffsetOnAxis(ap=slot[:, t:t + 1], axis=0),
                                             xn[:, t, :], None, bounds_check=SLOTS - 1,
                                             oob_is_err=False).then_inc(s["scattered"], 16)

            def wkv_products(b):
                i = b % 2
                if b >= 2:
                    pool.wait_ge(s["wkvT_ready"], b - 1)
                pool.wait_ge(s["v_ready"], b + 1)
                pool.wait_ge(s["exp_neg"], b + 1)
                nc.gpsimd.tensor_tensor(bv2[:, i, :], e_neg[:, i, 1, :], vT[:, blk(b)], ALU.mult).then_inc(s["bv2_ready"], 1)
                pool.wait_ge(s["exp_pos"], b + 1)
                nc.gpsimd.tensor_tensor(bv[:, i, :], e_pos[:, i, 0, :], vT[:, blk(b)], ALU.mult).then_inc(s["bv_ready"], 1)

            def wkv_times_r(b):
                i = b % 2
                pool.wait_ge(s["num_ready"], b + 1)
                pool.wait_ge(s["r_ready"], b + 1)
                nc.gpsimd.tensor_tensor(bv[:, i, :], num[:, i, :], rT[:, blk(b)], ALU.mult).then_inc(s["rn_ready"], 1)

            def gather(t):
                if t == 0:
                    pool.wait_ge(s["over_ready"], BLOCKS)
                    for stored in y_stored:
                        pool.wait_ge(stored, 16 * E // 2)
                nc.gpsimd.indirect_dma_start(moe[:, t, :], None, y_rows,
                                             bass.IndirectOffsetOnAxis(ap=slot[:, t:t + 1], axis=0),
                                             bounds_check=SLOTS - 1, oob_is_err=False).then_inc(gathered[t // CHUNK], 16)

            def gate_times(b):
                pool.wait_ge(s["gate_sigmoid"], b + 1)
                nc.gpsimd.tensor_tensor(gate[:, tls(b), :], gate[:, tls(b), :], moe[:, tls(b), :],
                                        ALU.mult).then_inc(s["gate_ready"], 1)

            for b in range(4):
                input_roots(b)
            for b in range(4):
                shift_diff(b)
            for t in range(16):
                scatter(t)
            wkv_products(0)
            wkv_products(1)
            wkv_times_r(0)
            wkv_times_r(1)
            wkv_products(2)
            x2_root(0)
            wkv_products(3)
            wkv_times_r(2)
            h3_diff(0)
            wkv_times_r(3)
            x2_root(1)
            x2_root(2)
            h3_diff(1)
            x2_root(3)
            h3_diff(2)
            h3_diff(3)
            for t in range(7):
                gather(t)
            gate_times(0)
            for t in range(7, 11):
                gather(t)
            gate_times(1)
            for t in range(11, 15):
                gather(t)
            gate_times(2)
            gather(15)
            gate_times(3)

        @block.tensor
        def _(pe):
            def turn_xn(b):
                if b == 0:
                    pe.wait_ge(s["ident_ready"], 1)
                if b >= 2:
                    pe.wait_ge(s["xnT_ready"], b - 1)
                pe.wait_ge(s["xn_ready"], CHUNK * (b + 1))
                for t in range(CHUNK):
                    last = nc.tensor.transpose(bank[b % 2][:, t * P:(t + 1) * P], xn[:, b * CHUNK + t, :], ident[:])
                last.then_inc(s["xn_turned"], 1)

            def turn_h(b):
                if b >= 2:
                    pe.wait_ge(s["hT_ready"], b - 1)
                pe.wait_ge(s["h_ready"], CHUNK * (b + 1))
                for t in range(CHUNK):
                    last = nc.tensor.transpose(bank[2 + 4 * (b % 2)][:, t * P:(t + 1) * P], h_tok[:, b % 2, t, :], ident[:])
                last.then_inc(s["h_turned"], 1)

            def project(b, n):
                name, ready, used, done = (
                    ("wk", s["mixed_k"], s["k_ready"], s["k_done"]), ("wv", s["mixed_v"], s["v_ready"], s["v_done"]),
                    ("wr", s["mixed_r"], s["r_ready"], s["r_done"]))[n]
                if b == 0 and n == 0:
                    pe.wait_ge(s["early_weights_loaded"], 16)
                pe.wait_ge(ready, b + 1)
                if b:
                    pe.wait_ge(used, b)
                nc.tensor.matmul(bank[3 + n][:, :], weight(name), mixed[:, b % 2, n, :], start=True,
                                 stop=True).then_inc(done, 1)

            def route_logits(b):
                if b == 0:
                    pe.wait_ge(s["params_loaded"], 16)
                pe.wait_ge(s["xnT_ready"], b + 1)
                at = pcol["router_w"][0]
                for t in range(b * CHUNK, (b + 1) * CHUNK):
                    last = nc.tensor.matmul(bank[7][:, 0:E * TILES].rearrange("p (e t) -> p e t", e=E)[:, :, t],
                                            xnT[:, t * P:(t + 1) * P], par[:, at:at + E], start=True, stop=True)
                last.then_inc(s["logits_done"], 1)

            def count_tokens():
                pe.wait_ge(s["onehot_ready"], 1)
                pe.wait_ge(s["tri_ready"], 1)
                flat = onehot[:, :, :].rearrange("p e t -> p (e t)")
                nc.tensor.matmul(bank[7][:, 128:256], tri[:], flat, start=True, stop=True)
                nc.tensor.matmul(bank[7][:, 256:384], ones[:], flat, start=True, stop=True).then_inc(s["counts_done"], 1)


            def overflow_hidden(b, c):
                n = b * HC + c
                if n == 0:
                    pe.wait_ge(s["weights_loaded"], 16)
                if n < 3:
                    pe.wait_ge(*((s["xnT_ready"], BLOCKS - 1), (s["xnT_ready"], BLOCKS), (s["hT_ready"], BLOCKS - 1))[n])
                else:
                    pe.wait_ge(s["over_hidden_ready"], n - 2)
                pe.wait_ge(s["xnT_ready"], b + 1)
                nc.tensor.matmul(bank[n % 3][:, :], weight("ow1", c), xnT[:, blk(b)], start=True,
                                 stop=True).then_inc(s["over_hidden_done"], 1)


            def overflow_out(b, *free):
                pe.wait_ge(*free)
                for c in range(HC):
                    pe.wait_ge(s["over_hidden_ready"], b * HC + c + 1)
                    last = nc.tensor.matmul(bank[6][:, :], weight("ow2", c), hid[:, b % 2, c, :], start=(c == 0),
                                            stop=(c == HC - 1))
                last.then_inc(s["over_out_done"], 1)

            def overflow_turn(b, *free):
                pe.wait_ge(*free)
                pe.wait_ge(s["over_outT_ready"], b + 1)
                for t in range(CHUNK):
                    last = nc.tensor.transpose(bank[6][:, t * P:(t + 1) * P], over_outT[:, b % 2, t * P:(t + 1) * P],
                                               ident[:])
                last.then_inc(s["over_turned"], 1)

            def turn_slots(g, *free):
                pe.wait_ge(*free)
                pe.wait_ge(s["buf_loaded"], 16)
                for n, t in enumerate(range(4 * g, min(4 * g + 4, SLOT_TILES))):
                    last = nc.tensor.transpose(bank[6][:, n * P:(n + 1) * P], buf_rows[:, t, :], ident[:])
                last.then_inc(s["buf_turned"], 1)

            def expert_hidden(e, c):
                m = BLOCKS * HC + e * HC + c
                if c == 0:
                    pe.wait_ge(w1_loaded[e % RING], 16 * (e // RING + 1))
                    pe.wait_ge(s["bufT_ready"], min(3, -(-(e + 1) * CAPACITY // NB)))
                if e == 0 and c < 3:
                    pe.wait_ge(s["over_hidden_ready"], m - 2)
                else:
                    pe.wait_ge(s["hidden_ready"], e * HC + c - 2)
                nc.tensor.matmul(bank[m % 3][:, 0:CAPACITY], w1_sb[:, e % RING, c * P:(c + 1) * P],
                                 bufT[:, e * CAPACITY:(e + 1) * CAPACITY], start=True, stop=True).then_inc(s["hidden_done"], 1)

            def expert_out(e, *free):
                pe.wait_ge(*free)
                pe.wait_ge(w2_loaded[e % RING], 16 * (e // RING + 1))
                for c in range(HC):
                    pe.wait_ge(s["hidden_ready"], e * HC + c + 1)
                    last = nc.tensor.matmul(bank[6][:, 0:CAPACITY], w2_sb[:, e % RING, c, :], e_hid[:, e % 2, c, :],
                                            start=(c == 0), stop=(c == HC - 1))
                last.then_inc(s["y_done"], 1)

            def expert_turn(e, *free):
                pe.wait_ge(*free)
                pe.wait_ge(s["yT_ready"], e + 1)
                for a in range(2):
                    last = nc.tensor.transpose(bank[6][0:HALF, a * P:(a + 1) * P], yT[:, e % 2, a * HALF:(a + 1) * HALF],
                                               ident[:])
                last.then_inc(s["y_turned"], 1)

            def attention_out(b, *free):
                pe.wait_ge(*free)
                pe.wait_ge(s["wkvT_ready"], b + 1)
                for t in range(CHUNK):
                    last = nc.tensor.matmul(bank[7][:, t * P:(t + 1) * P], wkvT[:, b % 2, t * P:(t + 1) * P],
                                            weight("wo"), start=True, stop=True)
                last.then_inc(s["att_done"], 1)

            def turn_h3(b, *free):
                pe.wait_ge(*free)
                pe.wait_ge(s["h3_ready"], CHUNK * (b + 1))
                for t in range(CHUNK):
                    last = nc.tensor.transpose(bank[5][:, t * P:(t + 1) * P], h_tok[:, b % 2, t, :], ident[:])
                last.then_inc(s["h3_turned"], 1)

            def ffn_hidden(b, c):
                n = b * HC + c
                pe.wait_ge(s["mixed_fk"], b + 1)
                if n < 2:
                    pe.wait_ge((s["k_ready"], s["v_ready"])[n], BLOCKS)
                else:
                    pe.wait_ge(s["ffn_relu_ready"], n - 1)
                nc.tensor.matmul(bank[3 + n % 2][:, :], weight("ffn_wk", c), mixed[:, b % 2, 0, :], start=True,
                                 stop=True).then_inc(s["ffn_hidden_done"], 1)

            def ffn_gate(b, *free):
                pe.wait_ge(*free)
                pe.wait_ge(s["mixed_fr"], b + 1)
                nc.tensor.matmul(bank[5][:, :], weight("ffn_wr"), mixed[:, b % 2, 1, :], start=True,
                                 stop=True).then_inc(s["ffn_r_done"], 1)

            def ffn_out(b, *free):
                pe.wait_ge(*free)
                for c in range(HC):
                    pe.wait_ge(s["ffn_hidden_ready"] if c % 2 == 0 else s["ffn_square_ready"], b * HC // 2 + c // 2 + 1)
                    last = nc.tensor.matmul(bank[7][:, :], weight("ffn_wv", c), hid[:, b % 2, c, :], start=(c == 0),
                                            stop=(c == HC - 1))
                last.then_inc(s["ffn_out_done"], 1)

            def ffn_turn(b):
                pe.wait_ge(s["ffn_gated"], b + 1)
                for t in range(CHUNK):
                    last = nc.tensor.transpose(bank[7][:, t * P:(t + 1) * P], gatedT[:, b % 2, t * P:(t + 1) * P],
                                               ident[:])
                last.then_inc(s["ffn_turned"], 1)

            turn_xn(0)
            turn_h(0)
            turn_h(1)
            turn_xn(1)
            route_logits(0)
            turn_xn(2)
            route_logits(1)
            turn_h(2)
            turn_xn(3)
            route_logits(2)
            overflow_hidden(0, 0)
            turn_h(3)
            route_logits(3)
            project(0, 0)
            overflow_hidden(0, 1)
            project(0, 1)
            overflow_hidden(0, 2)
            count_tokens()
            project(0, 2)
            overflow_hidden(0, 3)
            project(1, 0)
            overflow_hidden(1, 0)
            project(1, 1)
            overflow_out(0, s["hT_ready"], BLOCKS)
            project(1, 2)
            overflow_hidden(1, 1)
            project(2, 0)
            overflow_hidden(1, 2)
            project(2, 1)
            overflow_hidden(1, 3)
            project(2, 2)
            overflow_hidden(2, 0)
            project(3, 0)
            overflow_out(1, s["over_outT_ready"], 1)
            project(3, 1)
            overflow_hidden(2, 1)
            project(3, 2)
            overflow_hidden(2, 2)
            overflow_turn(0, s["over_outT_ready"], 2)
            overflow_hidden(2, 3)
            overflow_hidden(3, 0)
            overflow_hidden(3, 1)
            overflow_out(2, s["over_ready"], 1)
            overflow_hidden(3, 2)
            overflow_hidden(3, 3)
            turn_slots(0, s["over_outT_ready"], 3)
            turn_slots(1, s["bufT_ready"], 1)
            for c in range(3):
                expert_hidden(0, c)
            turn_slots(2, s["bufT_ready"], 2)
            expert_hidden(0, 3)
            overflow_turn(1, s["bufT_ready"], 3)
            for c in range(3):
                expert_hidden(1, c)
            overflow_out(3, s["over_ready"], 2)
            attention_out(0, s["rank_b"], 1)
            expert_hidden(1, 3)
            overflow_turn(2, s["over_outT_ready"], 4)
            for c in range(3):
                expert_hidden(2, c)
            overflow_turn(3, s["over_ready"], 3)
            expert_out(0, s["over_ready"], 4)
            expert_turn(0, s["yT_ready"], 1)
            expert_hidden(2, 3)
            expert_out(1, s["y_rows_ready"], 1)
            attention_out(1, s["x2_ready"], 1)
            expert_hidden(3, 0)
            expert_hidden(3, 1)
            expert_out(2, s["yT_ready"], 2)
            expert_hidden(3, 2)
            expert_hidden(3, 3)
            expert_turn(1, s["yT_ready"], 3)
            for c in range(3):
                expert_hidden(4, c)
            turn_h3(0, s["r_ready"], BLOCKS)
            expert_out(3, s["y_rows_ready"], 2)
            expert_hidden(4, 3)
            expert_hidden(5, 0)
            expert_hidden(5, 1)
            expert_turn(2, s["yT_ready"], 4)
            expert_hidden(5, 2)
            expert_hidden(5, 3)
            expert_out(4, s["y_rows_ready"], 3)
            expert_turn(3, s["yT_ready"], 5)
            for c in range(3):
                expert_hidden(6, c)
            expert_out(5, s["y_rows_ready"], 4)
            attention_out(2, s["x2_ready"], 2)
            expert_hidden(6, 3)
            expert_turn(4, s["yT_ready"], 6)
            for c in range(3):
                expert_hidden(7, c)
            turn_h3(1, s["h3T_ready"], 1)
            expert_out(6, s["y_rows_ready"], 5)
            expert_hidden(7, 3)
            attention_out(3, s["x2_ready"], 3)
            expert_turn(5, s["yT_ready"], 7)
            ffn_hidden(0, 0)
            expert_out(7, s["y_rows_ready"], 6)
            ffn_hidden(0, 1)
            ffn_gate(0, s["h3T_ready"], 2)
            ffn_hidden(0, 2)
            expert_turn(6, s["yT_ready"], 8)
            ffn_hidden(0, 3)
            turn_h3(2, s["rf_ready"], 1)
            ffn_hidden(1, 0)
            expert_turn(7, s["y_rows_ready"], 7)
            ffn_hidden(1, 1)
            turn_h3(3, s["h3T_ready"], 3)
            ffn_out(0, s["x2_ready"], 4)
            ffn_hidden(1, 2)
            ffn_gate(1, s["h3T_ready"], 4)
            ffn_hidden(1, 3)
            ffn_turn(0)
            ffn_hidden(2, 0)
            ffn_gate(2, s["rf_ready"], 2)
            ffn_hidden(2, 1)
            ffn_out(1, s["s_ready"], 1)
            ffn_hidden(2, 2)
            ffn_hidden(2, 3)
            ffn_turn(1)
            ffn_hidden(3, 0)
            ffn_gate(3, s["rf_ready"], 3)
            ffn_hidden(3, 1)
            ffn_out(2, s["s_ready"], 2)
            ffn_hidden(3, 2)
            ffn_hidden(3, 3)
            ffn_turn(2)
            ffn_out(3, s["s_ready"], 3)
            ffn_turn(3)

        @block.scalar
        def _(act):
            act.dma_start(par[:, :], params).then_inc(s["params_loaded"], 16)
            act.dma_start(wts[:, 0:EARLY_WEIGHTS], weights[:, 0:EARLY_WEIGHTS]).then_inc(s["early_weights_loaded"], 16)
            act.dma_start(wts[:, EARLY_WEIGHTS:], weights[:, EARLY_WEIGHTS:]).then_inc(s["weights_loaded"], 16)
            nc.scalar.preload_act_table_set("natural_log_exp_and_others")
            act.wait_ge(s["params_loaded"], 16)
            nc.scalar.activation(w_exp[:], param("decay"), ACT.Exp).then_inc(s["decay_exp"], 1)
            nc.scalar.preload_act_table_set("sigmoid_and_others")

            def copy_xn(b):
                act.wait_ge(s["xn_turned"], b + 1)
                nc.scalar.copy(xnT[:, blk(b)], bank[b % 2][:, :]).then_inc(s["xnT_ready"], 1)

            def h_normalise(b):
                act.wait_ge(s["x_rstd"], b + 1)
                act.wait_ge(s["h_bias_ready"], b + 1)
                if b >= 2:
                    act.wait_ge(s["h_turned"], b - 1)
                for t in range(CHUNK):
                    n = b * CHUNK + t
                    nc.scalar.activation(h_tok[:, b % 2, t, :], x_sb[:, n, :], ACT.Identity,
                                         bias=h_bias[:, n:n + 1], scale=rstd[:, 1, n:n + 1]).then_inc(s["h_ready"], 1)

            def copy_h(b):
                act.wait_ge(s["h_turned"], b + 1)
                q, cols = seq_cols(b, 1)
                nc.scalar.activation(hT[:, q, cols], bank[2 + 4 * (b % 2)][:, :], ACT.Identity, bias=param("ln_att_b"),
                                     scale=param("ln_att_g")).then_inc(s["hT_ready"], 1)

            def copy_projected(b, n):
                act.wait_ge((s["k_done"], s["v_done"], s["r_done"])[n], b + 1)
                if n < 2:
                    nc.scalar.copy((kT, vT)[n][:, blk(b)], bank[3 + n][:, :]).then_inc((s["k_ready"], s["v_ready"])[n], 1)
                else:
                    nc.scalar.activation(rT[:, blk(b)], bank[5][:, :], ACT.Sigmoid).then_inc(s["r_ready"], 1)

            def wkv_exponentials(b):
                i = b % 2
                act.wait_ge(s["gap_max"], b + 1)
                nc.scalar.activation(e_neg[:, i, :, :], e_neg[:, i, :, :], ACT.Exp, scale=-1.0).then_inc(s["exp_neg"], 1)
                act.wait_ge(s["gap_min"], b + 1)
                nc.scalar.activation(e_pos[:, i, :, :], e_pos[:, i, :, :], ACT.Exp).then_inc(s["exp_pos"], 1)

            def wkv_reciprocal(b):
                i = b % 2
                act.wait_ge(s["den_ready"], b + 1)
                if b >= 2:
                    act.wait_ge(s["wkvT_ready"], b - 1)
                nc.scalar.activation(den_log[:, i, :], den[:, i, :], ACT.Ln).then_inc(s["den_ln"], 1)
                act.wait_ge(s["den_ln"], b + 1)
                nc.scalar.activation(inv[:, i, :], den_log[:, i, :], ACT.Exp, scale=-1.0).then_inc(s["den_inv"], 1)

            def overflow_relu(b, c):
                n = b * HC + c
                if b >= 2:
                    act.wait_ge(s["over_out_done"], b - 1)
                act.wait_ge(s["over_hidden_done"], n + 1)
                nc.scalar.activation(hid[:, b % 2, c, :], bank[n % 3][:, :], ACT.Relu,
                                     bias=param("ob1", c)).then_inc(s["over_hidden_ready"], 1)

            def overflow_bias(b):
                act.wait_ge(s["over_out_done"], b + 1)
                if b >= 2:
                    act.wait_ge(s["over_turned"], b - 1)
                nc.scalar.activation(over_outT[:, b % 2, :], bank[6][:, :], ACT.Identity,
                                     bias=param("ob2")).then_inc(s["over_outT_ready"], 1)

            def overflow_tokens(b):
                act.wait_ge(s["over_turned"], b + 1)
                nc.scalar.copy(moe[:, tls(b), :], bank[6][:, :].rearrange("p (t d) -> p t d", d=D)).then_inc(
                    s["over_ready"], 1)

            def copy_slots(g):
                act.wait_ge(s["buf_turned"], g + 1)
                if g == 0:
                    act.wait_ge(s["over_hidden_done"], BLOCKS * HC)
                    act.wait_ge(s["logits_done"], BLOCKS)
                n = min(NB, SLOTS - g * NB)
                nc.scalar.copy(bufT[:, g * NB:g * NB + n], bank[6][:, 0:n]).then_inc(s["bufT_ready"], 1)

            def expert_relu(e, c):
                n = e * HC + c
                if e >= 2:
                    act.wait_ge(s["y_done"], e - 1)
                act.wait_ge(s["hidden_done"], n + 1)
                nc.scalar.activation(e_hid[:, e % 2, c, :], bank[(BLOCKS * HC + n) % 3][:, 0:CAPACITY], ACT.Relu,
                                     bias=param("b1", n)).then_inc(s["hidden_ready"], 1)

            def expert_bias(e):
                act.wait_ge(s["y_done"], e + 1)
                if e == 0:
                    act.wait_ge(s["over_turned"], BLOCKS)
                if e >= 2:
                    act.wait_ge(s["y_turned"], e - 1)
                nc.scalar.activation(yT[:, e % 2, :], bank[6][:, 0:CAPACITY], ACT.Identity,
                                     bias=param("b2", e)).then_inc(s["yT_ready"], 1)

            def expert_rows(e):
                act.wait_ge(s["y_turned"], e + 1)
                if e >= 2:
                    act.wait_ge(y_stored[e % 2], 16 * (e // 2))
                nc.scalar.copy(y_sb[:, e % 2, :, :], bank[6][0:HALF, 0:2 * P].rearrange("p (a d) -> p a d", a=2)).then_inc(
                    s["y_rows_ready"], 1)

            def copy_h3(b):
                act.wait_ge(s["h3_turned"], b + 1)
                if b == 0:
                    act.wait_ge(s["mixed_r"], BLOCKS)
                q, cols = seq_cols(b, 1)
                nc.scalar.activation(hT[:, q, cols], bank[5][:, :], ACT.Identity, bias=param("ln_ffn_b"),
                                     scale=param("ln_ffn_g")).then_inc(s["h3T_ready"], 1)

            def ffn_relu(b, c):
                n = b * HC + c
                act.wait_ge(s["ffn_hidden_done"], n + 1)
                if b < 2:
                    act.wait_ge(s["over_out_done"], BLOCKS - 1 + b)
                else:
                    act.wait_ge(s["ffn_out_done"], b - 1)
                nc.scalar.activation(hid[:, b % 2, c, :], bank[3 + n % 2][:, :], ACT.Relu).then_inc(s["ffn_relu_ready"], 1)

            def ffn_square_act(b, c):
                act.wait_ge(s["ffn_relu_ready"], b * HC + c + 1)
                nc.scalar.activation(hid[:, b % 2, c, :], hid[:, b % 2, c, :], ACT.Square).then_inc(s["ffn_square_ready"], 1)

            def ffn_sigmoid(b):
                act.wait_ge(s["ffn_r_done"], b + 1)
                if b < 2:
                    act.wait_ge(s["rn_ready"], b + 1)
                else:
                    act.wait_ge(s["ffn_gated"], b - 1)
                nc.scalar.activation(rfT[:, b % 2, :], bank[5][:, :], ACT.Sigmoid).then_inc(s["rf_ready"], 1)

            def gate_sigmoid(b):
                act.wait_ge(gathered[b], 16 * CHUNK)
                if b == 0:
                    act.wait_ge(s["gap_t"], BLOCKS)
                    act.wait_ge(s["gap_s"], BLOCKS)
                nc.scalar.activation(gate[:, tls(b), :], moe[:, tls(b), :], ACT.Sigmoid).then_inc(s["gate_sigmoid"], 1)

            h_normalise(0)
            h_normalise(1)
            copy_xn(0)
            h_normalise(2)
            copy_xn(1)
            copy_h(0)
            copy_xn(2)
            copy_h(1)
            h_normalise(3)
            copy_xn(3)
            copy_h(2)
            overflow_relu(0, 0)
            copy_h(3)
            copy_projected(0, 0)
            overflow_relu(0, 1)
            copy_projected(0, 1)
            overflow_relu(0, 2)
            copy_projected(0, 2)
            overflow_relu(0, 3)
            copy_projected(1, 0)
            overflow_relu(1, 0)
            copy_projected(1, 1)
            overflow_bias(0)
            copy_projected(1, 2)
            overflow_relu(1, 1)
            copy_projected(2, 0)
            overflow_relu(1, 2)
            copy_projected(2, 1)
            overflow_relu(1, 3)
            copy_projected(2, 2)
            overflow_relu(2, 0)
            copy_projected(3, 0)
            overflow_bias(1)
            copy_projected(3, 1)
            overflow_relu(2, 1)
            copy_projected(3, 2)
            nc.scalar.preload_act_table_set("natural_log_exp_and_others")
            overflow_relu(2, 2)
            overflow_tokens(0)
            overflow_relu(2, 3)
            wkv_exponentials(0)
            overflow_relu(3, 0)
            wkv_exponentials(1)
            overflow_relu(3, 1)
            overflow_bias(2)
            overflow_relu(3, 2)
            overflow_relu(3, 3)
            copy_slots(0)
            copy_slots(1)
            expert_relu(0, 0)
            wkv_reciprocal(0)
            copy_slots(2)
            for c in range(1, 4):
                expert_relu(0, c)
            overflow_tokens(1)
            for c in range(3):
                expert_relu(1, c)
            wkv_reciprocal(1)
            overflow_bias(3)
            expert_relu(1, 3)
            overflow_tokens(2)
            wkv_exponentials(2)
            overflow_tokens(3)
            expert_bias(0)
            for c in range(3):
                expert_relu(2, c)
            expert_rows(0)
            expert_relu(2, 3)
            wkv_exponentials(3)
            expert_bias(1)
            expert_relu(3, 0)
            expert_relu(3, 1)
            expert_bias(2)
            expert_relu(3, 2)
            expert_relu(3, 3)
            wkv_reciprocal(2)
            expert_rows(1)
            expert_relu(4, 0)
            expert_relu(4, 1)
            copy_h3(0)
            expert_relu(4, 2)
            expert_bias(3)
            expert_relu(4, 3)
            expert_relu(5, 0)
            expert_relu(5, 1)
            expert_rows(2)
            expert_relu(5, 2)
            expert_relu(5, 3)
            wkv_reciprocal(3)
            expert_bias(4)
            nc.scalar.preload_act_table_set("sigmoid_and_others")
            expert_rows(3)
            for c in range(3):
                expert_relu(6, c)
            expert_bias(5)
            expert_relu(6, 3)
            expert_rows(4)
            for c in range(3):
                expert_relu(7, c)
            copy_h3(1)
            expert_bias(6)
            expert_relu(7, 3)
            expert_rows(5)
            ffn_relu(0, 0)
            expert_bias(7)
            ffn_relu(0, 1)
            ffn_square_act(0, 1)
            ffn_sigmoid(0)
            ffn_relu(0, 2)
            expert_rows(6)
            ffn_relu(0, 3)
            copy_h3(2)
            ffn_square_act(0, 3)
            expert_rows(7)
            ffn_relu(1, 0)
            ffn_relu(1, 1)
            copy_h3(3)
            ffn_square_act(1, 1)
            ffn_relu(1, 2)
            ffn_sigmoid(1)
            ffn_relu(1, 3)
            ffn_square_act(1, 3)
            ffn_relu(2, 0)
            ffn_sigmoid(2)
            gate_sigmoid(0)
            ffn_relu(2, 1)
            ffn_square_act(2, 1)
            ffn_relu(2, 2)
            gate_sigmoid(1)
            ffn_relu(2, 3)
            ffn_square_act(2, 3)
            ffn_relu(3, 0)
            ffn_sigmoid(3)
            ffn_relu(3, 1)
            ffn_square_act(3, 1)
            gate_sigmoid(2)
            ffn_relu(3, 2)
            ffn_relu(3, 3)
            ffn_square_act(3, 3)
            gate_sigmoid(3)

        @block.vector
        def _(dve):
            def statistics(n, src, arrived, stats_done, mv_done, b):
                for t in range(b * CHUNK, (b + 1) * CHUNK):
                    arrived(t)
                    nc.vector.bn_stats(stats[:, n, t, :], src[:, t, :]).then_inc(stats_done, 1)
                for t in range(b * CHUNK, (b + 1) * CHUNK):
                    dve.wait_ge(stats_done, t + 1)
                    nc.vector.bn_aggr(mv[:, n, t, :], stats[:, n, t, :]).then_inc(mv_done, 1)

            def normalise(n, dst, src, rstd_done, done, b):
                dve.wait_ge(rstd_done, b + 1)
                for t in range(b * CHUNK, (b + 1) * CHUNK):
                    nc.vector.tensor_scalar(dst[:, t - b * CHUNK, :], src[:, t, :], mv[:, n, t, 0:1], rstd[:, n, t:t + 1],
                                            ALU.subtract, ALU.mult).then_inc(done, 1)

            def mix(b, names, diffs, dones, first_use):
                dve.wait_ge(diffs, b + 1)
                first_use()
                q, before = seq_cols(b, 0)
                for n, name in enumerate(names):
                    nc.vector.scalar_tensor_tensor(out=mixed[:, b % 2, n, :], in0=diff[:, b % 2, :], scalar=param(name),
                                                   in1=hT[:, q, before], op0=ALU.mult, op1=ALU.add).then_inc(dones[n], 1)

            def x_stats(b):
                statistics(0, x_sb, lambda t: dve.wait_ge(x_loaded[t // CHUNK], 16), s["x_stats"], s["x_mv"], b)

            def att_mix(b):
                def first_use():
                    if b == 0:
                        dve.wait_ge(s["params_loaded"], 16)
                    if b >= 2:
                        dve.wait_ge(s["r_done"], b - 1)
                mix(b, ("mix_k", "mix_v", "mix_r"), s["hT_diff"], (s["mixed_k"], s["mixed_v"], s["mixed_r"]), first_use)

            def route_choose():
                at = pcol["router_b"][0]
                dve.wait_ge(s["logits_done"], BLOCKS)
                nc.vector.tensor_tensor(logits[:, :, :], bank[7][:, 0:E * TILES].rearrange("p (e t) -> p e t", e=E),
                                        par[:, at:at + E].unsqueeze(2).to_broadcast([P, E, TILES]),
                                        ALU.add).then_inc(s["logits_biased"], 1)
                dve.wait_ge(s["logits_biased"], 1)
                nc.vector.tensor_reduce(row_max[:, :], logits[:, :, :].rearrange("p e t -> p t e"), AX_X,
                                        ALU.max).then_inc(s["logit_max"], 1)
                dve.wait_ge(s["logit_max"], 1)
                nc.vector.tensor_tensor(is_max[:, :, :], logits[:, :, :], row_max[:, :].unsqueeze(1).to_broadcast([P, E, TILES]),
                                        ALU.is_equal).then_inc(s["is_max"], 1)
                dve.wait_ge(s["is_max"], 1)
                dve.wait_ge(s["expert_code_ready"], 1)
                nc.vector.tensor_tensor(code[:, :, :], is_max[:, :, :], expert_code[:, :, :], ALU.mult).then_inc(s["max_code"], 1)
                dve.wait_ge(s["max_code"], 1)
                nc.vector.tensor_reduce(code_max[:, :], code[:, :, :].rearrange("p e t -> p t e"), AX_X,
                                        ALU.max).then_inc(s["code_max"], 1)
                dve.wait_ge(s["code_max"], 1)
                nc.vector.tensor_tensor(onehot[:, :, :], expert_code[:, :, :],
                                        code_max[:, :].unsqueeze(1).to_broadcast([P, E, TILES]),
                                        ALU.is_equal).then_inc(s["onehot_ready"], 1)
                nc.vector.tensor_scalar(base[:, :], code_max[:, :], -float(CAPACITY), float(E * CAPACITY - 1), ALU.mult,
                                        ALU.add).then_inc(s["expert_base"], 1)

            def route_slots():
                in_tile = bank[7][:, 128:256]
                totals = bank[7][:, 256:384]
                dve.wait_ge(s["counts_done"], 1)
                dve.wait_ge(s["run_mask_ready"], 1)
                nc.vector.tensor_tensor_scan(counts[:, :, :].rearrange("p e t -> p (e t)"),
                                             run_mask[:, :, :].rearrange("p e t -> p (e t)"), totals, 0.0, ALU.mult,
                                             ALU.add).then_inc(s["counts_run"], 1)
                dve.wait_ge(s["counts_run"], 1)
                nc.vector.tensor_tensor(rank_e[:, :, :].rearrange("p e t -> p (e t)"), in_tile,
                                        counts[:, :, :].rearrange("p e t -> p (e t)"), ALU.add).then_inc(s["rank_a"], 1)
                dve.wait_ge(s["rank_a"], 1)
                nc.vector.tensor_tensor(code[:, :, :].rearrange("p e t -> p (e t)"),
                                        rank_e[:, :, :].rearrange("p e t -> p (e t)"), totals,
                                        ALU.subtract).then_inc(s["rank_b"], 1)
                dve.wait_ge(s["rank_b"], 1)
                nc.vector.tensor_tensor(rank_e[:, :, :], code[:, :, :], onehot[:, :, :], ALU.mult).then_inc(s["rank_hot"], 1)
                dve.wait_ge(s["rank_hot"], 1)
                nc.vector.tensor_reduce(rank[:, :], rank_e[:, :, :].rearrange("p e t -> p t e"), AX_X,
                                        ALU.add).then_inc(s["rank_ready"], 1)
                dve.wait_ge(s["rank_ready"], 1)
                nc.vector.tensor_tensor(slot_f[:, :], base[:, :], rank[:, :], ALU.add).then_inc(s["slot_a"], 1)
                nc.vector.tensor_scalar(over[:, :], rank[:, :], float(CAPACITY), SKIP, ALU.is_gt,
                                        ALU.mult).then_inc(s["slot_over"], 1)
                dve.wait_ge(s["slot_a"], 1)
                dve.wait_ge(s["slot_over"], 1)
                nc.vector.tensor_tensor(slot[:, :], slot_f[:, :], over[:, :], ALU.add).then_inc(s["slot_ready"], 1)

            def wkv_gaps(b):
                i, (q, here), (_, before) = b % 2, seq_cols(b, 1), seq_cols(b, 0)
                dve.wait_ge(s["k_ready"], b + 1)
                if b == 0:
                    dve.wait_ge(s["decay_exp"], 1)
                    nc.vector.tensor_scalar(w_neg[:], w_exp[:], -1.0, None, ALU.mult).then_inc(s["w_ready"], 1)
                    dve.wait_ge(s["w_ready"], 1)
                    dve.wait_ge(s["state_zeroed"], 3)
                else:
                    dve.wait_ge(s["o_ready"], b)
                nc.vector.tensor_tensor_scan(o_state[:, q, here], w_neg[:].to_broadcast([P, NB]), kT[:, blk(b)],
                                             o_state[:, q, before.start:before.start + 1], ALU.add,
                                             ALU.max).then_inc(s["o_ready"], 1)
                dve.wait_ge(s["o_ready"], b + 1)
                nc.vector.scalar_tensor_tensor(out=gap[:, i, 0, :], in0=kT[:, blk(b)], scalar=param("first"),
                                               in1=o_state[:, q, before], op0=ALU.add,
                                               op1=ALU.subtract).then_inc(s["gap_t"], 1)
                nc.vector.scalar_tensor_tensor(out=gap[:, i, 1, :], in0=o_state[:, q, before], scalar=w_neg[:],
                                               in1=kT[:, blk(b)], op0=ALU.add, op1=ALU.subtract).then_inc(s["gap_s"], 1)
                dve.wait_ge(s["gap_t"], b + 1)
                dve.wait_ge(s["gap_s"], b + 1)
                nc.vector.tensor_scalar(e_neg[:, i, :, :], gap[:, i, :, :], 0.0, None, ALU.max).then_inc(s["gap_max"], 1)
                nc.vector.tensor_scalar(e_pos[:, i, :, :], gap[:, i, :, :], 0.0, None, ALU.min).then_inc(s["gap_min"], 1)

            def wkv_states(b):
                i, (q, here), (_, before) = b % 2, seq_cols(b, 1), seq_cols(b, 0)
                start = slice(before.start, before.start + 1)
                dve.wait_ge(s["exp_neg"], b + 1)
                dve.wait_ge(s["exp_pos"], b + 1)
                if b:
                    dve.wait_ge(s["q_ready"], b)
                nc.vector.tensor_tensor_scan(q_state[:, q, here], e_pos[:, i, 1, :], e_neg[:, i, 1, :],
                                             q_state[:, q, start], ALU.mult, ALU.add).then_inc(s["q_ready"], 1)
                dve.wait_ge(s["bv2_ready"], b + 1)
                if b:
                    dve.wait_ge(s["p_ready"], b)
                nc.vector.tensor_tensor_scan(p_state[:, q, here], e_pos[:, i, 1, :], bv2[:, i, :],
                                             p_state[:, q, start], ALU.mult, ALU.add).then_inc(s["p_ready"], 1)
                dve.wait_ge(s["q_ready"], b + 1)
                dve.wait_ge(s["p_ready"], b + 1)
                nc.vector.tensor_tensor(den[:, i, :], e_neg[:, i, 0, :], q_state[:, q, before],
                                        ALU.mult).then_inc(s["aq_ready"], 1)
                nc.vector.tensor_tensor(num[:, i, :], e_neg[:, i, 0, :], p_state[:, q, before],
                                        ALU.mult).then_inc(s["ap_ready"], 1)
                dve.wait_ge(s["aq_ready"], b + 1)
                nc.vector.tensor_tensor(den[:, i, :], den[:, i, :], e_pos[:, i, 0, :], ALU.add).then_inc(s["den_ready"], 1)
                dve.wait_ge(s["ap_ready"], b + 1)
                dve.wait_ge(s["bv_ready"], b + 1)
                nc.vector.tensor_tensor(num[:, i, :], num[:, i, :], bv[:, i, :], ALU.add).then_inc(s["num_ready"], 1)

            def wkv_divide(b):
                i = b % 2
                dve.wait_ge(s["den_inv"], b + 1)
                nc.vector.tensor_tensor(inv_err[:, i, :], den[:, i, :], inv[:, i, :], ALU.mult).then_inc(s["newton_a"], 1)
                dve.wait_ge(s["newton_a"], b + 1)
                nc.vector.scalar_tensor_tensor(out=inv_err[:, i, :], in0=inv_err[:, i, :], scalar=-2.0, in1=inv[:, i, :],
                                               op0=ALU.add, op1=ALU.mult).then_inc(s["newton_b"], 1)
                dve.wait_ge(s["newton_b"], b + 1)
                dve.wait_ge(s["rn_ready"], b + 1)
                if b >= 2:
                    dve.wait_ge(s["att_done"], b - 1)
                nc.vector.scalar_tensor_tensor(out=wkvT[:, i, :], in0=inv_err[:, i, :], scalar=-1.0, in1=bv[:, i, :],
                                               op0=ALU.mult, op1=ALU.mult).then_inc(s["wkvT_ready"], 1)

            def x2_and_stats(b):
                dve.wait_ge(s["att_done"], b + 1)
                if b == 0:
                    dve.wait_ge(s["scattered"], 16 * TILES)
                nc.vector.tensor_tensor(x2[:, tls(b), :], bank[7][:, :].rearrange("p (t d) -> p t d", d=D),
                                        xn[:, tls(b), :], ALU.add).then_inc(s["x2_ready"], 1)
                statistics(2, x2, lambda t: dve.wait_ge(s["x2_ready"], t // CHUNK + 1), s["x2_stats"], s["x2_mv"], b)

            def h3_normalise(b):
                if b < 2:
                    dve.wait_ge(s["h_turned"], BLOCKS)
                else:
                    dve.wait_ge(s["h3_turned"], b - 1)
                normalise(2, h_tok[:, b % 2, :, :], x2, s["x2_rstd"], s["h3_ready"], b)

            def ffn_mix(b):
                def first_use():
                    if b == 0:
                        dve.wait_ge(s["buf_turned"], 3)
                    elif b == 1:
                        dve.wait_ge(s["r_done"], BLOCKS)
                    else:
                        dve.wait_ge(s["ffn_r_done"], b - 1)
                        dve.wait_ge(s["ffn_hidden_done"], HC * (b - 1))
                mix(b, ("ffn_mix_k", "ffn_mix_r"), s["h3_diff"], (s["mixed_fk"], s["mixed_fr"]), first_use)

            def ffn_square(b, c):
                dve.wait_ge(s["ffn_relu_ready"], b * HC + c + 1)
                nc.vector.tensor_tensor(hid[:, b % 2, c, :], hid[:, b % 2, c, :], hid[:, b % 2, c, :],
                                        ALU.mult).then_inc(s["ffn_hidden_ready"], 1)

            def ffn_gated(b):
                dve.wait_ge(s["ffn_out_done"], b + 1)
                dve.wait_ge(s["rf_ready"], b + 1)
                if b >= 2:
                    dve.wait_ge(s["ffn_turned"], b - 1)
                nc.vector.tensor_tensor(gatedT[:, b % 2, :], bank[7][:, :], rfT[:, b % 2, :], ALU.mult).then_inc(s["ffn_gated"], 1)

            def add_channel_mix(b):
                dve.wait_ge(s["ffn_turned"], b + 1)
                nc.vector.tensor_tensor(x2[:, tls(b), :], bank[7][:, :].rearrange("p (t d) -> p t d", d=D),
                                        x2[:, tls(b), :], ALU.add).then_inc(s["s_ready"], 1)

            def finish(b):
                dve.wait_ge(s["s_ready"], b + 1)
                dve.wait_ge(s["gate_ready"], b + 1)
                nc.vector.tensor_tensor(x2[:, tls(b), :], x2[:, tls(b), :], gate[:, tls(b), :],
                                        ALU.mult).then_inc(s["s_gated"], 1)
                dve.wait_ge(s["s_gated"], b + 1)
                nc.vector.tensor_tensor(x_sb[:, tls(b), :], x_sb[:, tls(b), :], x2[:, tls(b), :],
                                        ALU.add).then_inc(s["out_ready"], 1)

            def xn_normalise(b):
                normalise(0, xn[:, tls(b), :], x_sb, s["x_rstd"], s["xn_ready"], b)

            for b in range(3):
                x_stats(b)
            xn_normalise(0)
            x_stats(3)
            for b in range(1, 4):
                xn_normalise(b)
            att_mix(0)
            att_mix(1)
            route_choose()
            wkv_gaps(0)
            route_slots()
            wkv_gaps(1)
            att_mix(2)
            att_mix(3)
            wkv_states(0)
            wkv_states(1)
            wkv_divide(0)
            wkv_gaps(2)
            wkv_divide(1)
            wkv_gaps(3)
            x2_and_stats(0)
            wkv_states(2)
            h3_normalise(0)
            wkv_states(3)
            wkv_divide(2)
            x2_and_stats(1)
            wkv_divide(3)
            h3_normalise(1)
            x2_and_stats(2)
            ffn_mix(0)
            x2_and_stats(3)
            h3_normalise(2)
            ffn_square(0, 0)
            h3_normalise(3)
            ffn_mix(1)
            ffn_square(0, 2)
            ffn_square(1, 0)
            ffn_mix(2)
            ffn_gated(0)
            ffn_square(1, 2)
            ffn_mix(3)
            add_channel_mix(0)
            ffn_square(2, 0)
            finish(0)
            ffn_gated(1)
            ffn_square(2, 2)
            add_channel_mix(1)
            ffn_square(3, 0)
            finish(1)
            ffn_gated(2)
            ffn_square(3, 2)
            add_channel_mix(2)
            finish(2)
            ffn_gated(3)
            add_channel_mix(3)
            finish(3)


def kernel(**inputs):
    import numpy as np
    import concourse.bacc as bacc
    from concourse.bass_utils import run_bass_kernel_spmd

    a = {name: np.asarray(value) for name, value in inputs.items()}
    att, ffn = "L0_attn_", "L0_ffn_"

    def column(v):
        return v.reshape(-1, P).T

    def chunks(w):
        return w.reshape(-1, P, w.shape[1]).transpose(1, 0, 2).reshape(P, -1)

    packed = {"ln_att_g": column(a[att + "ln_att_g"]), "ln_att_b": column(a[att + "ln_att_b"]),
              "ln_ffn_g": column(a[att + "ln_ffn_g"]), "ln_ffn_b": column(a[att + "ln_ffn_b"]),
              "decay": column(a[att + "att_time_decay"]), "first": column(a[att + "att_time_first"]),
              "mix_k": column(a[att + "att_mix_k"]), "mix_v": column(a[att + "att_mix_v"]),
              "mix_r": column(a[att + "att_mix_r"]), "ffn_mix_k": column(a[att + "ffn_mix_k"]),
              "ffn_mix_r": column(a[att + "ffn_mix_r"]), "ob2": column(a[ffn + "ob2"]), "ob1": column(a[ffn + "ob1"]),
              "b1": column(a[ffn + "b1"]), "b2": column(a[ffn + "b2"]),
              "router_b": np.repeat(a[ffn + "router_b"][None], P, axis=0), "router_w": a[ffn + "router_w"]}
    mats = {"wk": a[att + "att_wk"], "wv": a[att + "att_wv"], "wr": a[att + "att_wr"], "wo": a[att + "att_wo"],
            "ffn_wr": a[att + "ffn_wr"], "ffn_wk": a[att + "ffn_wk"], "ffn_wv": chunks(a[att + "ffn_wv"]),
            "ow1": a[ffn + "ow1"], "ow2": chunks(a[ffn + "ow2"])}
    x = a[att + "x"]
    arrays = {"x_dram": np.ascontiguousarray(x.reshape(-1, x.shape[-1])),
              "params_dram": np.ascontiguousarray(np.concatenate([packed[n] for n in PARAMS], axis=1)),
              "weights_dram": np.ascontiguousarray(np.concatenate([mats[n] for n in WEIGHTS], axis=1)),
              "w1_dram": np.ascontiguousarray(a[ffn + "w1"]), "w2_dram": np.ascontiguousarray(a[ffn + "w2"])}

    nc = bacc.Bacc("TRN2", target_bir_lowering=False, num_devices=1)
    args = [nc.dram_tensor(n, v.shape, mybir.dt.from_np(v.dtype), kind="ExternalInput").ap() for n, v in arrays.items()]
    out = nc.dram_tensor("out_dram", arrays["x_dram"].shape, F32, kind="ExternalOutput").ap()
    build(nc, *args, out)
    result = run_bass_kernel_spmd(nc, [arrays], core_ids=[0])
    return result.results[0]["out_dram"].reshape(x.shape)
```

```python
from contextlib import ExitStack

import concourse.bass as bass
from concourse import mybir

ALU = mybir.AluOpType
ACT = mybir.ActivationFunctionType
F32 = mybir.dt.float32
F32R = mybir.dt.float32r
I32 = mybir.dt.int32
AX_X = mybir.AxisListType.X

P = 128
EPS = 1e-5
CAPACITY = 160
NO_STATE = -1e38
SKIP = 4096.0

PARAMS = {"ln_att_g": 1, "ln_att_b": 1, "ln_ffn_g": 1, "ln_ffn_b": 1, "decay": 1, "first": 1, "mix_k": 1, "mix_v": 1,
          "mix_r": 1, "ffn_mix_k": 1, "ffn_mix_r": 1, "ob2": 1, "ob1": 4, "b1": 32, "b2": 8, "router_b": 8, "router_w": 8}
WEIGHTS = {"wk": 128, "wv": 128, "wr": 128, "wo": 128, "ffn_wr": 128, "ffn_wk": 512, "ffn_wv": 512, "ow1": 512, "ow2": 512}
EARLY_WEIGHTS = 3 * P
WARM_UP = 15

SEMAPHORES = """
first_tiles_loaded x_loaded0 x_loaded1 x_loaded2 x_loaded3 params_loaded early_weights_loaded weights_loaded
w1_loaded0 w1_loaded1 w1_loaded2 w2_loaded0 w2_loaded1 w2_loaded2
ident_cleared ident_ready tri_ready ones_ready pow_ready expert_code_ready run_mask_set run_mask_ready zeros_ready
column_zeroed state_zeroed decay_exp w_ready buf_zeroed
x_stats x_mv x_var_eps h_var_eps x_rstd h_rstd h_bias_ready xn_ready h_ready
xn_turned h_turned xnT_ready hT_ready hT_diff mixed_k mixed_v mixed_r k_done v_done r_done k_ready v_ready r_ready
logits_done logits_biased logit_max is_max max_code code_max onehot_ready counts_done counts_run rank_a rank_b rank_hot
rank_ready expert_base slot_a slot_over slot_ready scattered buf_loaded buf_turned bufT_ready
o_ready gap_t gap_s gap_max gap_min exp_neg exp_pos bv2_ready bv_ready p_ready q_ready ap_ready aq_ready num_ready den_ready
den_ln den_inv rn_ready newton_a newton_b wkvT_ready
att_done x2_ready x2_stats x2_mv x2_var_eps x2_rstd h3_ready h3_turned h3T_ready h3_diff mixed_fk mixed_fr
w_split_a w_split_b xn_split_a xn_split_b fk_split_a fk_split_b
over_hidden_done over_hidden_ready over_out_done over_outT_ready over_turned over_ready
hidden_done hidden_ready y_done yT_ready y_turned y_rows_ready y_stored0 y_stored1
gathered0 gathered1 gathered2 gathered3
ffn_hidden_done ffn_relu_ready ffn_hidden_ready ffn_square_ready ffn_r_done rf_ready ffn_out_done ffn_gated ffn_turned s_ready
last_out_done last_gated last_turned rest_gated rest_ready last_gate last_ready
gate_sigmoid gate_ready s_gated out_ready out_stored
""".split()


def columns(table):
    at, out = 0, {}
    for name, n in table.items():
        out[name] = (at, at + n)
        at += n
    return out


def build(nc, x, params, weights, w1, w2, out):
    n_tokens = x.shape[0]
    TILES = n_tokens // P
    CHUNK = 4
    BLOCKS = TILES // CHUNK
    NB = CHUNK * P
    SEQ = n_tokens // 2
    E, D, H = w1.shape
    HC = H // P
    SLOTS = E * CAPACITY
    SLOT_TILES = SLOTS // P
    HALF = CAPACITY // 2
    SLOT_BANK = (6, 5, 6)
    OUT_BANK = (7, 2, 7)
    RING = 3
    pcol, wcol = columns(PARAMS), columns(WEIGHTS)

    x_tiles = x.rearrange("(t p) d -> p t d", p=P)
    out_tiles = out.rearrange("(t p) d -> p t d", p=P)
    slot_rows = nc.dram_tensor("slot_rows", (SLOTS, D), F32, kind="Internal").ap()
    y_rows = nc.dram_tensor("y_rows", (SLOTS, D), F32, kind="Internal").ap()

    with ExitStack() as ctx:
        def sb(name, shape, dt=F32):
            return ctx.enter_context(nc.sbuf_tensor(name, shape, dt))

        s = {n: ctx.enter_context(nc.semaphore(n)) for n in SEMAPHORES}
        x_loaded = [s["x_loaded0"], s["x_loaded1"], s["x_loaded2"], s["x_loaded3"]]
        y_stored = [s["y_stored0"], s["y_stored1"]]
        gathered = [s["gathered0"], s["gathered1"], s["gathered2"], s["gathered3"]]
        w1_loaded = [s["w1_loaded0"], s["w1_loaded1"], s["w1_loaded2"]]
        w2_loaded = [s["w2_loaded0"], s["w2_loaded1"], s["w2_loaded2"]]
        bank = [ctx.enter_context(nc.psum_tensor(f"bank{i}", [P, 512], F32)) for i in range(8)]

        par = sb("par", [P, sum(PARAMS.values())])
        wts = sb("wts", [P, sum(WEIGHTS.values())])
        w1_sb = sb("w1_sb", [P, RING, H])
        w2_sb = sb("w2_sb", [P, RING, HC, D])
        ident = sb("ident", [P, P])
        tri = sb("tri", [P, P])
        ones = sb("ones", [P, P])
        zeros = sb("zeros", [P, D])
        minus_half = sb("minus_half", [P, CHUNK])
        expert_code = sb("expert_code", [P, E, TILES])
        run_mask = sb("run_mask", [P, E, TILES])
        w_neg = sb("w_neg", [P, 1])
        w_exp = sb("w_exp", [P, 1])

        x_sb = sb("x_sb", [P, TILES, D])
        xn = sb("xn", [P, TILES, D])
        h_tok = sb("h_tok", [P, 2, CHUNK, D])
        stats = sb("stats", [P, 3, TILES, 6])
        mv = sb("mv", [P, 3, TILES, 2])
        h_bias = sb("h_bias", [P, TILES])
        var_eps = sb("var_eps", [P, 3, TILES])
        rstd = sb("rstd", [P, 3, TILES])
        xnT = sb("xnT", [P, n_tokens])
        hT = sb("hT", [P, 2, SEQ + 1])
        diff = sb("diff", [P, 2, NB])
        mixed = sb("mixed", [P, 2, 3, NB])
        kT = sb("kT", [P, n_tokens])
        vT = sb("vT", [P, n_tokens])
        rT = sb("rT", [P, n_tokens])

        logits = sb("logits", [P, E, TILES])
        row_max = sb("row_max", [P, TILES])
        is_max = sb("is_max", [P, E, TILES])
        code = sb("code", [P, E, TILES])
        code_max = sb("code_max", [P, TILES])
        onehot = sb("onehot", [P, E, TILES])
        counts = sb("counts", [P, E, TILES])
        rank_e = sb("rank_e", [P, E, TILES])
        rank = sb("rank", [P, TILES])
        base = sb("base", [P, TILES])
        over = sb("over", [P, TILES])
        slot_f = sb("slot_f", [P, TILES])
        slot = sb("slot", [P, TILES], I32)

        o_state = sb("o_state", [P, SEQ + 1])
        p_state = sb("p_state", [P, SEQ + 1])
        q_state = sb("q_state", [P, SEQ + 1])
        gap = sb("gap", [P, 2, 2, NB])
        e_neg = sb("e_neg", [P, 2, 2, NB])
        e_pos = gap
        bv = sb("bv", [P, 2, NB])
        bv2 = sb("bv2", [P, 2, NB])
        num = sb("num", [P, 2, NB])
        den = bv2
        inv = sb("inv", [P, 2, NB])
        den_log = inv
        inv_err = den
        wkvT = sb("wkvT", [P, 2, NB])
        act_a = sb("act_a", [P, 2, NB], F32R)
        act_b = sb("act_b", [P, 2, NB], F32R)
        w_a = sb("w_a", [P, H], F32R)
        w_b = sb("w_b", [P, H], F32R)

        x2 = xn
        rfT = rT[:, 0:2 * NB].rearrange("p (i n) -> p i n", i=2)
        hid = sb("hid", [P, 2, HC, NB])
        e_hid = sb("e_hid", [P, 2, HC, CAPACITY])
        over_outT = sb("over_outT", [P, 2, NB])
        yT = over_outT[:, :, 0:CAPACITY]
        gatedT = sb("gatedT", [P, 2, NB])
        moe = sb("moe", [P, TILES, D])
        buf_rows = mixed[:, :, :, :].rearrange("p i n c -> p (i n c)")[:, 0:SLOT_TILES * D].rearrange(
            "p (t d) -> p t d", d=D)
        bufT = xnT
        y_sb = sb("y_sb", [HALF, 2, 2, D])
        gate = kT[:, :].rearrange("p (t d) -> p t d", d=D)

        def param(name, i=0):
            at = pcol[name][0] + i
            return par[:, at:at + 1]

        def weight(name, c=0):
            at = wcol[name][0] + c * P
            return wts[:, at:at + P]

        def seq_cols(b, shift):
            at = (b % 2) * NB + shift
            return b // 2, slice(at, at + NB)

        def blk(b):
            return slice(b * NB, (b + 1) * NB)

        def half(i):
            return slice(i * NB // 2, (i + 1) * NB // 2)

        def half_tiles(i):
            at = TILES - CHUNK + i * CHUNK // 2
            return slice(at, at + CHUNK // 2)

        def tls(b):
            return slice(b * CHUNK, (b + 1) * CHUNK)

        block = ctx.enter_context(nc.Block())

        @block.sync
        def _(sp):
            sp.dma_start(x_sb[:, 0:2, :], x_tiles[:, 0:2, :]).then_inc(s["first_tiles_loaded"], 16)
            sp.dma_start(x_sb[:, 2:CHUNK, :], x_tiles[:, 2:CHUNK, :]).then_inc(x_loaded[0], 16)
            sp.dma_start(x_sb[:, tls(1), :], x_tiles[:, tls(1), :]).then_inc(x_loaded[1], 16)
            sp.dma_start(par[:, :], params).then_inc(s["params_loaded"], 16)
            for b in range(2, BLOCKS):
                sp.dma_start(x_sb[:, tls(b), :], x_tiles[:, tls(b), :]).then_inc(x_loaded[b], 16)
            sp.dma_start(wts[:, 0:EARLY_WEIGHTS], weights[:, 0:EARLY_WEIGHTS]).then_inc(s["early_weights_loaded"], 16)
            sp.dma_start(wts[:, EARLY_WEIGHTS:], weights[:, EARLY_WEIGHTS:]).then_inc(s["weights_loaded"], 16)

            def load_w1(e):
                sp.dma_start(w1_sb[:, e % RING, :], w1[e]).then_inc(w1_loaded[e % RING], 16)

            def load_w2(e):
                sp.dma_start(w2_sb[:, e % RING, :, :], w2[e].rearrange("(c p) d -> p c d", p=P)).then_inc(
                    w2_loaded[e % RING], 16)

            sp.wait_ge(s["zeros_ready"], 1)
            sp.dma_start(slot_rows.rearrange("(p r) d -> p r d", p=P),
                         zeros[:, :].unsqueeze(1).to_broadcast([P, SLOT_TILES, D])).then_inc(s["buf_zeroed"], 16)
            for e in range(RING):
                load_w1(e)
                load_w2(e)
            sp.wait_ge(s["r_done"], BLOCKS - 1)
            sp.wait_ge(s["scattered"], 16 * TILES)
            sp.dma_start(buf_rows[:, :, :], slot_rows.rearrange("(t p) d -> p t d", p=P)).then_inc(s["buf_loaded"], 16)

            def store_rows(e):
                sp.wait_ge(s["y_rows_ready"], e + 1)
                sp.dma_start(y_rows.rearrange("(e a p) d -> p e a d", e=E, a=2)[:, e], y_sb[:, e % 2, :, :]).then_inc(
                    y_stored[e % 2], 16)

            for e in range(E - RING):
                sp.wait_ge(s["hidden_done"], HC * (e + 1))
                load_w1(e + RING)
                if e:
                    store_rows(e - 1)
                sp.wait_ge(s["y_done"], e + 1)
                load_w2(e + RING)
            for e in range(E - RING - 1, E):
                store_rows(e)
            for b in range(BLOCKS - 1):
                sp.wait_ge(s["out_ready"], b + 1)
                sp.dma_start(out_tiles[:, tls(b), :], x_sb[:, tls(b), :]).then_inc(s["out_stored"], 16)
            for i in range(2):
                sp.wait_ge(s["last_ready"], i + 1)
                sp.dma_start(out_tiles[:, half_tiles(i), :], x_sb[:, half_tiles(i), :]).then_inc(s["out_stored"], 16)
            sp.wait_ge(s["out_stored"], 16 * (BLOCKS + 1))

        @block.gpsimd
        def _(pool):
            nc.gpsimd.memset(ident[:], 0.0).then_inc(s["ident_cleared"], 1)
            nc.gpsimd.memset(minus_half[:], -0.5).then_inc(s["pow_ready"], 1)
            nc.gpsimd.memset(ones[:], 1.0).then_inc(s["ones_ready"], 1)
            pool.wait_ge(s["ident_cleared"], 1)
            nc.gpsimd.affine_select(out=ident[:], in_=ident[:], compare_op=ALU.not_equal, fill=1.0, base=0,
                                    pattern=[[-1, P]], channel_multiplier=1).then_inc(s["ident_ready"], 1)
            nc.gpsimd.memset(zeros[:], 0.0).then_inc(s["zeros_ready"], 1)
            nc.gpsimd.memset(hT[:, :, 0:1], 0.0).then_inc(s["column_zeroed"], 1)
            pool.wait_ge(s["ones_ready"], 1)
            nc.gpsimd.affine_select(out=tri[:], in_=ones[:], compare_op=ALU.is_ge, fill=0.0, base=0,
                                    pattern=[[1, P]], channel_multiplier=-1).then_inc(s["tri_ready"], 1)
            nc.gpsimd.iota(expert_code[:, :, :], [[-1, E], [0, TILES]], base=E, channel_multiplier=0,
                           allow_small_or_imprecise_dtypes=True).then_inc(s["expert_code_ready"], 1)
            nc.gpsimd.memset(run_mask[:], 1.0).then_inc(s["run_mask_set"], 1)
            pool.wait_ge(s["run_mask_set"], 1)
            nc.gpsimd.memset(run_mask[:, :, 0:1], 0.0).then_inc(s["run_mask_ready"], 1)
            nc.gpsimd.memset(o_state[:, 0:1], NO_STATE).then_inc(s["state_zeroed"], 1)
            nc.gpsimd.memset(p_state[:, 0:1], 0.0).then_inc(s["state_zeroed"], 1)
            nc.gpsimd.memset(q_state[:, 0:1], 0.0).then_inc(s["state_zeroed"], 1)
            pool.wait_ge(s["pow_ready"], 1)

            def power(n, ready, done, b):
                pool.wait_ge(ready, b + 1)
                nc.gpsimd.tensor_tensor(rstd[:, n, tls(b)], var_eps[:, n, tls(b)], minus_half[:, :],
                                        ALU.pow).then_inc(done, 1)

            def input_roots(b):
                power(0, s["x_var_eps"], s["x_rstd"], b)

            def h_root(b):
                power(1, s["h_var_eps"], s["h_rstd"], b)

            def x2_root(b):
                power(2, s["x2_var_eps"], s["x2_rstd"], b)

            def less_before(b, ready, mixed_last, done):
                pool.wait_ge(ready, b + 1)
                if b >= 2:
                    pool.wait_ge(mixed_last, b - 1)
                else:
                    pool.wait_ge(s["column_zeroed"], 1)
                q, here = seq_cols(b, 1)
                _, before = seq_cols(b, 0)
                nc.gpsimd.tensor_tensor(diff[:, b % 2, :], hT[:, q, here], hT[:, q, before],
                                        ALU.subtract).then_inc(done, 1)

            def shift_diff(b):
                less_before(b, s["hT_ready"], s["mixed_r"], s["hT_diff"])

            def h3_diff(b):
                less_before(b, s["h3T_ready"], s["mixed_fr"], s["h3_diff"])

            def scatter(t):
                if t == 0:
                    pool.wait_ge(s["slot_ready"], 1)
                    pool.wait_ge(s["xn_ready"], TILES)
                    pool.wait_ge(s["buf_zeroed"], 16)
                nc.gpsimd.indirect_dma_start(slot_rows, bass.IndirectOffsetOnAxis(ap=slot[:, t:t + 1], axis=0),
                                             xn[:, t, :], None, bounds_check=SLOTS - 1,
                                             oob_is_err=False).then_inc(s["scattered"], 16)

            def wkv_products(b):
                i = b % 2
                if b >= 2:
                    pool.wait_ge(s["wkvT_ready"], b - 1)
                pool.wait_ge(s["v_ready"], b + 1)
                pool.wait_ge(s["exp_neg"], b + 1)
                nc.gpsimd.tensor_tensor(bv2[:, i, :], e_neg[:, i, 1, :], vT[:, blk(b)], ALU.mult).then_inc(s["bv2_ready"], 1)
                pool.wait_ge(s["exp_pos"], b + 1)
                nc.gpsimd.tensor_tensor(bv[:, i, :], e_pos[:, i, 0, :], vT[:, blk(b)], ALU.mult).then_inc(s["bv_ready"], 1)

            def wkv_times_r(b):
                i = b % 2
                pool.wait_ge(s["num_ready"], b + 1)
                pool.wait_ge(s["r_ready"], b + 1)
                nc.gpsimd.tensor_tensor(bv[:, i, :], num[:, i, :], rT[:, blk(b)], ALU.mult).then_inc(s["rn_ready"], 1)

            def weight_b(name, n):
                pool.wait_ge(s["w_split_a"], n + 1)
                nc.gpsimd.tensor_tensor(w_b[:, :], wts[:, wcol[name][0]:wcol[name][1]], w_a[:, :].bitcast(F32),
                                        ALU.subtract).then_inc(s["w_split_b"], 1)

            def ow1_b():
                weight_b("ow1", 0)

            def ffn_wk_b():
                weight_b("ffn_wk", 1)

            def gather(t):
                if t == 0:
                    pool.wait_ge(s["over_ready"], BLOCKS)
                    for stored in y_stored:
                        pool.wait_ge(stored, 16 * E // 2)
                nc.gpsimd.indirect_dma_start(moe[:, t, :], None, y_rows,
                                             bass.IndirectOffsetOnAxis(ap=slot[:, t:t + 1], axis=0),
                                             bounds_check=SLOTS - 1, oob_is_err=False).then_inc(gathered[t // CHUNK], 16)

            def gate_times(b):
                pool.wait_ge(s["gate_sigmoid"], b + 1)
                nc.gpsimd.tensor_tensor(gate[:, tls(b), :], gate[:, tls(b), :], moe[:, tls(b), :],
                                        ALU.mult).then_inc(s["gate_ready"], 1)

            h_root(0)
            input_roots(0)
            h_root(1)
            input_roots(1)
            input_roots(2)
            shift_diff(0)
            input_roots(3)
            h_root(2)
            h_root(3)
            shift_diff(1)
            ow1_b()
            shift_diff(2)
            shift_diff(3)
            for t in range(11):
                scatter(t)
            wkv_products(0)
            for t in range(11, 16):
                scatter(t)
            wkv_products(1)
            wkv_times_r(0)
            wkv_times_r(1)
            ffn_wk_b()
            wkv_products(2)
            wkv_products(3)
            x2_root(0)
            wkv_times_r(2)
            x2_root(1)
            h3_diff(0)
            wkv_times_r(3)
            h3_diff(1)
            x2_root(2)
            h3_diff(2)
            x2_root(3)
            for t in range(3):
                gather(t)
            h3_diff(3)
            for t in range(3, 11):
                gather(t)
            gate_times(0)
            for t in range(11, 16):
                gather(t)
            for b in range(1, 4):
                gate_times(b)

        @block.tensor
        def _(pe):
            def turn_xn(b):
                if b == 0:
                    pe.wait_ge(s["ident_ready"], 1)
                if b >= 2:
                    pe.wait_ge(s["xnT_ready"], b - 1)
                pe.wait_ge(s["xn_ready"], CHUNK * (b + 1))
                for t in range(CHUNK):
                    last = nc.tensor.transpose(bank[b % 2][:, t * P:(t + 1) * P], xn[:, b * CHUNK + t, :], ident[:])
                last.then_inc(s["xn_turned"], 1)

            def turn_h(b):
                if b >= 2:
                    pe.wait_ge(s["hT_ready"], b - 1)
                pe.wait_ge(s["h_ready"], CHUNK * (b + 1))
                for t in range(CHUNK):
                    last = nc.tensor.transpose(bank[2 + 4 * (b % 2)][:, t * P:(t + 1) * P], h_tok[:, b % 2, t, :], ident[:])
                last.then_inc(s["h_turned"], 1)

            def project(b, n):
                name, ready, used, done = (
                    ("wk", s["mixed_k"], s["k_ready"], s["k_done"]), ("wv", s["mixed_v"], s["v_ready"], s["v_done"]),
                    ("wr", s["mixed_r"], s["r_ready"], s["r_done"]))[n]
                if b == 0 and n == 0:
                    pe.wait_ge(s["early_weights_loaded"], 16)
                pe.wait_ge(ready, b + 1)
                if b:
                    pe.wait_ge(used, b)
                nc.tensor.matmul(bank[3 + n][:, :], weight(name), mixed[:, b % 2, n, :], start=True,
                                 stop=True).then_inc(done, 1)

            def route_logits(b):
                if b == 0:
                    pe.wait_ge(s["params_loaded"], 16)
                pe.wait_ge(s["xnT_ready"], b + 1)
                at = pcol["router_w"][0]
                for t in range(b * CHUNK, (b + 1) * CHUNK):
                    last = nc.tensor.matmul(bank[7][:, 0:E * TILES].rearrange("p (e t) -> p e t", e=E)[:, :, t],
                                            xnT[:, t * P:(t + 1) * P], par[:, at:at + E], start=True, stop=True)
                last.then_inc(s["logits_done"], 1)

            def count_tokens():
                pe.wait_ge(s["onehot_ready"], 1)
                pe.wait_ge(s["tri_ready"], 1)
                flat = onehot[:, :, :].rearrange("p e t -> p (e t)")
                nc.tensor.matmul(bank[7][:, 128:256], tri[:], flat, start=True, stop=True)
                nc.tensor.matmul(bank[7][:, 256:384], ones[:], flat, start=True, stop=True).then_inc(s["counts_done"], 1)

            def split_product(out, b, c):
                rows = slice(c * P, (c + 1) * P)
                nc.tensor.matmul(out[:, :], w_a[:, rows], act_a[:, b % 2, :], start=True, stop=False)
                nc.tensor.matmul(out[:, :], w_a[:, rows], act_b[:, b % 2, :], start=False, stop=False)
                return nc.tensor.matmul(out[:, :], w_b[:, rows], act_a[:, b % 2, :], start=False, stop=True)


            def overflow_hidden(b, c):
                n = b * HC + c
                if n == 0:
                    pe.wait_ge(s["weights_loaded"], 16)
                if n < 3:
                    pe.wait_ge(*((s["xnT_ready"], BLOCKS - 1), (s["xnT_ready"], BLOCKS), (s["hT_ready"], BLOCKS - 1))[n])
                else:
                    pe.wait_ge(s["over_hidden_ready"], n - 2)
                if b == 0:
                    pe.wait_ge(s["xnT_ready"], 1)
                    nc.tensor.matmul(bank[n % 3][:, :], weight("ow1", c), xnT[:, blk(b)], start=True,
                                     stop=True).then_inc(s["over_hidden_done"], 1)
                else:
                    pe.wait_ge(s["w_split_b"], 1)
                    pe.wait_ge(s["xn_split_b"], b)
                    split_product(bank[n % 3], b, c).then_inc(s["over_hidden_done"], 1)


            def overflow_out(b, *free):
                pe.wait_ge(*free)
                for c in range(HC):
                    pe.wait_ge(s["over_hidden_ready"], b * HC + c + 1)
                    last = nc.tensor.matmul(bank[6][:, :], weight("ow2", c), hid[:, b % 2, c, :], start=(c == 0),
                                            stop=(c == HC - 1))
                last.then_inc(s["over_out_done"], 1)

            def overflow_turn(b, *free):
                pe.wait_ge(*free)
                pe.wait_ge(s["over_outT_ready"], b + 1)
                for t in range(CHUNK):
                    last = nc.tensor.transpose(bank[5][:, t * P:(t + 1) * P], over_outT[:, b % 2, t * P:(t + 1) * P],
                                               ident[:])
                last.then_inc(s["over_turned"], 1)

            def turn_slots(g, *free):
                pe.wait_ge(*free)
                pe.wait_ge(s["buf_loaded"], 16)
                for n, t in enumerate(range(4 * g, min(4 * g + 4, SLOT_TILES))):
                    last = nc.tensor.transpose(bank[SLOT_BANK[g]][:, n * P:(n + 1) * P], buf_rows[:, t, :], ident[:])
                last.then_inc(s["buf_turned"], 1)

            def expert_hidden(e, c):
                m = BLOCKS * HC + e * HC + c
                if c == 0:
                    pe.wait_ge(w1_loaded[e % RING], 16 * (e // RING + 1))
                    pe.wait_ge(s["bufT_ready"], min(3, -(-(e + 1) * CAPACITY // NB)))
                if e == 0 and c < 3:
                    pe.wait_ge(s["over_hidden_ready"], m - 2)
                else:
                    pe.wait_ge(s["hidden_ready"], e * HC + c - 2)
                nc.tensor.matmul(bank[m % 3][:, 0:CAPACITY], w1_sb[:, e % RING, c * P:(c + 1) * P],
                                 bufT[:, e * CAPACITY:(e + 1) * CAPACITY], start=True, stop=True).then_inc(s["hidden_done"], 1)

            def expert_out(e, *free):
                pe.wait_ge(*free)
                pe.wait_ge(w2_loaded[e % RING], 16 * (e // RING + 1))
                for c in range(HC):
                    pe.wait_ge(s["hidden_ready"], e * HC + c + 1)
                    last = nc.tensor.matmul(bank[6][:, 0:CAPACITY], w2_sb[:, e % RING, c, :], e_hid[:, e % 2, c, :],
                                            start=(c == 0), stop=(c == HC - 1))
                last.then_inc(s["y_done"], 1)

            def expert_turn(e, *free):
                pe.wait_ge(*free)
                pe.wait_ge(s["yT_ready"], e + 1)
                for a in range(2):
                    last = nc.tensor.transpose(bank[6][0:HALF, a * P:(a + 1) * P], yT[:, e % 2, a * HALF:(a + 1) * HALF],
                                               ident[:])
                last.then_inc(s["y_turned"], 1)

            def attention_out(b, *free):
                pe.wait_ge(*free)
                pe.wait_ge(s["wkvT_ready"], b + 1)
                for t in range(CHUNK):
                    last = nc.tensor.matmul(bank[7][:, t * P:(t + 1) * P], wkvT[:, b % 2, t * P:(t + 1) * P],
                                            weight("wo"), start=True, stop=True)
                last.then_inc(s["att_done"], 1)

            def turn_h3(b, *free):
                pe.wait_ge(*free)
                pe.wait_ge(s["h3_ready"], CHUNK * (b + 1))
                for t in range(CHUNK):
                    last = nc.tensor.transpose(bank[5][:, t * P:(t + 1) * P], h_tok[:, b % 2, t, :], ident[:])
                last.then_inc(s["h3_turned"], 1)

            def ffn_hidden(b, c):
                n = b * HC + c
                pe.wait_ge(s["fk_split_b"], b + 1)
                if n < 2:
                    pe.wait_ge((s["k_ready"], s["v_ready"])[n], BLOCKS)
                else:
                    pe.wait_ge(s["ffn_relu_ready"], n - 1)
                pe.wait_ge(s["w_split_b"], 2)
                split_product(bank[3 + n % 2], b, c).then_inc(s["ffn_hidden_done"], 1)

            def ffn_gate(b, *free):
                pe.wait_ge(*free)
                pe.wait_ge(s["mixed_fr"], b + 1)
                nc.tensor.matmul(bank[5][:, :], weight("ffn_wr"), mixed[:, b % 2, 1, :], start=True,
                                 stop=True).then_inc(s["ffn_r_done"], 1)

            def square_arrived(b, c):
                pe.wait_ge(s["ffn_hidden_ready"] if c % 2 == 0 else s["ffn_square_ready"], b * HC // 2 + c // 2 + 1)

            def ffn_out(b, *free):
                pe.wait_ge(*free)
                for c in range(HC):
                    square_arrived(b, c)
                    last = nc.tensor.matmul(bank[OUT_BANK[b]][:, :], weight("ffn_wv", c), hid[:, b % 2, c, :],
                                            start=(c == 0), stop=(c == HC - 1))
                last.then_inc(s["ffn_out_done"], 1)

            def ffn_turn(b):
                pe.wait_ge(s["ffn_gated"], b + 1)
                for t in range(CHUNK):
                    last = nc.tensor.transpose(bank[OUT_BANK[b]][:, t * P:(t + 1) * P],
                                               gatedT[:, b % 2, t * P:(t + 1) * P], ident[:])
                last.then_inc(s["ffn_turned"], 1)

            def last_out(i):
                if i == 0:
                    pe.wait_ge(s["hidden_ready"], E * HC)
                for c in range(HC):
                    square_arrived(BLOCKS - 1, c)
                    last = nc.tensor.matmul(bank[i][:, 0:NB // 2], weight("ffn_wv", c), hid[:, (BLOCKS - 1) % 2, c, half(i)],
                                            start=(c == 0), stop=(c == HC - 1))
                last.then_inc(s["last_out_done"], 1)

            def last_turn(i):
                pe.wait_ge(s["last_gated"], i + 1)
                for t in range(CHUNK // 2):
                    tile = i * CHUNK // 2 + t
                    last = nc.tensor.transpose(bank[i][:, t * P:(t + 1) * P],
                                               gatedT[:, (BLOCKS - 1) % 2, tile * P:(tile + 1) * P], ident[:])
                last.then_inc(s["last_turned"], 1)

            def keep_warm(products):
                for _ in range(products):
                    nc.tensor.matmul(bank[7][:, 384:512], zeros[:], zeros[:], start=True, stop=True)

            pe.wait_ge(s["zeros_ready"], 1)
            keep_warm(WARM_UP)

            turn_h(0)
            turn_xn(0)
            keep_warm(3)
            route_logits(0)
            keep_warm(1)
            turn_xn(1)
            turn_h(1)
            turn_xn(2)
            route_logits(1)
            turn_xn(3)
            route_logits(2)
            overflow_hidden(0, 0)
            turn_h(2)
            route_logits(3)
            for c in range(3):
                project(0, c)
            turn_h(3)
            project(1, 0)
            count_tokens()
            project(1, 1)
            project(1, 2)
            overflow_hidden(0, 1)
            for c in range(3):
                project(2, c)
            overflow_hidden(0, 2)
            overflow_hidden(0, 3)
            overflow_hidden(1, 0)
            for c in range(3):
                project(3, c)
            overflow_out(0, s["hT_ready"], BLOCKS)
            for c in range(1, 4):
                overflow_hidden(1, c)
            overflow_turn(0, s["r_ready"], BLOCKS)
            for c in range(4):
                overflow_hidden(2, c)
            overflow_hidden(3, 0)
            overflow_out(1, s["over_outT_ready"], 1)
            overflow_hidden(3, 1)
            overflow_hidden(3, 2)
            overflow_out(2, s["over_outT_ready"], 2)
            overflow_turn(1, s["over_ready"], 1)
            overflow_hidden(3, 3)
            turn_slots(0, s["over_outT_ready"], 3)
            turn_slots(1, s["over_ready"], 2)
            turn_slots(2, s["bufT_ready"], 1)
            expert_hidden(0, 0)
            expert_hidden(0, 1)
            overflow_out(3, s["bufT_ready"], 3)
            expert_hidden(0, 2)
            attention_out(0, s["rank_b"], 1)
            expert_hidden(0, 3)
            overflow_turn(2, s["bufT_ready"], 2)
            for c in range(3):
                expert_hidden(1, c)
            overflow_turn(3, s["over_ready"], 3)
            expert_hidden(1, 3)
            expert_hidden(2, 0)
            expert_hidden(2, 1)
            expert_out(0, s["over_outT_ready"], 4)
            attention_out(1, s["x2_ready"], 1)
            expert_turn(0, s["yT_ready"], 1)
            expert_hidden(2, 2)
            expert_hidden(2, 3)
            expert_hidden(3, 0)
            expert_out(1, s["y_rows_ready"], 1)
            expert_hidden(3, 1)
            expert_hidden(3, 2)
            expert_out(2, s["yT_ready"], 2)
            expert_hidden(3, 3)
            expert_hidden(4, 0)
            expert_turn(1, s["yT_ready"], 3)
            expert_hidden(4, 1)
            turn_h3(0, s["over_ready"], 4)
            expert_turn(2, s["y_rows_ready"], 2)
            expert_hidden(4, 2)
            expert_hidden(4, 3)
            expert_hidden(5, 0)
            expert_out(3, s["y_rows_ready"], 3)
            for c in range(1, 4):
                expert_hidden(5, c)
            expert_turn(3, s["yT_ready"], 4)
            turn_h3(1, s["h3T_ready"], 1)
            expert_out(4, s["y_rows_ready"], 4)
            attention_out(2, s["x2_ready"], 2)
            expert_turn(4, s["yT_ready"], 5)
            expert_hidden(6, 0)
            expert_hidden(6, 1)
            expert_out(5, s["y_rows_ready"], 5)
            expert_hidden(6, 2)
            expert_hidden(6, 3)
            expert_hidden(7, 0)
            expert_turn(5, s["yT_ready"], 6)
            for c in range(1, 4):
                expert_hidden(7, c)
            expert_out(6, s["y_rows_ready"], 6)
            ffn_gate(0, s["h3T_ready"], 2)
            expert_turn(6, s["yT_ready"], 7)
            attention_out(3, s["x2_ready"], 3)
            turn_h3(2, s["rf_ready"], 1)
            expert_out(7, s["y_rows_ready"], 7)
            ffn_hidden(0, 0)
            expert_turn(7, s["yT_ready"], 8)
            ffn_hidden(0, 1)
            ffn_hidden(0, 2)
            ffn_gate(1, s["h3T_ready"], 3)
            ffn_hidden(0, 3)
            ffn_hidden(1, 0)
            ffn_hidden(1, 1)
            turn_h3(3, s["rf_ready"], 2)
            ffn_hidden(1, 2)
            ffn_hidden(1, 3)
            ffn_out(0, s["x2_ready"], 4)
            ffn_hidden(2, 0)
            ffn_hidden(2, 1)
            ffn_turn(0)
            ffn_hidden(2, 2)
            ffn_gate(2, s["h3T_ready"], 4)
            ffn_hidden(2, 3)
            ffn_hidden(3, 0)
            ffn_out(1, s["hidden_ready"], E * HC)
            ffn_hidden(3, 1)
            ffn_out(2, s["s_ready"], 1)
            ffn_turn(1)
            ffn_hidden(3, 2)
            ffn_turn(2)
            ffn_hidden(3, 3)
            ffn_gate(3, s["rf_ready"], 3)
            last_out(0)
            last_out(1)
            last_turn(0)
            last_turn(1)

        @block.scalar
        def _(act):
            nc.scalar.preload_act_table_set("natural_log_exp_and_others")
            act.wait_ge(s["params_loaded"], 16)
            nc.scalar.activation(w_exp[:], param("decay"), ACT.Exp).then_inc(s["decay_exp"], 1)
            nc.scalar.preload_act_table_set("sigmoid_and_others")

            def copy_xn(b):
                act.wait_ge(s["xn_turned"], b + 1)
                nc.scalar.copy(xnT[:, blk(b)], bank[b % 2][:, :]).then_inc(s["xnT_ready"], 1)

            def h_normalise(b):
                act.wait_ge(s["h_rstd"], b + 1)
                act.wait_ge(s["h_bias_ready"], b + 1)
                if b >= 2:
                    act.wait_ge(s["h_turned"], b - 1)
                for t in range(CHUNK):
                    n = b * CHUNK + t
                    nc.scalar.activation(h_tok[:, b % 2, t, :], x_sb[:, n, :], ACT.Identity,
                                         bias=h_bias[:, n:n + 1], scale=rstd[:, 1, n:n + 1]).then_inc(s["h_ready"], 1)

            def copy_h(b):
                act.wait_ge(s["h_turned"], b + 1)
                q, cols = seq_cols(b, 1)
                nc.scalar.activation(hT[:, q, cols], bank[2 + 4 * (b % 2)][:, :], ACT.Identity, bias=param("ln_att_b"),
                                     scale=param("ln_att_g")).then_inc(s["hT_ready"], 1)

            def copy_projected(b, n):
                act.wait_ge((s["k_done"], s["v_done"], s["r_done"])[n], b + 1)
                if n < 2:
                    nc.scalar.copy((kT, vT)[n][:, blk(b)], bank[3 + n][:, :]).then_inc((s["k_ready"], s["v_ready"])[n], 1)
                else:
                    nc.scalar.activation(rT[:, blk(b)], bank[5][:, :], ACT.Sigmoid).then_inc(s["r_ready"], 1)

            def wkv_exponentials(b):
                i = b % 2
                act.wait_ge(s["gap_max"], b + 1)
                nc.scalar.activation(e_neg[:, i, :, :], e_neg[:, i, :, :], ACT.Exp, scale=-1.0).then_inc(s["exp_neg"], 1)
                act.wait_ge(s["gap_min"], b + 1)
                nc.scalar.activation(e_pos[:, i, :, :], e_pos[:, i, :, :], ACT.Exp).then_inc(s["exp_pos"], 1)

            def wkv_reciprocal(b):
                i = b % 2
                act.wait_ge(s["den_ready"], b + 1)
                if b >= 2:
                    act.wait_ge(s["wkvT_ready"], b - 1)
                nc.scalar.activation(den_log[:, i, :], den[:, i, :], ACT.Ln).then_inc(s["den_ln"], 1)
                act.wait_ge(s["den_ln"], b + 1)
                nc.scalar.activation(inv[:, i, :], den_log[:, i, :], ACT.Exp, scale=-1.0).then_inc(s["den_inv"], 1)

            def overflow_relu(b, c):
                n = b * HC + c
                if b >= 2:
                    act.wait_ge(s["over_out_done"], b - 1)
                act.wait_ge(s["over_hidden_done"], n + 1)
                nc.scalar.activation(hid[:, b % 2, c, :], bank[n % 3][:, :], ACT.Relu,
                                     bias=param("ob1", c)).then_inc(s["over_hidden_ready"], 1)

            def ow1_a():
                act.wait_ge(s["weights_loaded"], 16)
                nc.scalar.copy(w_a[:, :], wts[:, wcol["ow1"][0]:wcol["ow1"][1]]).then_inc(s["w_split_a"], 1)

            def ffn_wk_a():
                act.wait_ge(s["over_hidden_done"], BLOCKS * HC)
                nc.scalar.copy(w_a[:, :], wts[:, wcol["ffn_wk"][0]:wcol["ffn_wk"][1]]).then_inc(s["w_split_a"], 1)

            def xn_a(b):
                act.wait_ge(s["xnT_ready"], b + 1)
                if b == 3:
                    act.wait_ge(s["over_hidden_done"], 2 * HC)
                nc.scalar.copy(act_a[:, b % 2, :], xnT[:, blk(b)]).then_inc(s["xn_split_a"], 1)

            def fk_a(b):
                act.wait_ge(s["mixed_fk"], b + 1)
                if b < 2:
                    act.wait_ge(s["over_hidden_done"], (3 + b) * HC)
                else:
                    act.wait_ge(s["ffn_hidden_done"], (b - 1) * HC)
                nc.scalar.copy(act_a[:, b % 2, :], mixed[:, b % 2, 0, :]).then_inc(s["fk_split_a"], 1)

            def overflow_bias(b):
                act.wait_ge(s["over_out_done"], b + 1)
                if b >= 2:
                    act.wait_ge(s["over_turned"], b - 1)
                nc.scalar.activation(over_outT[:, b % 2, :], bank[6][:, :], ACT.Identity,
                                     bias=param("ob2")).then_inc(s["over_outT_ready"], 1)

            def overflow_tokens(b):
                act.wait_ge(s["over_turned"], b + 1)
                nc.scalar.copy(moe[:, tls(b), :], bank[5][:, :].rearrange("p (t d) -> p t d", d=D)).then_inc(
                    s["over_ready"], 1)

            def copy_slots(g):
                act.wait_ge(s["buf_turned"], g + 1)
                if g == 0:
                    act.wait_ge(s["over_hidden_done"], BLOCKS * HC)
                    act.wait_ge(s["logits_done"], BLOCKS)
                n = min(NB, SLOTS - g * NB)
                nc.scalar.copy(bufT[:, g * NB:g * NB + n], bank[SLOT_BANK[g]][:, 0:n]).then_inc(s["bufT_ready"], 1)

            def expert_relu(e, c):
                n = e * HC + c
                if e >= 2:
                    act.wait_ge(s["y_done"], e - 1)
                act.wait_ge(s["hidden_done"], n + 1)
                nc.scalar.activation(e_hid[:, e % 2, c, :], bank[(BLOCKS * HC + n) % 3][:, 0:CAPACITY], ACT.Relu,
                                     bias=param("b1", n)).then_inc(s["hidden_ready"], 1)

            def expert_bias(e):
                act.wait_ge(s["y_done"], e + 1)
                if e == 0:
                    act.wait_ge(s["over_turned"], BLOCKS)
                if e >= 2:
                    act.wait_ge(s["y_turned"], e - 1)
                nc.scalar.activation(yT[:, e % 2, :], bank[6][:, 0:CAPACITY], ACT.Identity,
                                     bias=param("b2", e)).then_inc(s["yT_ready"], 1)

            def expert_rows(e):
                act.wait_ge(s["y_turned"], e + 1)
                if e >= 2:
                    act.wait_ge(y_stored[e % 2], 16 * (e // 2))
                nc.scalar.copy(y_sb[:, e % 2, :, :], bank[6][0:HALF, 0:2 * P].rearrange("p (a d) -> p a d", a=2)).then_inc(
                    s["y_rows_ready"], 1)

            def copy_h3(b):
                act.wait_ge(s["h3_turned"], b + 1)
                if b == 0:
                    act.wait_ge(s["mixed_r"], BLOCKS)
                q, cols = seq_cols(b, 1)
                nc.scalar.activation(hT[:, q, cols], bank[5][:, :], ACT.Identity, bias=param("ln_ffn_b"),
                                     scale=param("ln_ffn_g")).then_inc(s["h3T_ready"], 1)

            def ffn_relu(b, c):
                n = b * HC + c
                act.wait_ge(s["ffn_hidden_done"], n + 1)
                if b < 2:
                    act.wait_ge(s["over_out_done"], BLOCKS - 1 + b)
                else:
                    act.wait_ge(s["ffn_out_done"], b - 1)
                nc.scalar.activation(hid[:, b % 2, c, :], bank[3 + n % 2][:, :], ACT.Relu).then_inc(s["ffn_relu_ready"], 1)

            def ffn_square_act(b, c):
                act.wait_ge(s["ffn_relu_ready"], b * HC + c + 1)
                nc.scalar.activation(hid[:, b % 2, c, :], hid[:, b % 2, c, :], ACT.Square).then_inc(s["ffn_square_ready"], 1)

            def ffn_sigmoid(b):
                act.wait_ge(s["ffn_r_done"], b + 1)
                if b < 2:
                    act.wait_ge(s["rn_ready"], b + 1)
                else:
                    act.wait_ge(s["ffn_gated"], b - 1)
                nc.scalar.activation(rfT[:, b % 2, :], bank[5][:, :], ACT.Sigmoid).then_inc(s["rf_ready"], 1)

            def gate_sigmoid(b):
                act.wait_ge(gathered[b], 16 * CHUNK)
                if b == 0:
                    act.wait_ge(s["gap_t"], BLOCKS)
                    act.wait_ge(s["gap_s"], BLOCKS)
                nc.scalar.activation(gate[:, tls(b), :], moe[:, tls(b), :], ACT.Sigmoid).then_inc(s["gate_sigmoid"], 1)

            h_normalise(0)
            copy_h(0)
            copy_xn(0)
            h_normalise(1)
            ow1_a()
            copy_xn(1)
            copy_h(1)
            copy_xn(2)
            h_normalise(2)
            copy_xn(3)
            xn_a(1)
            copy_h(2)
            xn_a(2)
            h_normalise(3)
            for c in range(3):
                copy_projected(0, c)
            overflow_relu(0, 0)
            copy_projected(1, 0)
            copy_h(3)
            copy_projected(1, 1)
            copy_projected(1, 2)
            overflow_relu(0, 1)
            for c in range(3):
                copy_projected(2, c)
            overflow_relu(0, 2)
            overflow_relu(0, 3)
            overflow_relu(1, 0)
            for c in range(3):
                copy_projected(3, c)
            nc.scalar.preload_act_table_set("natural_log_exp_and_others")
            wkv_exponentials(0)
            overflow_bias(0)
            overflow_relu(1, 1)
            overflow_relu(1, 2)
            xn_a(3)
            overflow_tokens(0)
            overflow_relu(1, 3)
            overflow_relu(2, 0)
            overflow_relu(2, 1)
            wkv_exponentials(1)
            overflow_relu(2, 2)
            overflow_relu(2, 3)
            wkv_reciprocal(0)
            overflow_bias(1)
            overflow_relu(3, 0)
            overflow_relu(3, 1)
            wkv_exponentials(2)
            overflow_relu(3, 2)
            overflow_bias(2)
            overflow_tokens(1)
            overflow_relu(3, 3)
            for b in range(3):
                copy_slots(b)
            expert_relu(0, 0)
            ffn_wk_a()
            wkv_reciprocal(1)
            wkv_exponentials(3)
            overflow_bias(3)
            for c in range(1, 4):
                expert_relu(0, c)
            overflow_tokens(2)
            for c in range(3):
                expert_relu(1, c)
            overflow_tokens(3)
            expert_relu(1, 3)
            expert_bias(0)
            expert_relu(2, 0)
            expert_relu(2, 1)
            expert_rows(0)
            expert_relu(2, 2)
            expert_relu(2, 3)
            wkv_reciprocal(2)
            expert_bias(1)
            for c in range(3):
                expert_relu(3, c)
            expert_bias(2)
            expert_relu(3, 3)
            expert_relu(4, 0)
            expert_rows(1)
            expert_relu(4, 1)
            copy_h3(0)
            expert_rows(2)
            expert_relu(4, 2)
            expert_relu(4, 3)
            expert_relu(5, 0)
            expert_bias(3)
            wkv_reciprocal(3)
            expert_rows(3)
            nc.scalar.preload_act_table_set("sigmoid_and_others")
            expert_relu(5, 1)
            expert_bias(4)
            expert_relu(5, 2)
            expert_relu(5, 3)
            expert_rows(4)
            expert_relu(6, 0)
            expert_relu(6, 1)
            copy_h3(1)
            expert_bias(5)
            expert_relu(6, 2)
            expert_relu(6, 3)
            expert_relu(7, 0)
            expert_rows(5)
            for c in range(1, 4):
                expert_relu(7, c)
            fk_a(0)
            expert_bias(6)
            ffn_sigmoid(0)
            expert_rows(6)
            fk_a(1)
            copy_h3(2)
            expert_bias(7)
            ffn_relu(0, 0)
            expert_rows(7)
            ffn_relu(0, 1)
            ffn_square_act(0, 1)
            ffn_relu(0, 2)
            ffn_sigmoid(1)
            ffn_relu(0, 3)
            ffn_square_act(0, 3)
            ffn_relu(1, 0)
            ffn_relu(1, 1)
            copy_h3(3)
            fk_a(2)
            ffn_relu(1, 2)
            ffn_relu(1, 3)
            ffn_square_act(1, 1)
            ffn_square_act(1, 3)
            fk_a(3)
            ffn_relu(2, 0)
            gate_sigmoid(0)
            ffn_relu(2, 1)
            ffn_relu(2, 2)
            ffn_square_act(2, 1)
            ffn_sigmoid(2)
            ffn_relu(2, 3)
            ffn_square_act(2, 3)
            gate_sigmoid(1)
            ffn_relu(3, 0)
            ffn_relu(3, 1)
            ffn_square_act(3, 1)
            gate_sigmoid(2)
            ffn_relu(3, 2)
            ffn_relu(3, 3)
            ffn_square_act(3, 3)
            ffn_sigmoid(3)
            gate_sigmoid(3)

        @block.vector
        def _(dve):
            def statistics(n, src, arrived, stats_done, mv_done, b):
                for t in range(b * CHUNK, (b + 1) * CHUNK):
                    arrived(t)
                    nc.vector.bn_stats(stats[:, n, t, :], src[:, t, :]).then_inc(stats_done, 1)
                for t in range(b * CHUNK, (b + 1) * CHUNK):
                    dve.wait_ge(stats_done, t + 1)
                    nc.vector.bn_aggr(mv[:, n, t, :], stats[:, n, t, :]).then_inc(mv_done, 1)

            def normalise(n, dst, src, rstd_done, done, b):
                dve.wait_ge(rstd_done, b + 1)
                for t in range(b * CHUNK, (b + 1) * CHUNK):
                    nc.vector.tensor_scalar(dst[:, t - b * CHUNK, :], src[:, t, :], mv[:, n, t, 0:1], rstd[:, n, t:t + 1],
                                            ALU.subtract, ALU.mult).then_inc(done, 1)

            def mix(b, names, diffs, dones, first_use):
                dve.wait_ge(diffs, b + 1)
                first_use()
                q, before = seq_cols(b, 0)
                for n, name in enumerate(names):
                    nc.vector.scalar_tensor_tensor(out=mixed[:, b % 2, n, :], in0=diff[:, b % 2, :], scalar=param(name),
                                                   in1=hT[:, q, before], op0=ALU.mult, op1=ALU.add).then_inc(dones[n], 1)

            def x_stats(b):
                statistics(0, x_sb, lambda t: dve.wait_ge(s["first_tiles_loaded"] if t < 2 else x_loaded[t // CHUNK], 16), s["x_stats"], s["x_mv"], b)
                dve.wait_ge(s["x_mv"], CHUNK * (b + 1))
                var = mv[:, 0, tls(b), 1]
                nc.vector.tensor_scalar(var_eps[:, 0, tls(b)], var, EPS, None, ALU.add).then_inc(s["x_var_eps"], 1)
                nc.vector.tensor_scalar(var_eps[:, 1, tls(b)], var, 1.0 + EPS, EPS * EPS, ALU.mult,
                                        ALU.add).then_inc(s["h_var_eps"], 1)

            def att_mix(b):
                def first_use():
                    if b == 0:
                        dve.wait_ge(s["params_loaded"], 16)
                    if b >= 2:
                        dve.wait_ge(s["r_done"], b - 1)
                mix(b, ("mix_k", "mix_v", "mix_r"), s["hT_diff"], (s["mixed_k"], s["mixed_v"], s["mixed_r"]), first_use)

            def route_choose():
                at = pcol["router_b"][0]
                dve.wait_ge(s["logits_done"], BLOCKS)
                nc.vector.tensor_tensor(logits[:, :, :], bank[7][:, 0:E * TILES].rearrange("p (e t) -> p e t", e=E),
                                        par[:, at:at + E].unsqueeze(2).to_broadcast([P, E, TILES]),
                                        ALU.add).then_inc(s["logits_biased"], 1)
                dve.wait_ge(s["logits_biased"], 1)
                nc.vector.tensor_reduce(row_max[:, :], logits[:, :, :].rearrange("p e t -> p t e"), AX_X,
                                        ALU.max).then_inc(s["logit_max"], 1)
                dve.wait_ge(s["logit_max"], 1)
                nc.vector.tensor_tensor(is_max[:, :, :], logits[:, :, :], row_max[:, :].unsqueeze(1).to_broadcast([P, E, TILES]),
                                        ALU.is_equal).then_inc(s["is_max"], 1)
                dve.wait_ge(s["is_max"], 1)
                dve.wait_ge(s["expert_code_ready"], 1)
                nc.vector.tensor_tensor(code[:, :, :], is_max[:, :, :], expert_code[:, :, :], ALU.mult).then_inc(s["max_code"], 1)
                dve.wait_ge(s["max_code"], 1)
                nc.vector.tensor_reduce(code_max[:, :], code[:, :, :].rearrange("p e t -> p t e"), AX_X,
                                        ALU.max).then_inc(s["code_max"], 1)
                dve.wait_ge(s["code_max"], 1)
                nc.vector.tensor_tensor(onehot[:, :, :], expert_code[:, :, :],
                                        code_max[:, :].unsqueeze(1).to_broadcast([P, E, TILES]),
                                        ALU.is_equal).then_inc(s["onehot_ready"], 1)
                nc.vector.tensor_scalar(base[:, :], code_max[:, :], -float(CAPACITY), float(E * CAPACITY - 1), ALU.mult,
                                        ALU.add).then_inc(s["expert_base"], 1)

            def route_slots():
                in_tile = bank[7][:, 128:256]
                totals = bank[7][:, 256:384]
                dve.wait_ge(s["counts_done"], 1)
                dve.wait_ge(s["run_mask_ready"], 1)
                nc.vector.tensor_tensor_scan(counts[:, :, :].rearrange("p e t -> p (e t)"),
                                             run_mask[:, :, :].rearrange("p e t -> p (e t)"), totals, 0.0, ALU.mult,
                                             ALU.add).then_inc(s["counts_run"], 1)
                dve.wait_ge(s["counts_run"], 1)
                nc.vector.tensor_tensor(rank_e[:, :, :].rearrange("p e t -> p (e t)"), in_tile,
                                        counts[:, :, :].rearrange("p e t -> p (e t)"), ALU.add).then_inc(s["rank_a"], 1)
                dve.wait_ge(s["rank_a"], 1)
                nc.vector.tensor_tensor(code[:, :, :].rearrange("p e t -> p (e t)"),
                                        rank_e[:, :, :].rearrange("p e t -> p (e t)"), totals,
                                        ALU.subtract).then_inc(s["rank_b"], 1)
                dve.wait_ge(s["rank_b"], 1)
                nc.vector.tensor_tensor(rank_e[:, :, :], code[:, :, :], onehot[:, :, :], ALU.mult).then_inc(s["rank_hot"], 1)
                dve.wait_ge(s["rank_hot"], 1)
                nc.vector.tensor_reduce(rank[:, :], rank_e[:, :, :].rearrange("p e t -> p t e"), AX_X,
                                        ALU.add).then_inc(s["rank_ready"], 1)
                dve.wait_ge(s["rank_ready"], 1)
                nc.vector.tensor_tensor(slot_f[:, :], base[:, :], rank[:, :], ALU.add).then_inc(s["slot_a"], 1)
                nc.vector.tensor_scalar(over[:, :], rank[:, :], float(CAPACITY), SKIP, ALU.is_gt,
                                        ALU.mult).then_inc(s["slot_over"], 1)
                dve.wait_ge(s["slot_a"], 1)
                dve.wait_ge(s["slot_over"], 1)
                nc.vector.tensor_tensor(slot[:, :], slot_f[:, :], over[:, :], ALU.add).then_inc(s["slot_ready"], 1)

            def wkv_gaps(b):
                i, (_, here), (_, before) = b % 2, seq_cols(b, 1), seq_cols(b, 0)
                dve.wait_ge(s["k_ready"], b + 1)
                if b == 0:
                    dve.wait_ge(s["decay_exp"], 1)
                    nc.vector.tensor_scalar(w_neg[:], w_exp[:], -1.0, None, ALU.mult).then_inc(s["w_ready"], 1)
                    dve.wait_ge(s["w_ready"], 1)
                    dve.wait_ge(s["state_zeroed"], 3)
                else:
                    dve.wait_ge(s["o_ready"], b)
                nc.vector.tensor_tensor_scan(o_state[:, here], w_neg[:].to_broadcast([P, NB]), kT[:, blk(b)],
                                             o_state[:, before.start:before.start + 1], ALU.add,
                                             ALU.max).then_inc(s["o_ready"], 1)
                dve.wait_ge(s["o_ready"], b + 1)
                nc.vector.scalar_tensor_tensor(out=gap[:, i, 0, :], in0=kT[:, blk(b)], scalar=param("first"),
                                               in1=o_state[:, before], op0=ALU.add,
                                               op1=ALU.subtract).then_inc(s["gap_t"], 1)
                nc.vector.scalar_tensor_tensor(out=gap[:, i, 1, :], in0=o_state[:, before], scalar=w_neg[:],
                                               in1=kT[:, blk(b)], op0=ALU.add, op1=ALU.subtract).then_inc(s["gap_s"], 1)
                dve.wait_ge(s["gap_t"], b + 1)
                dve.wait_ge(s["gap_s"], b + 1)
                nc.vector.tensor_scalar(e_neg[:, i, :, :], gap[:, i, :, :], 0.0, None, ALU.max).then_inc(s["gap_max"], 1)
                nc.vector.tensor_scalar(e_pos[:, i, :, :], gap[:, i, :, :], 0.0, None, ALU.min).then_inc(s["gap_min"], 1)

            def wkv_states(b):
                i, (_, here), (_, before) = b % 2, seq_cols(b, 1), seq_cols(b, 0)
                start = slice(before.start, before.start + 1)
                dve.wait_ge(s["exp_neg"], b + 1)
                dve.wait_ge(s["exp_pos"], b + 1)
                if b:
                    dve.wait_ge(s["q_ready"], b)
                nc.vector.tensor_tensor_scan(q_state[:, here], e_pos[:, i, 1, :], e_neg[:, i, 1, :],
                                             q_state[:, start], ALU.mult, ALU.add).then_inc(s["q_ready"], 1)
                dve.wait_ge(s["bv2_ready"], b + 1)
                if b:
                    dve.wait_ge(s["p_ready"], b)
                nc.vector.tensor_tensor_scan(p_state[:, here], e_pos[:, i, 1, :], bv2[:, i, :],
                                             p_state[:, start], ALU.mult, ALU.add).then_inc(s["p_ready"], 1)
                dve.wait_ge(s["q_ready"], b + 1)
                dve.wait_ge(s["p_ready"], b + 1)
                nc.vector.tensor_tensor(den[:, i, :], e_neg[:, i, 0, :], q_state[:, before],
                                        ALU.mult).then_inc(s["aq_ready"], 1)
                nc.vector.tensor_tensor(num[:, i, :], e_neg[:, i, 0, :], p_state[:, before],
                                        ALU.mult).then_inc(s["ap_ready"], 1)
                dve.wait_ge(s["aq_ready"], b + 1)
                nc.vector.tensor_tensor(den[:, i, :], den[:, i, :], e_pos[:, i, 0, :], ALU.add).then_inc(s["den_ready"], 1)
                dve.wait_ge(s["ap_ready"], b + 1)
                dve.wait_ge(s["bv_ready"], b + 1)
                nc.vector.tensor_tensor(num[:, i, :], num[:, i, :], bv[:, i, :], ALU.add).then_inc(s["num_ready"], 1)

            def wkv_divide(b):
                i = b % 2
                dve.wait_ge(s["den_inv"], b + 1)
                nc.vector.tensor_tensor(inv_err[:, i, :], den[:, i, :], inv[:, i, :], ALU.mult).then_inc(s["newton_a"], 1)
                dve.wait_ge(s["newton_a"], b + 1)
                nc.vector.scalar_tensor_tensor(out=inv_err[:, i, :], in0=inv_err[:, i, :], scalar=-2.0, in1=inv[:, i, :],
                                               op0=ALU.add, op1=ALU.mult).then_inc(s["newton_b"], 1)
                dve.wait_ge(s["newton_b"], b + 1)
                dve.wait_ge(s["rn_ready"], b + 1)
                if b >= 2:
                    dve.wait_ge(s["att_done"], b - 1)
                nc.vector.scalar_tensor_tensor(out=wkvT[:, i, :], in0=inv_err[:, i, :], scalar=-1.0, in1=bv[:, i, :],
                                               op0=ALU.mult, op1=ALU.mult).then_inc(s["wkvT_ready"], 1)

            def x2_and_stats(b):
                dve.wait_ge(s["att_done"], b + 1)
                if b == 0:
                    dve.wait_ge(s["scattered"], 16 * TILES)
                nc.vector.tensor_tensor(x2[:, tls(b), :], bank[7][:, :].rearrange("p (t d) -> p t d", d=D),
                                        xn[:, tls(b), :], ALU.add).then_inc(s["x2_ready"], 1)
                statistics(2, x2, lambda t: dve.wait_ge(s["x2_ready"], t // CHUNK + 1), s["x2_stats"], s["x2_mv"], b)
                dve.wait_ge(s["x2_mv"], CHUNK * (b + 1))
                nc.vector.tensor_scalar(var_eps[:, 2, tls(b)], mv[:, 2, tls(b), 1], EPS, None, ALU.add).then_inc(
                    s["x2_var_eps"], 1)

            def h3_normalise(b):
                if b < 2:
                    dve.wait_ge(s["h_turned"], BLOCKS)
                else:
                    dve.wait_ge(s["h3_turned"], b - 1)
                normalise(2, h_tok[:, b % 2, :, :], x2, s["x2_rstd"], s["h3_ready"], b)

            def ffn_mix(b):
                def first_use():
                    if b == 0:
                        dve.wait_ge(s["buf_turned"], 3)
                    elif b == 1:
                        dve.wait_ge(s["r_done"], BLOCKS)
                    else:
                        dve.wait_ge(s["ffn_r_done"], b - 1)
                        dve.wait_ge(s["fk_split_b"], b - 1)
                mix(b, ("ffn_mix_k", "ffn_mix_r"), s["h3_diff"], (s["mixed_fk"], s["mixed_fr"]), first_use)

            def xn_b(b):
                dve.wait_ge(s["xn_split_a"], b)
                if b == 3:
                    dve.wait_ge(s["over_hidden_done"], 2 * HC)
                nc.vector.tensor_tensor(act_b[:, b % 2, :], xnT[:, blk(b)], act_a[:, b % 2, :].bitcast(F32),
                                        ALU.subtract).then_inc(s["xn_split_b"], 1)

            def fk_b(b):
                dve.wait_ge(s["fk_split_a"], b + 1)
                if b < 2:
                    dve.wait_ge(s["over_hidden_done"], (3 + b) * HC)
                else:
                    dve.wait_ge(s["ffn_hidden_done"], (b - 1) * HC)
                nc.vector.tensor_tensor(act_b[:, b % 2, :], mixed[:, b % 2, 0, :], act_a[:, b % 2, :].bitcast(F32),
                                        ALU.subtract).then_inc(s["fk_split_b"], 1)

            def ffn_square(b, c):
                dve.wait_ge(s["ffn_relu_ready"], b * HC + c + 1)
                nc.vector.tensor_tensor(hid[:, b % 2, c, :], hid[:, b % 2, c, :], hid[:, b % 2, c, :],
                                        ALU.mult).then_inc(s["ffn_hidden_ready"], 1)

            def ffn_gated(b):
                dve.wait_ge(s["ffn_out_done"], b + 1)
                dve.wait_ge(s["rf_ready"], b + 1)
                if b >= 2:
                    dve.wait_ge(s["ffn_turned"], b - 1)
                nc.vector.tensor_tensor(gatedT[:, b % 2, :], bank[OUT_BANK[b]][:, :], rfT[:, b % 2, :],
                                        ALU.mult).then_inc(s["ffn_gated"], 1)

            def add_channel_mix(b):
                dve.wait_ge(s["ffn_turned"], b + 1)
                nc.vector.tensor_tensor(x2[:, tls(b), :], bank[OUT_BANK[b]][:, :].rearrange("p (t d) -> p t d", d=D),
                                        x2[:, tls(b), :], ALU.add).then_inc(s["s_ready"], 1)

            def last_gated(i):
                dve.wait_ge(s["last_out_done"], i + 1)
                dve.wait_ge(s["rf_ready"], BLOCKS)
                dve.wait_ge(s["ffn_turned"], BLOCKS - 2)
                q = (BLOCKS - 1) % 2
                nc.vector.tensor_tensor(gatedT[:, q, half(i)], bank[i][:, 0:NB // 2], rfT[:, q, half(i)],
                                        ALU.mult).then_inc(s["last_gated"], 1)

            def gated_rest():
                b = BLOCKS - 1
                dve.wait_ge(s["x2_ready"], BLOCKS)
                dve.wait_ge(s["h3_ready"], TILES)
                dve.wait_ge(s["gate_ready"], BLOCKS)
                nc.vector.tensor_tensor(x2[:, tls(b), :], x2[:, tls(b), :], gate[:, tls(b), :],
                                        ALU.mult).then_inc(s["rest_gated"], 1)
                dve.wait_ge(s["rest_gated"], 1)
                nc.vector.tensor_tensor(x2[:, tls(b), :], x2[:, tls(b), :], x_sb[:, tls(b), :],
                                        ALU.add).then_inc(s["rest_ready"], 1)

            def last_finish(i):
                tiles = half_tiles(i)
                dve.wait_ge(s["last_turned"], i + 1)
                dve.wait_ge(s["rest_ready"], 1)
                nc.vector.tensor_tensor(x_sb[:, tiles, :], bank[i][:, 0:NB // 2].rearrange("p (t d) -> p t d", d=D),
                                        gate[:, tiles, :], ALU.mult).then_inc(s["last_gate"], 1)
                dve.wait_ge(s["last_gate"], i + 1)
                nc.vector.tensor_tensor(x_sb[:, tiles, :], x_sb[:, tiles, :], x2[:, tiles, :],
                                        ALU.add).then_inc(s["last_ready"], 1)

            def finish(b):
                dve.wait_ge(s["s_ready"], b + 1)
                dve.wait_ge(s["gate_ready"], b + 1)
                nc.vector.tensor_tensor(x2[:, tls(b), :], x2[:, tls(b), :], gate[:, tls(b), :],
                                        ALU.mult).then_inc(s["s_gated"], 1)
                dve.wait_ge(s["s_gated"], b + 1)
                nc.vector.tensor_tensor(x_sb[:, tls(b), :], x_sb[:, tls(b), :], x2[:, tls(b), :],
                                        ALU.add).then_inc(s["out_ready"], 1)

            def xn_normalise(b):
                normalise(0, xn[:, tls(b), :], x_sb, s["x_rstd"], s["xn_ready"], b)

            def h_offset(b):
                dve.wait_ge(s["h_rstd"], b + 1)
                nc.vector.scalar_tensor_tensor(out=h_bias[:, tls(b)], in0=mv[:, 0, tls(b), 0], scalar=-1.0,
                                               in1=rstd[:, 1, tls(b)], op0=ALU.mult, op1=ALU.mult).then_inc(
                                                   s["h_bias_ready"], 1)

            x_stats(0)
            x_stats(1)
            h_offset(0)
            x_stats(2)
            xn_normalise(0)
            h_offset(1)
            x_stats(3)
            for b in range(1, 4):
                xn_normalise(b)
            h_offset(2)
            att_mix(0)
            att_mix(1)
            h_offset(3)
            route_choose()
            xn_b(1)
            att_mix(2)
            route_slots()
            att_mix(3)
            xn_b(2)
            wkv_gaps(0)
            wkv_gaps(1)
            xn_b(3)
            wkv_states(0)
            wkv_gaps(2)
            wkv_states(1)
            wkv_gaps(3)
            wkv_divide(0)
            wkv_divide(1)
            x2_and_stats(0)
            wkv_states(2)
            x2_and_stats(1)
            h3_normalise(0)
            wkv_states(3)
            h3_normalise(1)
            wkv_divide(2)
            wkv_divide(3)
            x2_and_stats(2)
            ffn_mix(0)
            ffn_mix(1)
            h3_normalise(2)
            fk_b(0)
            x2_and_stats(3)
            fk_b(1)
            ffn_mix(2)
            ffn_square(0, 0)
            ffn_square(0, 2)
            h3_normalise(3)
            ffn_square(1, 0)
            fk_b(2)
            ffn_square(1, 2)
            ffn_mix(3)
            ffn_gated(0)
            fk_b(3)
            ffn_square(2, 0)
            add_channel_mix(0)
            ffn_square(2, 2)
            ffn_gated(1)
            ffn_square(3, 0)
            finish(0)
            ffn_gated(2)
            add_channel_mix(1)
            add_channel_mix(2)
            ffn_square(3, 2)
            finish(1)
            finish(2)
            last_gated(0)
            gated_rest()
            last_gated(1)
            last_finish(0)
            last_finish(1)


def kernel(**inputs):
    import numpy as np
    import concourse.bacc as bacc
    from concourse.bass_utils import run_bass_kernel_spmd

    a = {name: np.asarray(value) for name, value in inputs.items()}
    att, ffn = "L0_attn_", "L0_ffn_"

    def column(v):
        return v.reshape(-1, P).T

    def chunks(w):
        return w.reshape(-1, P, w.shape[1]).transpose(1, 0, 2).reshape(P, -1)

    packed = {"ln_att_g": column(a[att + "ln_att_g"]), "ln_att_b": column(a[att + "ln_att_b"]),
              "ln_ffn_g": column(a[att + "ln_ffn_g"]), "ln_ffn_b": column(a[att + "ln_ffn_b"]),
              "decay": column(a[att + "att_time_decay"]), "first": column(a[att + "att_time_first"]),
              "mix_k": column(a[att + "att_mix_k"]), "mix_v": column(a[att + "att_mix_v"]),
              "mix_r": column(a[att + "att_mix_r"]), "ffn_mix_k": column(a[att + "ffn_mix_k"]),
              "ffn_mix_r": column(a[att + "ffn_mix_r"]), "ob2": column(a[ffn + "ob2"]), "ob1": column(a[ffn + "ob1"]),
              "b1": column(a[ffn + "b1"]), "b2": column(a[ffn + "b2"]),
              "router_b": np.repeat(a[ffn + "router_b"][None], P, axis=0), "router_w": a[ffn + "router_w"]}
    mats = {"wk": a[att + "att_wk"], "wv": a[att + "att_wv"], "wr": a[att + "att_wr"], "wo": a[att + "att_wo"],
            "ffn_wr": a[att + "ffn_wr"], "ffn_wk": a[att + "ffn_wk"], "ffn_wv": chunks(a[att + "ffn_wv"]),
            "ow1": a[ffn + "ow1"], "ow2": chunks(a[ffn + "ow2"])}
    x = a[att + "x"]
    arrays = {"x_dram": np.ascontiguousarray(x.reshape(-1, x.shape[-1])),
              "params_dram": np.ascontiguousarray(np.concatenate([packed[n] for n in PARAMS], axis=1)),
              "weights_dram": np.ascontiguousarray(np.concatenate([mats[n] for n in WEIGHTS], axis=1)),
              "w1_dram": np.ascontiguousarray(a[ffn + "w1"]), "w2_dram": np.ascontiguousarray(a[ffn + "w2"])}

    nc = bacc.Bacc("TRN2", target_bir_lowering=False, num_devices=1)
    args = [nc.dram_tensor(n, v.shape, mybir.dt.from_np(v.dtype), kind="ExternalInput").ap() for n, v in arrays.items()]
    out = nc.dram_tensor("out_dram", arrays["x_dram"].shape, F32, kind="ExternalOutput").ap()
    build(nc, *args, out)
    result = run_bass_kernel_spmd(nc, [arrays], core_ids=[0])
    return result.results[0]["out_dram"].reshape(x.shape)
```
